# Optimizing a Trainium2 kernel written in Bass

```python
import numpy as np
import jax
import jax.numpy as jnp

def _softmax(x, axis=-1):
    return jax.nn.softmax(x, axis=axis)

def _gelu(x):
    return jax.nn.gelu(x, approximate=True)

def _silu(x):
    return jax.nn.silu(x)

def _sigmoid(x):
    return jax.nn.sigmoid(x)

def _layernorm(x, axis=-1, eps=1e-05):
    m = jnp.mean(x, axis=axis, keepdims=True)
    v = jnp.var(x, axis=axis, keepdims=True)
    return (x - m) / jnp.sqrt(v + eps)

def _scatter_add(tgt, idx, src, axis=0):
    return tgt.at[idx].add(src)

def _segment_sum(src, seg, n):
    return jax.ops.segment_sum(src, seg, n)
kernel_name = 'mk_prb_d1_jaxref_r4_83fe86'

def setup_inputs(seed: int=0):
    np.random.seed(seed)
    _w = jnp.asarray

    def _L0_attn_setup():
        import jax, jax.numpy as jnp
        import numpy as np
        D_MODEL = 256
        N_HEADS = 16
        HEAD_DIM = D_MODEL // N_HEADS
        EPS = 1e-05

        def _layernorm(x, g, b):
            mu = jnp.mean(x, axis=-1, keepdims=True)
            var = jnp.mean(jnp.square(x - mu), axis=-1, keepdims=True)
            return (x - mu) * jax.lax.rsqrt(var + EPS) * g + b

        def _gdn(x, Wq, Wk, Wv, Wb, Wg, Wo, bo):
            B, S, D = x.shape
            H, Dh = (N_HEADS, HEAD_DIM)
            q = (x @ Wq).reshape(B, S, H, Dh) * Dh ** (-0.5)
            k = (x @ Wk).reshape(B, S, H, Dh)
            k = k / (jnp.linalg.norm(k, axis=-1, keepdims=True) + 1e-06)
            v = (x @ Wv).reshape(B, S, H, Dh)
            beta = jax.nn.sigmoid(x @ Wb)
            g = jax.nn.sigmoid(x @ Wg)
            qt = jnp.moveaxis(q, 1, 0)
            kt = jnp.moveaxis(k, 1, 0)
            vt = jnp.moveaxis(v, 1, 0)
            bt = jnp.moveaxis(beta, 1, 0)
            gt = jnp.moveaxis(g, 1, 0)
            S0 = jnp.zeros((B, H, Dh, Dh), x.dtype)

            def step(Sst, inp):
                q_t, k_t, v_t, b_t, g_t = inp
                Sst = Sst * g_t[..., None, None]
                kS = jnp.einsum('bhk,bhkv->bhv', k_t, Sst)
                Sst = Sst + b_t[..., None, None] * jnp.einsum('bhk,bhv->bhkv', k_t, v_t - kS)
                o_t = jnp.einsum('bhk,bhkv->bhv', q_t, Sst)
                return (Sst, o_t)
            _, out = jax.lax.scan(step, S0, (qt, kt, vt, bt, gt))
            out = jnp.moveaxis(out, 0, 1).reshape(B, S, D)
            return out @ Wo + bo
        key = jax.random.key(seed)
        ks = jax.random.split(key, 16)
        B, S, D = (4, 512, D_MODEL)
        s = 0.02
        inp = {'x': jax.random.normal(ks[0], (B, S, D), dtype=jnp.float32), 'Wq': jax.random.normal(ks[1], (D, D), jnp.float32) * s, 'Wk': jax.random.normal(ks[2], (D, D), jnp.float32) * s, 'Wv': jax.random.normal(ks[3], (D, D), jnp.float32) * s, 'Wb': jax.random.normal(ks[4], (D, N_HEADS), jnp.float32) * s, 'Wg': jax.random.normal(ks[5], (D, N_HEADS), jnp.float32) * s, 'Wo': jax.random.normal(ks[6], (D, D), jnp.float32) * s, 'bo': jnp.zeros((D,), jnp.float32), 'ln1_g': jnp.ones((D,), jnp.float32), 'ln1_b': jnp.zeros((D,), jnp.float32), 'ln2_g': jnp.ones((D,), jnp.float32), 'ln2_b': jnp.zeros((D,), jnp.float32), 'w1': jax.random.normal(ks[7], (D, 4 * D), jnp.float32) * s, 'b1': jnp.zeros((4 * D,), jnp.float32), 'w2': jax.random.normal(ks[8], (4 * D, D), jnp.float32) * s, 'b2': jnp.zeros((D,), jnp.float32)}
        return inp
    _L0_attn_in = _L0_attn_setup()

    def _L0_ffn_setup():
        import jax, jax.numpy as jnp
        import numpy as np
        B, S, D = (1, 512, 256)
        E, K, F = (64, 8, 192)
        SF = 192
        C = 128
        ROUTED_SCALE = 1.0

        def _moe_forward(x, router_w, w_gate, w_up, w_down, ws_gate_up, ws_down):
            T = x.shape[0]
            logits = x.astype(jnp.float32) @ router_w.T
            probs = jax.nn.softmax(logits, axis=-1)
            topk_w, topk_ids = jax.lax.top_k(probs, K)
            topk_w = topk_w / jnp.sum(topk_w, axis=-1, keepdims=True)
            topk_w = topk_w.astype(x.dtype)
            N = T * K
            flat_e = topk_ids.reshape(-1)
            flat_w = topk_w.reshape(-1)
            tok = jnp.arange(N) // K
            onehot = flat_e[:, None] == jnp.arange(E)[None, :]
            pos = jnp.cumsum(onehot, axis=0)[jnp.arange(N), flat_e] - 1
            valid = pos < C
            idx = jnp.where(valid, flat_e * C + pos, E * C)
            x_buf = jnp.zeros((E * C + 1, x.shape[1]), x.dtype).at[idx].set(x[tok])
            xb = x_buf[:E * C].reshape(E, C, -1)
            g = jnp.einsum('ecd,edf->ecf', xb, w_gate)
            u = jnp.einsum('ecd,edf->ecf', xb, w_up)
            h = jax.nn.silu(g) * u
            y = jnp.einsum('ecf,efd->ecd', h, w_down).reshape(E * C, -1)
            safe = jnp.where(valid, idx, 0)
            contrib = y[safe] * (flat_w * valid.astype(flat_w.dtype))[:, None]
            routed = jax.ops.segment_sum(contrib, tok, num_segments=T)
            routed = routed * ROUTED_SCALE
            gu = x @ ws_gate_up
            sg, su = (gu[:, :SF], gu[:, SF:])
            shared = jax.nn.silu(sg) * su @ ws_down
            return routed + shared
        key = jax.random.key(seed)
        ks = jax.random.split(key, 7)
        w = 0.02
        return {'hidden_states': jax.random.normal(ks[0], (B, S, D), jnp.float32), 'router_w': jax.random.normal(ks[1], (E, D), jnp.float32) * w, 'w_gate': jax.random.normal(ks[2], (E, D, F), jnp.float32) * w, 'w_up': jax.random.normal(ks[3], (E, D, F), jnp.float32) * w, 'w_down': jax.random.normal(ks[4], (E, F, D), jnp.float32) * w, 'ws_gate_up': jax.random.normal(ks[5], (D, 2 * SF), jnp.float32) * w, 'ws_down': jax.random.normal(ks[6], (SF, D), jnp.float32) * w}
    _L0_ffn_in = _L0_ffn_setup()
    _d = {'L0_attn_x': _L0_attn_in['x'], 'L0_attn_Wq': _L0_attn_in['Wq'], 'L0_attn_Wk': _L0_attn_in['Wk'], 'L0_attn_Wv': _L0_attn_in['Wv'], 'L0_attn_Wb': _L0_attn_in['Wb'], 'L0_attn_Wg': _L0_attn_in['Wg'], 'L0_attn_Wo': _L0_attn_in['Wo'], 'L0_attn_bo': _L0_attn_in['bo'], 'L0_attn_ln1_g': _L0_attn_in['ln1_g'], 'L0_attn_ln1_b': _L0_attn_in['ln1_b'], 'L0_attn_ln2_g': _L0_attn_in['ln2_g'], 'L0_attn_ln2_b': _L0_attn_in['ln2_b'], 'L0_attn_w1': _L0_attn_in['w1'], 'L0_attn_b1': _L0_attn_in['b1'], 'L0_attn_w2': _L0_attn_in['w2'], 'L0_attn_b2': _L0_attn_in['b2'], 'L0_ffn_router_w': _L0_ffn_in['router_w'], 'L0_ffn_w_gate': _L0_ffn_in['w_gate'], 'L0_ffn_w_up': _L0_ffn_in['w_up'], 'L0_ffn_w_down': _L0_ffn_in['w_down'], 'L0_ffn_ws_gate_up': _L0_ffn_in['ws_gate_up'], 'L0_ffn_ws_down': _L0_ffn_in['ws_down']}
    _x0 = _d['L0_attn_x']
    _d['L0_attn_x'] = jax.random.normal(jax.random.fold_in(jax.random.key(seed), 1), (16, 512, 256), dtype=_x0.dtype)
    del _x0
    return _d

def reference(L0_attn_x, L0_attn_Wq, L0_attn_Wk, L0_attn_Wv, L0_attn_Wb, L0_attn_Wg, L0_attn_Wo, L0_attn_bo, L0_attn_ln1_g, L0_attn_ln1_b, L0_attn_ln2_g, L0_attn_ln2_b, L0_attn_w1, L0_attn_b1, L0_attn_w2, L0_attn_b2, L0_ffn_router_w, L0_ffn_w_gate, L0_ffn_w_up, L0_ffn_w_down, L0_ffn_ws_gate_up, L0_ffn_ws_down):

    def _L0_attn_ref(x, Wq, Wk, Wv, Wb, Wg, Wo, bo, ln1_g, ln1_b, ln2_g, ln2_b, w1, b1, w2, b2):
        import jax, jax.numpy as jnp
        import numpy as np
        D_MODEL = 256
        N_HEADS = 16
        HEAD_DIM = D_MODEL // N_HEADS
        EPS = 1e-05

        def _layernorm(x, g, b):
            mu = jnp.mean(x, axis=-1, keepdims=True)
            var = jnp.mean(jnp.square(x - mu), axis=-1, keepdims=True)
            return (x - mu) * jax.lax.rsqrt(var + EPS) * g + b

        def _gdn(x, Wq, Wk, Wv, Wb, Wg, Wo, bo):
            B, S, D = x.shape
            H, Dh = (N_HEADS, HEAD_DIM)
            q = (x @ Wq).reshape(B, S, H, Dh) * Dh ** (-0.5)
            k = (x @ Wk).reshape(B, S, H, Dh)
            k = k / (jnp.linalg.norm(k, axis=-1, keepdims=True) + 1e-06)
            v = (x @ Wv).reshape(B, S, H, Dh)
            beta = jax.nn.sigmoid(x @ Wb)
            g = jax.nn.sigmoid(x @ Wg)
            qt = jnp.moveaxis(q, 1, 0)
            kt = jnp.moveaxis(k, 1, 0)
            vt = jnp.moveaxis(v, 1, 0)
            bt = jnp.moveaxis(beta, 1, 0)
            gt = jnp.moveaxis(g, 1, 0)
            S0 = jnp.zeros((B, H, Dh, Dh), x.dtype)

            def step(Sst, inp):
                q_t, k_t, v_t, b_t, g_t = inp
                Sst = Sst * g_t[..., None, None]
                kS = jnp.einsum('bhk,bhkv->bhv', k_t, Sst)
                Sst = Sst + b_t[..., None, None] * jnp.einsum('bhk,bhv->bhkv', k_t, v_t - kS)
                o_t = jnp.einsum('bhk,bhkv->bhv', q_t, Sst)
                return (Sst, o_t)
            _, out = jax.lax.scan(step, S0, (qt, kt, vt, bt, gt))
            out = jnp.moveaxis(out, 0, 1).reshape(B, S, D)
            return out @ Wo + bo
        x = x + _gdn(_layernorm(x, ln1_g, ln1_b), Wq, Wk, Wv, Wb, Wg, Wo, bo)
        h = _layernorm(x, ln2_g, ln2_b)
        h = jax.nn.gelu(h @ w1 + b1, approximate=False) @ w2 + b2
        return x + h

    def _L0_ffn_ref(hidden_states, router_w, w_gate, w_up, w_down, ws_gate_up, ws_down):
        import jax, jax.numpy as jnp
        import numpy as np
        B, S, D = (1, 512, 256)
        E, K, F = (64, 8, 192)
        SF = 192
        C = 128
        ROUTED_SCALE = 1.0

        def _moe_forward(x, router_w, w_gate, w_up, w_down, ws_gate_up, ws_down):
            T = x.shape[0]
            logits = x.astype(jnp.float32) @ router_w.T
            probs = jax.nn.softmax(logits, axis=-1)
            topk_w, topk_ids = jax.lax.top_k(probs, K)
            topk_w = topk_w / jnp.sum(topk_w, axis=-1, keepdims=True)
            topk_w = topk_w.astype(x.dtype)
            N = T * K
            flat_e = topk_ids.reshape(-1)
            flat_w = topk_w.reshape(-1)
            tok = jnp.arange(N) // K
            onehot = flat_e[:, None] == jnp.arange(E)[None, :]
            pos = jnp.cumsum(onehot, axis=0)[jnp.arange(N), flat_e] - 1
            valid = pos < C
            idx = jnp.where(valid, flat_e * C + pos, E * C)
            x_buf = jnp.zeros((E * C + 1, x.shape[1]), x.dtype).at[idx].set(x[tok])
            xb = x_buf[:E * C].reshape(E, C, -1)
            g = jnp.einsum('ecd,edf->ecf', xb, w_gate)
            u = jnp.einsum('ecd,edf->ecf', xb, w_up)
            h = jax.nn.silu(g) * u
            y = jnp.einsum('ecf,efd->ecd', h, w_down).reshape(E * C, -1)
            safe = jnp.where(valid, idx, 0)
            contrib = y[safe] * (flat_w * valid.astype(flat_w.dtype))[:, None]
            routed = jax.ops.segment_sum(contrib, tok, num_segments=T)
            routed = routed * ROUTED_SCALE
            gu = x @ ws_gate_up
            sg, su = (gu[:, :SF], gu[:, SF:])
            shared = jax.nn.silu(sg) * su @ ws_down
            return routed + shared
        b, s, d = hidden_states.shape
        x = hidden_states.reshape(-1, d)
        out = _moe_forward(x, router_w, w_gate, w_up, w_down, ws_gate_up, ws_down)
        return out.reshape(b, s, d)
    x = L0_attn_x
    xn = _layernorm(x, axis=-1)
    x = x + _L0_attn_ref(xn, L0_attn_Wq, L0_attn_Wk, L0_attn_Wv, L0_attn_Wb, L0_attn_Wg, L0_attn_Wo, L0_attn_bo, L0_attn_ln1_g, L0_attn_ln1_b, L0_attn_ln2_g, L0_attn_ln2_b, L0_attn_w1, L0_attn_b1, L0_attn_w2, L0_attn_b2) + _L0_ffn_ref(xn, L0_ffn_router_w, L0_ffn_w_gate, L0_ffn_w_up, L0_ffn_w_down, L0_ffn_ws_gate_up, L0_ffn_ws_down)
    return x

_drawn_inputs = setup_inputs


def setup_inputs(seed=0):
    import zlib

    import numpy as np

    out = dict(_drawn_inputs(seed))
    spreads = {'L0_attn_bo': (0.0, 0.8),
     'L0_attn_ln1_g': (1.0, 0.6),
     'L0_attn_ln1_b': (0.0, 0.8),
     'L0_attn_ln2_g': (1.0, 0.6),
     'L0_attn_ln2_b': (0.0, 2.0),
     'L0_attn_b1': (0.0, 2.0),
     'L0_attn_b2': (0.0, 0.8)}
    factors = {'L0_attn_Wq': 8.0,
     'L0_attn_Wk': 8.0,
     'L0_attn_Wv': 8.0,
     'L0_attn_Wb': 8.0,
     'L0_attn_Wg': 8.0,
     'L0_attn_Wo': 8.0,
     'L0_ffn_router_w': 8.0,
     'L0_ffn_w_gate': 8.0,
     'L0_ffn_w_up': 8.0,
     'L0_ffn_w_down': 8.0,
     'L0_ffn_ws_gate_up': 7.717,
     'L0_ffn_ws_down': 7.734,
     'L0_attn_w1': 3.545,
     'L0_attn_w2': 2.684}
    for name, (base, spread) in spreads.items():
        noise = np.random.default_rng([zlib.crc32(name.encode()), seed]).standard_normal(out[name].shape)
        drawn = base * np.exp(spread * noise) if base else spread * noise
        out[name] = jnp.asarray(drawn.astype(out[name].dtype))
    for name, factor in factors.items():
        out[name] = (out[name] * factor).astype(out[name].dtype)
    return out
```

```python
from contextlib import ExitStack

import concourse.bass as bass
from concourse import mybir

ALU = mybir.AluOpType
ACT = mybir.ActivationFunctionType
AX = mybir.AxisListType
F32 = mybir.dt.float32
BF16 = mybir.dt.bfloat16
I32 = mybir.dt.int32

P = 128
B, T, D = 16, 512, 256
H, DH = 16, 16
DC = D // P
BLK = 64
NBLK = T // BLK
ST = 8
NB2 = B // 2
NT = NBLK * NB2
E, K, CAP = 64, 8, 128
F = 192
FH = F // 2
M = 4 * D
MC = M // P
TOK = B * T
XW = D + E
EPS = 1e-5
AHEAD = 2
RT = 4
S2 = DH * DH
ROUTE, EXPERTS, BACK2, BACK2_LATE, BACK1 = range(5)
PHASES = [(ROUTE, 0, 2), (EXPERTS, 2, 2), (BACK2, 4, 2), (BACK2_LATE, 6, 1), (BACK1, 7, 1)]
FST = 10 * 16
BUF = 2


def layer(nc, x, Wq, Wk, Wv, Wb, Wg, Wo, bo, ln1_g, ln1_b, ln2_g, ln2_b, w1, b1, w2, b2,
          router_wT, w_gate, w_up, w_down, ws_gate_up, ws_down, out):
    ctx = ExitStack()
    with ctx:
        def sb(name, shape, dt=F32):
            return ctx.enter_context(nc.sbuf_tensor(name, shape, dt))

        def sem(name):
            return ctx.enter_context(nc.semaphore(name))

        qkv_d = nc.dram_tensor("qkv_d", (NBLK, 3, B, 2, P, BLK), F32, kind="Internal").ap()
        gat_d = nc.dram_tensor("gat_d", (NBLK, 2, B, H, BLK), F32, kind="Internal").ap()
        o_d = nc.dram_tensor("o_d", (NBLK, B, 2, P, BLK), F32, kind="Internal").ap()
        xw_d = nc.dram_tensor("xw_d", (TOK + P, XW), F32, kind="Internal").ap()
        acc_d = nc.dram_tensor("acc_d", (TOK + P, D), F32, kind="Internal").ap()
        cum_d = nc.dram_tensor("cum_d", (E, BLK + TOK), F32, kind="Internal").ap()

        ident = sb("ident", [P, P])
        ones = sb("ones", [P, P])
        iot = sb("iot", [P, CAP + 1], I32)
        zeros = sb("zeros", [P, XW])
        slot_row = sb("slot_row", [P, CAP])
        slot_col = sb("slot_col", [P, 1])
        half_pow = sb("half_pow", [P, 2])
        wqkvg = sb("wqkvg", [P, DC, 3 * D + 2 * H])
        wo_s = sb("wo_s", [P, DC, D])
        rw_s = sb("rw_s", [P, DC, E])
        wsgu_s = sb("wsgu_s", [P, DC, 2 * F])
        wsd_s = sb("wsd_s", [FH, 2, D])
        bo_s = sb("bo_s", [1, D])
        b2_s = sb("b2_s", [1, D])
        lncol = sb("lncol", [P, 4, DC])
        bqkv = sb("bqkv", [P, 8])
        b1_in = sb("b1_in", [P, MC])
        b1_s = sb("b1_s", [P, MC])
        mean = sb("mean", [P, NT])
        var = sb("var", [P, NT])
        rstd = sb("rstd", [P, NT])
        nmr = sb("nmr", [P, NT])
        sA = sb("sA", [P, NT])
        bA = sb("bA", [P, NT])
        tmp_st = sb("tmp_st", [P, NT])

        xt = sb("xt", [P, D])
        xa = sb("xa", [P, D])
        xaT = sb("xaT", [P, DC, P])
        stg = sb("stg", [P, 6, P])
        gst = sb("gst", [2 * H, P])

        win = [sb(f"win_{n}", [P, BUF, 2, DH, BLK]) for n in "qkv"]
        gwin = sb("gwin", [P, BUF, 2, 2, BLK])
        sq = sb("sq", [P, ST * 2, DH])
        n2 = sb("n2", [P, ST * 2])
        nrm = sb("nrm", [P, ST * 2])
        nrm_e = sb("nrm_e", [P, ST * 2])
        rk = sb("rk", [P, ST * 2])
        kn = [sb(f"kn{h}", [P, ST, 2, DH]) for h in range(BUF)]
        bv = [sb(f"bv{h}", [P, ST, 2, DH]) for h in range(BUF)]
        qs = [sb(f"qs{h}", [P, ST, 2, DH]) for h in range(BUF)]
        g8 = [sb(f"g8{h}", [P, ST, 2]) for h in range(BUF)]
        bg = [sb(f"bg{h}", [P, ST, 2]) for h in range(BUF)]
        S = [sb(f"S{h}", [P, ST, 2, S2]) for h in range(BUF)]
        prod = sb("prod", [P, 2, S2])
        outer = sb("outer", [P, 2, S2])
        kS = sb("kS", [P, 2, DH])
        nu = sb("nu", [P, 2, DH])
        HS = ST // 2
        rp = sb("rp", [P, HS * 2 * DH, 16])
        r1 = sb("r1", [P, HS * 2 * DH, 8])
        r2 = sb("r2", [P, HS * 2 * DH, 4])
        r3 = sb("r3", [P, HS * 2 * DH, 2])
        oblk = sb("oblk", [P, 2, DH, BLK])

        gT = sb("gT", [P, DC, P])
        sgu = sb("sgu", [FH, 2 * P])
        hg_s = sb("hg_s", [FH, 2, P])

        REG = 12288
        region = sb("region", [P, REG])
        at = [0]

        def carve(words, restart=False):
            if restart:
                at[0] = 0
            a = region[:, at[0]:at[0] + words]
            at[0] += words
            assert at[0] <= REG
            return a

        xs = [carve(NB2 * D, n == 0).rearrange("p (q d) -> p q d", d=D) for n in range(BUF)]
        wraw = carve(DC * (3 * D + 2 * H)).rearrange("p (c n) -> p c n", c=DC)
        bn6 = carve(NB2 * 6).rearrange("p (q s) -> p q s", s=6)
        mv8 = carve(NB2 * 2).rearrange("p (q s) -> p q s", s=2)
        x4 = carve(RT * D, True).rearrange("p (r d) -> p r d", r=RT)
        xw = carve(RT * XW).rearrange("p (r d) -> p r d", r=RT)
        acc4 = carve(RT * D).rearrange("p (r d) -> p r d", r=RT)
        lg, ex, mk, wt, rep = [carve(RT * E).rearrange("p (r e) -> p r e", r=RT) for _ in range(5)]
        mx = carve(RT * 8).rearrange("p (r e) -> p r e", r=RT)
        negm, wsum, wrec = [carve(RT) for _ in range(3)]
        at[0] = TOK
        maskT = carve(TOK // 2)[0:E, :].bitcast(BF16)
        cum = carve(TOK, True)[0:E, :]
        cur = region[:, 0:E * BLK].rearrange("p (e j) -> p e j", e=E)
        prv = region[:, E * BLK:2 * E * BLK].rearrange("p (e j) -> p e j", e=E)
        at[0] = 2 * E * BLK
        CW = BLK + 1
        onh = [carve(RT * CAP).rearrange("p (r s) -> p r s", r=RT) for _ in range(2)]
        diff = [carve(RT * CW).rearrange("p (r s) -> p r s", r=RT) for _ in range(2)]
        cnt = [carve(RT * BLK).rearrange("p (r s) -> p r s", r=RT) for _ in range(2)]
        csum = [carve(RT) for _ in range(2)]
        sidx = carve(E)
        sgei = carve(E)
        idx_i = sb("idx_i", [P, E], I32)
        ew_g = [carve(DC * F, r == 0).rearrange("p (c f) -> p c f", c=DC) for r in range(RT)]
        ew_u = [carve(DC * F).rearrange("p (c f) -> p c f", c=DC) for r in range(RT)]
        ew_d = [carve(2 * D)[0:FH, :].rearrange("p (c f) -> p c f", c=2) for r in range(RT)]
        xg = [carve(XW) for r in range(RT)]
        yw = [carve(D) for r in range(RT)]
        idx4 = sb("idx4", [P, RT], I32)
        w1_s = carve(DC * M, True).rearrange("p (c n) -> p c n", c=DC)
        w2_s = carve(MC * D).rearrange("p (c n) -> p c n", c=MC)
        oT = [carve(2 * 2 * BLK).rearrange("p (g b t) -> p g b t", b=2, g=2) for _ in range(2)]
        xn_b = [carve(D) for _ in range(2)]
        ac_b = [carve(D) for _ in range(2)]
        x1 = [carve(D) for _ in range(2)]
        hb = [carve(D) for _ in range(2)]
        fin = [carve(D) for _ in range(2)]
        hT = [carve(DC * P).rearrange("p (c t) -> p c t", c=DC) for _ in range(2)]
        mid = [carve(MC * P).rearrange("p (c t) -> p c t", c=MC) for _ in range(2)]
        bn_b = carve(2 * 6).rearrange("p (r s) -> p r s", r=2)
        mv_b = carve(2 * 2).rearrange("p (r s) -> p r s", r=2)
        ve_b, sd_b, rs_b, nb_b = [carve(2) for _ in range(4)]

        bank = [ctx.enter_context(nc.psum_tensor(f"bank{i}", [P, 512], F32)) for i in range(8)]
        FT, FQ, FV, TB, LG, G0, G1, YB = bank

        const_ld = sem("const_ld"); raw_ld = sem("raw_ld"); consts = sem("consts")
        xs_ld = [sem(f"xs_ld{i}") for i in range(BUF)]
        xs_used = sem("xs_used"); stats_in = sem("stats_in"); stats_done = sem("stats_done")
        pch = sem("pch"); vch = sem("vch"); ach = sem("ach")
        bias_mm = sem("bias_mm"); w_scaled = sem("w_scaled"); bias_done = sem("bias_done")
        xt_ld = sem("xt_ld"); xa_ready = sem("xa_ready"); fT_done = sem("fT_done")
        xaT_ready = sem("xaT_ready"); qkv_done = sem("qkv_done"); stg_ready = sem("stg_ready")
        f_stored = sem("f_stored")
        win_ld = sem("win_ld"); sq_ready = sem("sq_ready"); n2_ready = sem("n2_ready")
        nrm_ready = sem("nrm_ready"); rk_ready = sem("rk_ready")
        act_staged = sem("act_staged"); pool_staged = sem("pool_staged")
        rec_done = sem("rec_done"); prod_done = sem("prod_done"); o_stored = sem("o_stored")
        x4_ld = sem("x4_ld"); xn_ready = sem("xn_ready"); t_done = sem("t_done")
        gT_ready = sem("gT_ready"); gu_done = sem("gu_done"); sg_ready = sem("sg_ready")
        h_ready = sem("h_ready"); y_done = sem("y_done"); acc_ready = sem("acc_ready")
        lg_done = sem("lg_done"); lg_copied = sem("lg_copied"); negm_ready = sem("negm_ready")
        e_ready = sem("e_ready"); mask_ready = sem("mask_ready"); w_ready = sem("w_ready")
        mt_done = sem("mt_done"); mT_ready = sem("mT_ready"); r_stored = sem("r_stored")
        zero_st = sem("zero_st")
        cum_ready = sem("cum_ready"); cum_st = sem("cum_st"); cur_ld = sem("cur_ld")
        onh_ready = sem("onh_ready"); slot_mm = sem("slot_mm"); slot_used = sem("slot_used")
        slots_ready = sem("slots_ready")
        ew_ld = [sem(f"ew_ld{r}") for r in range(RT)]
        g_ld = [sem(f"g_ld{r}") for r in range(RT)]
        yw_ready = sem("yw_ready"); sc_done = sem("sc_done")
        mlp_ld = sem("mlp_ld"); mlp_bias = sem("mlp_bias"); mlp_w = sem("mlp_w")
        bk_ld = [sem(f"bk_ld{r}") for r in range(2)]
        at_done = sem("at_done"); x1_ready = sem("x1_ready"); ve_ready = sem("ve_ready")
        sd_ready = sem("sd_ready"); nb_ready = sem("nb_ready"); hb_ready = sem("hb_ready")
        hT_done = sem("hT_done"); hT_ready = sem("hT_ready"); mid_done = sem("mid_done")
        gelu_done = sem("gelu_done"); out_done = sem("out_done"); fin_ready = sem("fin_ready")
        fin_st = sem("fin_st")

        passed = sem("passed")

        x_t = x.rearrange("(q b) (k t) d -> k q b t d", b=2, t=BLK)
        out_t = out.rearrange("(q b) (k t) d -> k q b t d", b=2, t=BLK)
        x_r = x.rearrange("(q b) (m r t) d -> m q b t r d", b=2, t=BLK, r=RT)
        xw_r = xw_d[0:TOK, :].rearrange("(q b m r t) d -> m q b t r d", q=NB2, b=2, m=T // (RT * BLK), t=BLK)
        acc_r = acc_d[0:TOK, :].rearrange("(q b m r t) d -> m q b t r d", q=NB2, b=2, m=T // (RT * BLK), t=BLK)
        xw_t = xw_d[0:TOK, :].rearrange("(q b k t) d -> k q b t d", q=NB2, b=2, t=BLK)
        acc_t = acc_d[0:TOK, :].rearrange("(q b k t) d -> k q b t d", q=NB2, b=2, t=BLK)
        qkv_st = qkv_d.rearrange("k m (q b) g p t -> k q b p m g t", b=2)
        gat_st = gat_d.rearrange("k w (q b) h t -> k q b w h t", b=2)
        qkv_ld = qkv_d.rearrange("k m (s b) g (h d) t -> k m s (b g h) (d t)", s=2, h=P // DH)
        gat_ld = gat_d.rearrange("k w (s b) h t -> k s (b h) w t", s=2)
        o_st = o_d.rearrange("k (s b) g (h v) t -> k (b g h) s (v t)", s=2, h=P // DH)
        o_ld = o_d.rearrange("k (q b) g p t -> k q b p g t", b=2)
        maskT_v = maskT.rearrange("e (q b m r t) -> e q m r b t", q=NB2, b=2, r=RT, t=BLK)

        def iteration(kb0, kb, jj, h):
            return (kb + kb0) * NB2 + jj * 2 + h

        def lookup(L):
            return (L >> 3) & 1, (L & 7) * ST

        UNITS_R = NT

        block = ctx.enter_context(nc.Block())

        @block.sync
        def _(sp):
            for m, w in enumerate((Wq, Wk, Wv)):
                sp.dma_start(wraw[:, :, m * D:(m + 1) * D], w.rearrange("(c p) n -> p c n", p=P)).then_inc(raw_ld, 16)
            for m, w in enumerate((Wb, Wg)):
                sp.dma_start(wraw[:, :, 3 * D + m * H:3 * D + (m + 1) * H],
                             w.rearrange("(c p) n -> p c n", p=P)).then_inc(raw_ld, 16)
            for m, w in enumerate((ln1_g, ln1_b, ln2_g, ln2_b)):
                sp.dma_start(lncol[:, m, :], w.rearrange("(c p) -> p c", p=P), allow_slow_non_contiguous=True).then_inc(raw_ld, 16)

            def load_xs(k, s):
                for b in range(2):
                    sp.dma_start(xs[s][BLK * b:BLK * (b + 1), :, :],
                                 x_t[k].rearrange("q b t d -> b t q d")[b]).then_inc(xs_ld[s], 16)

            with sp.Fori(0, NBLK // 2) as i:
                for s in range(2):
                    sp.wait_ge(xs_used, i * 2)
                    load_xs(i * 2 + s, s)
            sp.dma_start(wo_s[:, :, :], Wo.rearrange("(c p) n -> p c n", p=P)).then_inc(const_ld, 16)
            sp.dma_start(rw_s[:, :, :], router_wT.rearrange("(c p) n -> p c n", p=P)).then_inc(const_ld, 16)
            sp.dma_start(wsgu_s[:, :, :], ws_gate_up.rearrange("(c p) n -> p c n", p=P)).then_inc(const_ld, 16)
            sp.dma_start(wsd_s[:, :, :], ws_down.rearrange("(c p) n -> p c n", p=FH)).then_inc(const_ld, 16)
            sp.dma_start(bo_s[:, :], bo.rearrange("(a n) -> a n", a=1)).then_inc(const_ld, 16)
            sp.dma_start(b2_s[:, :], b2.rearrange("(a n) -> a n", a=1)).then_inc(const_ld, 16)
            sp.dma_start(b1_in[:, :], b1.rearrange("(c p) -> p c", p=P), allow_slow_non_contiguous=True).then_inc(const_ld, 16)
            sp.wait_ge(consts, 5)
            sp.dma_start(xw_d[TOK:TOK + P, :], zeros[:, :]).then_inc(zero_st, 16)
            sp.dma_start(acc_d[TOK:TOK + P, :], zeros[:, 0:D]).then_inc(zero_st, 16)

            def front(f, k, q):
                sp.wait_ge(xa_ready, f)
                for b in range(2):
                    sp.dma_start(xt[BLK * b:BLK * (b + 1), :], x_t[k, q, b]).then_inc(xt_ld, 16)

            def load_window(k, par, jobs):
                sp.wait_ge(f_stored, jobs * FST)
                sp.sem_inc(passed, 1)
                for m in range(3):
                    for s in range(2):
                        sp.dma_start(win[m][:, par, s].rearrange("p d t -> p (d t)"), qkv_ld[k, m, s]).then_inc(win_ld, 16)
                for s in range(2):
                    sp.dma_start(gwin[:, par, s], gat_ld[k, s]).then_inc(win_ld, 16)

            with sp.Fori(0, AHEAD) as k:
                with sp.Fori(0, NB2) as q:
                    front(k * NB2 + q, k, q)
            load_window(0, 0, NB2)

            def route(I, k, q):
                sp.wait_ge(acc_ready, I * RT)
                for b in range(2):
                    sp.dma_start(x4[BLK * b:BLK * (b + 1), :, :], x_r[k, q, b]).then_inc(x4_ld, 16)
                sp.wait_ge(w_ready, I + 1)
                sp.sem_inc(passed, 1)
                sp.wait_ge(acc_ready, (I + 1) * RT)
                for b in range(2):
                    sp.dma_start(xw_r[k, q, b], xw[BLK * b:BLK * (b + 1), :, :]).then_inc(r_stored, 16)
                    sp.dma_start(acc_r[k, q, b], acc4[BLK * b:BLK * (b + 1), :, :]).then_inc(r_stored, 16)

            def experts(n):
                for r in range(RT):
                    e = n * RT + r
                    sp.wait_ge(y_done, e + (UNITS_R - RT + 1))
                    sp.dma_start(ew_g[r], w_gate[e].rearrange("(c p) f -> p c f", p=P)).then_inc(ew_ld[r], 16)
                    sp.dma_start(ew_u[r], w_up[e].rearrange("(c p) f -> p c f", p=P)).then_inc(ew_ld[r], 16)
                    sp.dma_start(ew_d[r], w_down[e].rearrange("(c p) f -> p c f", p=FH)).then_inc(ew_ld[r], 16)

            def back_load(c, r, slot_uses, k, q):
                sp.wait_ge(fin_ready, c)
                for b in range(2):
                    sp.dma_start(oT[r][:, :, b, :], o_ld[k, q, b]).then_inc(bk_ld[r], 16)
                    sp.dma_start(xn_b[r][BLK * b:BLK * (b + 1), :], xw_t[k, q, b, :, 0:D]).then_inc(bk_ld[r], 16)
                    sp.dma_start(ac_b[r][BLK * b:BLK * (b + 1), :], acc_t[k, q, b]).then_inc(bk_ld[r], 16)

            def back_store(c, r, k, q):
                sp.wait_ge(fin_ready, c + 1)
                for b in range(2):
                    sp.dma_start(out_t[k, q, b], fin[r][BLK * b:BLK * (b + 1), :]).then_inc(fin_st, 16)

            for phase, kb0, nb in PHASES:
                if phase == EXPERTS:
                    sp.wait_ge(cum_ready, 1)
                    sp.dma_start(cum_d[:, BLK:BLK + TOK], cum).then_inc(cum_st, 16)
                    sp.dma_start(cum_d[:, 0:BLK], zeros[0:E, 0:BLK]).then_inc(cum_st, 16)
                    sp.wait_ge(cum_st, 32)
                    cum_b = cum_d.rearrange("e (k j) -> k e j", j=BLK)
                    sp.dma_start(cur, cum_b[1:P + 1]).then_inc(cur_ld, 16)
                    sp.dma_start(prv, cum_b[0:P]).then_inc(cur_ld, 16)
                    sp.wait_ge(slots_ready, 1)
                if phase == BACK2:
                    sp.wait_ge(sc_done, 16 * E)
                    sp.dma_start(w1_s, w1.rearrange("(c p) n -> p c n", p=P)).then_inc(mlp_ld, 16)
                    sp.dma_start(w2_s, w2.rearrange("(c p) n -> p c n", p=P)).then_inc(mlp_ld, 16)
                with sp.Fori(0, nb) as kb:
                    if phase != BACK1:
                        sp.wait_ge(act_staged, (kb + kb0) * NB2)
                        sp.wait_ge(pool_staged, (kb + kb0) * NB2)
                        sp.wait_ge(win_ld, (kb + (kb0 + 1)) * 128)
                        load_window(kb + (kb0 + 1), (kb + (kb0 + 1)) & 1, (kb + (kb0 + 2)) * NB2)
                    if phase == BACK2:
                        sp.wait_ge(o_stored, kb * 32 + 32)
                        sp.sem_inc(passed, 1)
                    if phase == BACK2_LATE:
                        sp.wait_ge(o_stored, 6 * 16)
                    if phase == BACK1:
                        sp.wait_ge(o_stored, 7 * 16)
                    with sp.Fori(0, NB2 // 2) as jj:
                        for h in range(2):
                            I = iteration(kb0, kb, jj, h)
                            j = jj * 2 + h
                            if phase in (ROUTE, EXPERTS, BACK2):
                                front(I + AHEAD * NB2, kb + (kb0 + AHEAD), j)
                            if phase == ROUTE:
                                route(I, kb, j)
                            if phase == EXPERTS:
                                experts(kb * NB2 + j)
                            if phase == BACK2:
                                c = (kb * NB2 + j) * 2
                                for r in range(2):
                                    back_load(c, r, 0, kb * 2 + r, j)
                                for r in range(2):
                                    back_store(c + r, r, kb * 2 + r, j)
                            if phase == BACK2_LATE:
                                c = j * 2 + 4 * NB2
                                for r in range(2):
                                    back_load(c, r, 0, 4 + r, j)
                                for r in range(2):
                                    back_store(c + r, r, 4 + r, j)
                            if phase == BACK1:
                                c = j + 6 * NB2
                                back_load(c, h, 0, 6, j)
                                back_store(c, h, 6, j)
            sp.wait_ge(o_stored, 16 * NBLK)
            with sp.Fori(0, NB2 // 2) as jj:
                for r in range(2):
                    c = jj * 2 + r + 7 * NB2
                    back_load(c - r, r, 0, 7, jj * 2 + r)
                for r in range(2):
                    c = jj * 2 + r + 7 * NB2
                    back_store(c, r, 7, jj * 2 + r)
            sp.wait_ge(fin_st, 32 * NT)
            sp.wait_ge(r_stored, 64 * NB2 * 2)
            sp.wait_ge(zero_st, 32)
            sp.wait_ge(f_stored, FST * NT)

        @block.gpsimd
        def _(pool):
            count = [0]

            def link(ins):
                count[0] += 1
                ins.then_inc(pch, 1)
                pool.wait_ge(pch, count[0])

            def relink():
                pool.wait_ge(pch, count[0])
                pool.sem_clear(pch)
                count[0] = 0

            g = nc.gpsimd
            link(g.memset(ident[:, :], 0.0))
            g.memset(ones[:, :], 1.0).then_inc(consts, 1)
            g.memset(zeros[:, :], 0.0).then_inc(consts, 1)
            g.memset(half_pow[:, 0:1], -0.5)
            link(g.memset(half_pow[:, 1:2], 0.5))
            link(g.iota(iot[:, 0:CAP], [[1, CAP]], base=0, channel_multiplier=0))
            link(g.iota(iot[:, CAP:CAP + 1], [[0, 1]], base=0, channel_multiplier=1))
            g.tensor_copy(slot_row[:, :], iot[:, 0:CAP]).then_inc(consts, 1)
            g.tensor_copy(slot_col[:, :], iot[:, CAP:CAP + 1]).then_inc(consts, 1)
            g.affine_select(out=ident[:, :], in_=ident[:, :], compare_op=ALU.not_equal, fill=1.0,
                            base=0, pattern=[[-1, P]], channel_multiplier=1).then_inc(consts, 1)
            pool.sem_inc(prod_done, 2)

            def power(o, a, which, n):
                return g.tensor_tensor(o, a, half_pow[:, which:which + 1].to_broadcast([P, n]), ALU.pow)

            pool.wait_ge(stats_in, 1)
            link(g.tensor_scalar(tmp_st[:, :], var[:, :], EPS, None, ALU.add))
            link(power(rstd[:, :], tmp_st[:, :], 0, NT))
            link(g.tensor_tensor(tmp_st[:, :], var[:, :], rstd[:, :], ALU.mult))
            link(g.tensor_tensor(tmp_st[:, :], tmp_st[:, :], rstd[:, :], ALU.mult))
            link(g.tensor_scalar(tmp_st[:, :], tmp_st[:, :], EPS, None, ALU.add))
            link(power(sA[:, :], tmp_st[:, :], 0, NT))
            link(g.tensor_tensor(sA[:, :], sA[:, :], rstd[:, :], ALU.mult))
            link(g.tensor_scalar(tmp_st[:, :], mean[:, :], -1.0, None, ALU.mult))
            g.tensor_tensor(bA[:, :], tmp_st[:, :], sA[:, :], ALU.mult).then_inc(stats_done, 1)
            g.tensor_tensor(nmr[:, :], tmp_st[:, :], rstd[:, :], ALU.mult).then_inc(stats_done, 1)
            relink()

            def stage_values(L, h):
                par, t0 = lookup(L)
                pool.wait_ge(win_ld, ((L >> 3) + 1) * 128)
                pool.wait_ge(rec_done, L * 2)
                beta = gwin[:, par, :, 0, bass.ds(t0, ST)].rearrange("p s t -> p t s")
                gg = gwin[:, par, :, 1, bass.ds(t0, ST)].rearrange("p s t -> p t s")
                g.tensor_tensor(bg[h][:, :, :], beta, gg, ALU.mult)
                for s in range(2):
                    g.tensor_tensor(bv[h][:, :, s, :],
                                    win[2][:, par, s, :, bass.ds(t0, ST)].rearrange("p d t -> p t d"),
                                    gwin[:, par, s, 0, bass.ds(t0, ST)].unsqueeze(2).to_broadcast([P, ST, DH]),
                                    ALU.mult)

            def stage_norm(L):
                pool.wait_ge(n2_ready, L + 1)
                power(nrm[:, :], n2[:, :], 1, ST * 2).then_inc(nrm_ready, 1)

            def stage_keys(L, h):
                par, t0 = lookup(L)
                pool.wait_ge(rk_ready, L + 1)
                for s in range(2):
                    last = g.tensor_tensor(
                        kn[h][:, :, s, :],
                        win[1][:, par, s, :, bass.ds(t0, ST)].rearrange("p d t -> p t d"),
                        rk[:, :].rearrange("p (t s) -> p t s", s=2)[:, :, s].unsqueeze(2).to_broadcast([P, ST, DH]),
                        ALU.mult)
                last.then_inc(pool_staged, 1)

            def reads(I, h, half, j, mid_work=None):
                lo = half * HS
                pool.wait_ge(rec_done, I * 2 + (3 + half))
                pool.wait_ge(act_staged, I + 1)
                g.tensor_tensor(
                    rp[:, :, :].rearrange("p (a v) d -> p a v d", v=DH),
                    S[h][:, lo:lo + HS].rearrange("p t s (v d) -> p (t s) v d", v=DH),
                    qs[h][:, lo:lo + HS].rearrange("p t s d -> p (t s) d").unsqueeze(2).to_broadcast([P, HS * 2, DH, DH]),
                    ALU.mult).then_inc(prod_done, 1)
                if mid_work is not None:
                    mid_work()
                pool.wait_ge(prod_done, I * 2 + (3 + half))
                link(g.tensor_tensor(r1[:, :, :], rp[:, :, 0:8], rp[:, :, 8:16], ALU.add))
                link(g.tensor_tensor(r2[:, :, :], r1[:, :, 0:4], r1[:, :, 4:8], ALU.add))
                link(g.tensor_tensor(r3[:, :, :], r2[:, :, 0:2], r2[:, :, 2:4], ALU.add))
                a = r3[:, :, :].rearrange("p (t s v) c -> p s v t c", t=HS, s=2)
                for s in range(2):
                    link(g.tensor_tensor(oblk[:, s, :, bass.ds(j * ST + lo, HS)], a[:, s, :, :, 0], a[:, s, :, :, 1], ALU.add))

            def gather(n):
                pool.wait_ge(sc_done, n * (16 * RT))
                link(g.tensor_copy(idx4[:, :], idx_i[:, bass.ds(n * RT, RT)]))
                for r in range(RT):
                    g.indirect_dma_start(xg[r], None, xw_d[:, :],
                                         bass.IndirectOffsetOnAxis(ap=idx4[:, r:r + 1], axis=0)).then_inc(g_ld[r], 16)

            def scatter(e, r):
                pool.wait_ge(yw_ready, e + 1)
                pool.wait_ge(sc_done, e * 16)
                pool.sem_inc(passed, 1)
                g.indirect_dma_start(acc_d[:, :], bass.IndirectOffsetOnAxis(ap=idx4[:, r:r + 1], axis=0),
                                     yw[r], None, compute_op=ALU.add).then_inc(sc_done, 16)

            stage_values(0, 0)
            stage_norm(0)
            stage_keys(0, 0)
            for phase, kb0, nb in PHASES:
                if phase == EXPERTS:
                    pool.wait_ge(slots_ready, 1)
                    pool.wait_ge(r_stored, 64 * 2 * NB2)
                    pool.wait_ge(zero_st, 32)

                def body(kb, jj, h, last=False):
                    I = iteration(kb0, kb, jj, h)
                    j = jj * 2 + h
                    n = kb * NB2 + j
                    if phase == EXPERTS:
                        gather(n)
                    if not last:
                        stage_values(I + 1, 1 - h)
                        stage_norm(I + 1)
                    if phase == EXPERTS:
                        reads(I, h, 0, j, lambda: scatter(n * RT, 0))
                        scatter(n * RT + 1, 1)
                    else:
                        reads(I, h, 0, j)
                    if not last:
                        stage_keys(I + 1, 1 - h)
                    if phase == EXPERTS:
                        scatter(n * RT + 2, 2)
                        reads(I, h, 1, j, lambda: scatter(n * RT + 3, 3))
                    else:
                        reads(I, h, 1, j)

                with pool.Fori(0, nb) as kb:
                    pool.wait_ge(o_stored, (kb + kb0) * 16)
                    pool.sem_inc(passed, 1)
                    if phase != BACK1:
                        with pool.Fori(0, NB2 // 2) as jj:
                            body(kb, jj, 0)
                            body(kb, jj, 1)
                            relink()
                    else:
                        with pool.Fori(0, NB2 // 2 - 1) as jj:
                            body(kb, jj, 0)
                            body(kb, jj, 1)
                            relink()
                        body(kb, NB2 // 2 - 1, 0)
                        body(kb, NB2 // 2 - 1, 1, last=True)
                        relink()
                    g.dma_start(o_st[kb + kb0], oblk[:, :, :, :].rearrange("p s v t -> p s (v t)")).then_inc(o_stored, 16)
            pool.wait_ge(o_stored, 16 * NBLK)

        @block.vector
        def _(dve):
            v = nc.vector
            count = [0]

            def mark(ins):
                count[0] += 1
                ins.then_inc(vch, 1)
                return count[0]

            def link(ins):
                dve.wait_ge(vch, mark(ins))

            def relink():
                dve.wait_ge(vch, count[0])
                dve.sem_clear(vch)
                count[0] = 0

            with dve.Fori(0, NBLK // 2) as i:
                for s in range(2):
                    dve.wait_ge(xs_ld[s], i * 32 + 32)
                    for q in range(NB2):
                        m = mark(v.bn_stats(bn6[:, q, :], xs[s][:, q, :]))
                    dve.wait_ge(vch, m)
                    for q in range(NB2):
                        m = mark(v.bn_aggr(mv8[:, q, :], bn6[:, q, :]))
                    dve.wait_ge(vch, m)
                    v.tensor_copy(mean[:, bass.ds((i * 2 + s) * NB2, NB2)], mv8[:, :, 0])
                    v.tensor_copy(var[:, bass.ds((i * 2 + s) * NB2, NB2)], mv8[:, :, 1]).then_inc(xs_used, 1)
                    dve.wait_ge(xs_used, i * 2 + (s + 1))
                    dve.sem_inc(passed, 1)
                relink()
            dve.sem_inc(h_ready, 1)
            link(v.memset(S[1][:, ST - 1], 0.0))
            dve.sem_inc(stats_in, 1)
            dve.sem_inc(rec_done, 2)
            relink()

            def norms(L, part):
                if part == 0:
                    dve.wait_ge(sq_ready, L + 1)
                    v.tensor_reduce(n2[:, :], sq[:, :, :], AX.X, ALU.add).then_inc(n2_ready, 1)
                else:
                    dve.wait_ge(nrm_ready, L + 1)
                    link(v.tensor_scalar(nrm_e[:, :], nrm[:, :], 1e-6, None, ALU.add))
                    v.reciprocal(rk[:, :], nrm_e[:, :]).then_inc(rk_ready, 1)

            def unit_product(q):
                dve.wait_ge(sg_ready, q + 1)
                dve.wait_ge(y_done, q)
                b = GUB[0]
                v.tensor_tensor(hg_s[:, :, :].rearrange("p a t -> p (a t)"), sgu[:, :], b[0:FH, 2 * P:4 * P],
                                ALU.mult).then_inc(h_ready, 1)

            GUB = [None]

            def product(q, r):
                GUB[0] = (G0, G1)[r % 2]
                unit_product(q)

            def route_sum(q, r):
                dve.wait_ge(y_done, q + 1)
                v.tensor_tensor(acc4[:, r, :], YB[:, 0:D], x4[:, r, :], ALU.add).then_inc(acc_ready, 1)

            def top8(I):
                dve.wait_ge(lg_copied, I + 1)
                dve.sem_inc(passed, 1)
                for r in range(RT):
                    m = mark(v.max(mx[:, r, :], lg[:, r, :]))
                dve.wait_ge(vch, m)
                v.tensor_scalar(negm, mx[:, :, 0], -1.0, None, ALU.mult).then_inc(negm_ready, 1)
                for r in range(RT):
                    m = mark(v.match_replace(rep[:, r, :], mx[:, r, :], lg[:, r, :], -3.0e38))
                dve.wait_ge(vch, m)
                v.tensor_tensor(mk, rep, lg, ALU.not_equal).then_inc(mask_ready, 1)

            def top8_weights(I):
                dve.wait_ge(mask_ready, I + 1)
                dve.wait_ge(e_ready, I + 1)
                link(v.tensor_tensor(wt, ex, mk, ALU.mult))
                link(v.tensor_reduce(wsum, wt, AX.X, ALU.add))
                link(v.reciprocal(wrec, wsum))
                v.tensor_tensor(xw[:, :, D:XW], wt, wrec.unsqueeze(2).to_broadcast([P, RT, E]),
                                ALU.mult).then_inc(w_ready, 1)

            def back_x1(c, r):
                dve.wait_ge(at_done, c + 1)
                bk = (TB, LG)[r]
                m = mark(v.tensor_tensor(x1[r], bk[:, 0:D], xn_b[r], ALU.add))
                dve.wait_ge(vch, m)
                m = mark(v.bn_stats(bn_b[:, r, :], x1[r]))
                dve.wait_ge(vch, m)
                link(v.bn_aggr(mv_b[:, r, :], bn_b[:, r, :]))
                v.tensor_scalar(ve_b[:, r:r + 1], mv_b[:, r, 1:2], EPS, None, ALU.add).then_inc(ve_ready, 1)

            def back_rstd(c, r):
                dve.wait_ge(sd_ready, c + 1)
                link(v.reciprocal(rs_b[:, r:r + 1], sd_b[:, r:r + 1]))
                v.scalar_tensor_tensor(nb_b[:, r:r + 1], mv_b[:, r, 0:1], -1.0, rs_b[:, r:r + 1],
                                       ALU.mult, ALU.mult).then_inc(nb_ready, 1)

            def back_sum(c, r, ob):
                dve.wait_ge(out_done, c + 1)
                link(v.tensor_tensor(fin[r], ob[:, 0:D], x1[r], ALU.add))
                v.tensor_tensor(fin[r], fin[r], ac_b[r], ALU.add).then_inc(fin_ready, 1)

            OUTB = (YB, LG)

            def step(I, h, s, ready):
                before = S[h][:, s - 1] if s else S[1 - h][:, ST - 1]
                key = [kn[h][:, s, G, :].unsqueeze(1).to_broadcast([P, DH, DH]) for G in range(2)]
                m = [0, 0]
                for G in range(2):
                    if ready[G] is not None:
                        dve.wait_ge(*ready[G])
                    m[G] = mark(v.tensor_tensor(prod[:, G].rearrange("p (v d) -> p v d", v=DH),
                                                before[:, G].rearrange("p (v d) -> p v d", v=DH), key[G], ALU.mult))
                for G in range(2):
                    dve.wait_ge(vch, m[G])
                    m[G] = mark(v.tensor_reduce(kS[:, G], prod[:, G].rearrange("p (v d) -> p v d", v=DH), AX.X, ALU.add))
                for G in range(2):
                    dve.wait_ge(vch, m[G])
                    m[G] = mark(v.scalar_tensor_tensor(nu[:, G], kS[:, G], bg[h][:, s, G:G + 1], bv[h][:, s, G, :],
                                                       ALU.mult, ALU.subtract))
                for G in range(2):
                    dve.wait_ge(vch, m[G])
                    m[G] = mark(v.tensor_tensor(outer[:, G].rearrange("p (v d) -> p v d", v=DH),
                                                nu[:, G].unsqueeze(2).to_broadcast([P, DH, DH]), key[G], ALU.mult))
                for G in range(2):
                    dve.wait_ge(vch, m[G])
                    ins = v.scalar_tensor_tensor(S[h][:, s, G], before[:, G], g8[h][:, s, G:G + 1], outer[:, G],
                                                 ALU.mult, ALU.subtract)
                    if G == 1 and s in (HS - 1, ST - 1):
                        ins.then_inc(rec_done, 1)
                        ready[G] = (rec_done, I * 2 + (3 if s == HS - 1 else 4))
                    else:
                        ready[G] = (vch, mark(ins))

            def slots():
                dve.wait_ge(mT_ready, 2 * NB2)
                dve.wait_ge(r_stored, 64 * 2 * NB2)
                v.tensor_tensor_scan(cum, ones[0:E, 0:1].to_broadcast([E, TOK]), maskT, 0.0,
                                     ALU.mult, ALU.add).then_inc(cum_ready, 1)
                dve.wait_ge(cum_ready, 1)
                for a in range(2):
                    link(v.memset(diff[a][:, :, BLK:CW], float(BLK)))
                dve.wait_ge(cur_ld, 32)
                relink()
                with dve.Fori(0, E // RT // 2) as i:
                    for a in range(2):
                        e0 = (i * 2 + a) * RT
                        dve.wait_ge(slot_mm, i * 2)
                        for r in range(RT):
                            v.tensor_scalar(onh[a][:, r, :], slot_row[:, :], prv[:, e0 + r, BLK - 1:BLK],
                                            None, ALU.is_ge)
                        v.tensor_tensor(diff[a][:, :, 0:BLK], cur[:, bass.ds(e0, RT), :], prv[:, bass.ds(e0, RT), :],
                                        ALU.subtract).then_inc(onh_ready, 1)
                    for a in range(2):
                        e0 = (i * 2 + a) * RT
                        dve.wait_ge(slot_mm, i * 2 + (a + 1))
                        ps = (LG, TB)[a][:, 0:RT * CW].rearrange("p (r j) -> p r j", r=RT)
                        link(v.tensor_scalar(cnt[a], ps[:, :, 0:BLK], slot_col[:, 0:1], None, ALU.is_le))
                        link(v.tensor_reduce(csum[a], cnt[a], AX.X, ALU.add))
                        v.scalar_tensor_tensor(sidx[:, bass.ds(e0, RT)], csum[a], -float(BLK), ps[:, :, BLK],
                                               ALU.add, ALU.add).then_inc(slot_used, 1)
                    relink()
                dve.wait_ge(slot_used, E // RT)
                link(v.tensor_scalar(sgei, sidx, float(TOK), None, ALU.is_ge))
                link(v.scalar_tensor_tensor(sidx, sgei, slot_col[:, 0:1], sidx, ALU.mult, ALU.add))
                v.tensor_copy(idx_i[:, :], sidx).then_inc(slots_ready, 1)
                relink()

            norms(0, 0)
            norms(0, 1)
            relink()
            for phase, kb0, nb in PHASES:
                if phase == EXPERTS:
                    slots()
                if phase == BACK2:
                    dve.wait_ge(mlp_bias, 1)
                    v.tensor_tensor(b1_s[:, :], TB[:, 0:MC], b1_in[:, :], ALU.add).then_inc(mlp_bias, 1)

                def body(kb, jj, h, ready, last=False):
                    I = iteration(kb0, kb, jj, h)
                    j = jj * 2 + h
                    n = kb * NB2 + j
                    dve.wait_ge(pool_staged, I + 1)
                    dve.wait_ge(act_staged, I + 1)
                    dve.wait_ge(prod_done, I * 2)
                    ready[1] = (rec_done, I * 2 + 2)
                    if phase in (BACK2, BACK2_LATE):
                        c = n * 2 + (0 if phase == BACK2 else 4 * NB2)
                        rs = (0, 1)
                    elif phase == BACK1:
                        c = j + (6 * NB2 - h)
                        rs = (h,)
                    for s in range(ST):
                        step(I, h, s, ready)
                        if s == 1 and not last:
                            norms(I + 1, 0)
                        if s == 4 and not last:
                            norms(I + 1, 1)
                        if phase in (ROUTE, EXPERTS):
                            q = n * RT + (0 if phase == ROUTE else UNITS_R)
                            r = {2: 0, 4: 1, 5: 2, 6: 3}.get(s)
                            if r is not None:
                                product(q + r, r)
                            r = {4: 0, 5: 1, 6: 2, 7: 3}.get(s)
                            if phase == ROUTE and r is not None:
                                route_sum(q + r, r)
                            if phase == ROUTE and s == 7:
                                top8(I)
                                top8_weights(I)
                        else:
                            if s == 0:
                                for r in rs:
                                    back_x1(c + r, r)
                            if s == 1:
                                for r in rs:
                                    back_rstd(c + r, r)
                            if s == 6 and len(rs) == 2:
                                back_sum(c, 0, OUTB[0])
                            if s == 7:
                                back_sum(c + rs[-1], rs[-1], OUTB[rs[-1]])

                def pair(kb, jj, last=False):
                    ready = [None, None]
                    body(kb, jj, 0, ready)
                    body(kb, jj, 1, ready, last)
                    relink()

                with dve.Fori(0, nb) as kb:
                    if phase != BACK1:
                        with dve.Fori(0, NB2 // 2) as jj:
                            pair(kb, jj)
                    else:
                        with dve.Fori(0, NB2 // 2 - 1) as jj:
                            pair(kb, jj)
                        pair(kb, NB2 // 2 - 1, last=True)
            with dve.Fori(0, NB2 // 2) as jj:
                c = jj * 2 + 7 * NB2
                for r in range(2):
                    back_x1(c + r, r)
                for r in range(2):
                    back_rstd(c + r, r)
                for r in range(2):
                    back_sum(c + r, r, OUTB[r])
                relink()

        @block.scalar
        def _(act):
            a_ = nc.scalar
            act.sem_inc(gelu_done, 1)
            act.wait_ge(raw_ld, 16 * 9)
            for c in range(DC):
                a_.activation(wqkvg[:, c, :], wraw[:, c, :], ACT.Copy, scale=lncol[:, 0, c:c + 1]).then_inc(w_scaled, 1)
            act.wait_ge(bias_mm, 1)
            a_.activation(bqkv[:, 0:2], FT[:, 0:2], ACT.Copy, scale=DH ** -0.5).then_inc(bias_done, 1)
            a_.activation(bqkv[:, 2:6], FT[:, 2:6], ACT.Copy).then_inc(bias_done, 1)
            a_.activation(bqkv[0:2 * H, 6:7], FT[0:2 * H, 6:7], ACT.Copy).then_inc(bias_done, 1)
            act.wait_ge(stats_done, 2)
            act.wait_ge(bias_done, 3)

            def front_norm(f):
                act.wait_ge(xt_ld, f * 32 + 32)
                act.wait_ge(fT_done, f)
                a_.activation(xa[:, :], xt[:, :], ACT.Identity, scale=sA[:, bass.ds(f, 1)],
                              bias=bA[:, bass.ds(f, 1)]).then_inc(xa_ready, 1)

            def front_evac(f):
                act.wait_ge(fT_done, f + 1)
                act.wait_ge(qkv_done, f)
                a_.activation(xaT[:, :, :].rearrange("p c t -> p (c t)"), FT[:, 0:DC * P], ACT.Copy).then_inc(xaT_ready, 1)

            def front_out(f, k, q):
                act.wait_ge(qkv_done, f + 1)
                act.wait_ge(f_stored, f * FST)
                for m in range(3):
                    for hg in range(2):
                        i = m * 2 + hg
                        src = FQ[:, i * P:(i + 1) * P] if i < 4 else FV[:, (i - 4) * P:(i - 3) * P]
                        a_.activation(stg[:, i, :], src, ACT.Identity, bias=bqkv[:, i:i + 1],
                                      scale=DH ** -0.5 if m == 0 else 1.0)
                a_.activation(gst[:, :], FV[0:2 * H, 2 * P:3 * P], ACT.Sigmoid, bias=bqkv[0:2 * H, 6:7]).then_inc(stg_ready, 1)
                act.wait_ge(stg_ready, f + 1)
                for b in range(2):
                    for m in range(3):
                        act.dma_start(qkv_st[k, q, b, :, m], stg[:, 2 * m:2 * m + 2, BLK * b:BLK * (b + 1)]).then_inc(f_stored, 16)
                    for w in range(2):
                        act.dma_start(gat_st[k, q, b, w], gst[w * H:(w + 1) * H, BLK * b:BLK * (b + 1)]).then_inc(f_stored, 16)

            def stage(L, h):
                par, t0 = lookup(L)
                act.wait_ge(win_ld, ((L >> 3) + 1) * 128)
                act.wait_ge(n2_ready, L)
                for s in range(2):
                    last = a_.activation(sq[:, :, :].rearrange("p (t s) d -> p t s d", s=2)[:, :, s],
                                         win[1][:, par, s, :, bass.ds(t0, ST)].rearrange("p d t -> p t d"), ACT.Square)
                last.then_inc(sq_ready, 1)
                act.wait_ge(prod_done, L * 2)
                act.wait_ge(rec_done, L * 2)
                for s in range(2):
                    a_.activation(qs[h][:, :, s, :], win[0][:, par, s, :, bass.ds(t0, ST)].rearrange("p d t -> p t d"),
                                  ACT.Copy)
                a_.activation(g8[h][:, :, :], gwin[:, par, :, 1, bass.ds(t0, ST)].rearrange("p s t -> p t s"),
                              ACT.Copy).then_inc(act_staged, 1)

            def route_norm(I, k, q):
                act.wait_ge(x4_ld, I * 32 + 32)
                act.wait_ge(r_stored, I * 64)
                for r in range(RT):
                    tile = (k * RT + r) * NB2 + q
                    a_.activation(xw[:, r, 0:D], x4[:, r, :], ACT.Identity, scale=rstd[:, bass.ds(tile, 1)],
                                  bias=nmr[:, bass.ds(tile, 1)]).then_inc(xn_ready, 1)

            def unit_evac(q):
                act.wait_ge(t_done, q + 1)
                act.wait_ge(gu_done, q)
                a_.activation(gT[:, :, :].rearrange("p c t -> p (c t)"), TB[:, 0:DC * P], ACT.Copy).then_inc(gT_ready, 1)

            def unit_silu(q, r):
                act.wait_ge(gu_done, q + 1)
                act.wait_ge(h_ready, q + 1)
                a_.activation(sgu[:, :], (G0, G1)[r % 2][0:FH, 0:2 * P], ACT.Silu).then_inc(sg_ready, 1)

            def expert_out(e, r):
                act.wait_ge(y_done, e + (UNITS_R + 1))
                a_.activation(yw[r], YB[:, 0:D], ACT.Copy, scale=xg[r][:, bass.ds(e + D, 1)]).then_inc(yw_ready, 1)

            with act.Fori(0, AHEAD) as k:
                with act.Fori(0, NB2) as q:
                    f = k * NB2 + q
                    front_norm(f)
                    front_evac(f)
                    front_out(f, k, q)
            stage(0, 0)

            def back_sqrt(c, rs):
                act.wait_ge(ve_ready, c + len(rs))
                for r in rs:
                    a_.activation(sd_b[:, r:r + 1], ve_b[:, r:r + 1], ACT.Sqrt).then_inc(sd_ready, 1)

            def back_norm(c, r):
                act.wait_ge(nb_ready, c + 1)
                a_.activation(hb[r], x1[r], ACT.Identity, scale=rs_b[:, r:r + 1], bias=nb_b[:, r:r + 1]).then_inc(hb_ready, 1)

            def back_evac(c, r):
                act.wait_ge(hT_done, c + 1)
                a_.activation(hT[r].rearrange("p c t -> p (c t)"), (TB, LG)[r][:, D:2 * D], ACT.Copy).then_inc(hT_ready, 1)

            def back_gelu(c, r, half):
                act.wait_ge(mid_done, c * 2 + (half + 1))
                for i in range(MC // 2):
                    m = half * (MC // 2) + i
                    last = a_.activation(mid[r][:, m, :], (G0, G1)[half][:, i * P:(i + 1) * P], ACT.Gelu, bias=b1_s[:, m:m + 1])
                last.then_inc(gelu_done, 1)

            for phase, kb0, nb in PHASES:
                if phase == BACK2:
                    act.wait_ge(mlp_bias, 2)
                    for c in range(DC):
                        a_.activation(w1_s[:, c, :], w1_s[:, c, :], ACT.Copy, scale=lncol[:, 2, c:c + 1]).then_inc(mlp_w, 1)

                def body(kb, jj, h, last=False):
                    I = iteration(kb0, kb, jj, h)
                    j = jj * 2 + h
                    n = kb * NB2 + j
                    f, k = I + AHEAD * NB2, kb + (kb0 + AHEAD)
                    if not last:
                        stage(I + 1, 1 - h)
                    if phase in (ROUTE, EXPERTS):
                        q = n * RT + (0 if phase == ROUTE else UNITS_R)
                        front_norm(f)
                        if phase == ROUTE:
                            route_norm(I, kb, j)
                        unit_evac(q)
                        front_evac(f)
                        unit_silu(q, 0)
                        front_out(f, k, j)
                        unit_evac(q + 1)
                        unit_silu(q + 1, 1)
                        unit_evac(q + 2)
                        if phase == EXPERTS:
                            expert_out(n * RT, 0)
                        unit_silu(q + 2, 2)
                        unit_evac(q + 3)
                        if phase == EXPERTS:
                            expert_out(n * RT + 1, 1)
                        unit_silu(q + 3, 3)
                        if phase == EXPERTS:
                            expert_out(n * RT + 2, 2)
                            expert_out(n * RT + 3, 3)
                        else:
                            act.wait_ge(lg_done, I + 1)
                            act.wait_ge(w_ready, I)
                            a_.activation(lg.rearrange("p r e -> p (r e)"), LG[:, 0:RT * E], ACT.Copy).then_inc(lg_copied, 1)
                            act.wait_ge(negm_ready, I + 1)
                            for r in range(RT):
                                x_ = a_.activation(ex[:, r, :], lg[:, r, :], ACT.Exp, bias=negm[:, r:r + 1])
                            x_.then_inc(e_ready, 1)
                            act.wait_ge(mt_done, I + 1)
                            for r in range(RT):
                                x_ = a_.activation(maskT_v[:, j, kb, r],
                                                   LG[0:E, r * P:(r + 1) * P].rearrange("e (b t) -> e b t", b=2), ACT.Copy)
                            x_.then_inc(mT_ready, 1)
                        return
                    if phase == BACK1:
                        c, rs = j + (6 * NB2 - h), (h,)
                    else:
                        c, rs = n * 2 + (0 if phase == BACK2 else 4 * NB2), (0, 1)
                    if phase == BACK2:
                        front_norm(f)
                        front_evac(f)
                    back_act(c, rs, (lambda: front_out(f, k, j)) if phase == BACK2 else None)

                def back_act(c, rs, between):
                    c0 = c + rs[0]
                    back_sqrt(c0, rs)
                    for r in rs:
                        back_norm(c + r, r)
                    if between is not None:
                        between()
                    for r in rs:
                        back_evac(c + r, r)
                    for r in rs:
                        for half in range(2):
                            back_gelu(c + r, r, half)

                with act.Fori(0, nb) as kb:
                    if phase != BACK1:
                        with act.Fori(0, NB2 // 2) as jj:
                            body(kb, jj, 0)
                            body(kb, jj, 1)
                    else:
                        with act.Fori(0, NB2 // 2 - 1) as jj:
                            body(kb, jj, 0)
                            body(kb, jj, 1)
                        body(kb, NB2 // 2 - 1, 0)
                        body(kb, NB2 // 2 - 1, 1, last=True)
            with act.Fori(0, NB2 // 2) as jj:
                back_act(jj * 2 + 7 * NB2, (0, 1), None)

        @block.tensor
        def _(pe):
            mm = nc.tensor.matmul
            pe.wait_ge(consts, 5)
            pe.wait_ge(raw_ld, 16 * 9)
            for i in range(7):
                n = P if i < 6 else 2 * H
                for c in range(DC):
                    last = mm(FT[0:n, i:i + 1], wraw[:, c, i * P:i * P + n], lncol[:, 1, c:c + 1], start=(c == 0), stop=(c == DC - 1))
            last.then_inc(bias_mm, 1)
            pe.wait_ge(w_scaled, DC)
            pe.wait_ge(bias_done, 3)
            pe.wait_ge(const_ld, 16 * 7)

            def front_T(f):
                pe.wait_ge(xa_ready, f + 1)
                pe.wait_ge(xaT_ready, f)
                for c in range(DC):
                    last = nc.tensor.transpose(FT[:, c * P:(c + 1) * P], xa[:, c * P:(c + 1) * P], ident[:, :])
                last.then_inc(fT_done, 1)

            def front_mm(f):
                pe.wait_ge(xaT_ready, f + 1)
                pe.wait_ge(stg_ready, f)
                for i in range(7):
                    n = P if i < 6 else 2 * H
                    dst = FQ[:, i * P:(i + 1) * P] if i < 4 else FV[0:n, (i - 4) * P:(i - 3) * P]
                    for c in range(DC):
                        last = mm(dst, wqkvg[:, c, i * P:i * P + n], xaT[:, c, :], start=(c == 0), stop=(c == DC - 1))
                last.then_inc(qkv_done, 1)

            def unit_T(q, src):
                pe.wait_ge(gT_ready, q)
                for c in range(DC):
                    last = nc.tensor.transpose(TB[:, c * P:(c + 1) * P], src[:, c * P:(c + 1) * P], ident[:, :])
                last.then_inc(t_done, 1)

            def unit_gu(q, r, wg, wu):
                pe.wait_ge(h_ready, q)
                bk = (G0, G1)[r % 2]
                for i in range(4):
                    w = wg if i < 2 else wu
                    for c in range(DC):
                        last = mm(bk[0:FH, i * P:(i + 1) * P], w[:, c, (i % 2) * FH:(i % 2 + 1) * FH], gT[:, c, :],
                                  start=(c == 0), stop=(c == DC - 1))
                last.then_inc(gu_done, 1)

            def unit_y(q, wd, bias):
                pe.wait_ge(h_ready, q + 2)
                for c in range(2):
                    last = mm(YB[:, 0:D], hg_s[:, c, :], wd[:, c, :], start=(c == 0), stop=(c == 1 and bias is None))
                if bias is not None:
                    last = mm(YB[:, 0:D], ones[0:1, :], bias, start=False, stop=True)
                last.then_inc(y_done, 1)

            with pe.Fori(0, AHEAD) as k:
                with pe.Fori(0, NB2) as q:
                    f = k * NB2 + q
                    front_T(f)
                    front_mm(f)

            def route_T(I, q, r):
                pe.wait_ge(xn_ready, q + 1)
                unit_T(q, xw[:, r, :])

            def route_gu(I, q, r):
                pe.wait_ge(gT_ready, q + 1)
                if r == 0:
                    pe.wait_ge(mT_ready, I)
                for c in range(DC):
                    last = mm(LG[:, r * E:(r + 1) * E], gT[:, c, :], rw_s[:, c, :], start=(c == 0), stop=(c == DC - 1))
                if r == RT - 1:
                    last.then_inc(lg_done, 1)
                unit_gu(q, r, wsgu_s[:, :, 0:F], wsgu_s[:, :, F:2 * F])

            def route_y(q):
                pe.wait_ge(acc_ready, q)
                unit_y(q, wsd_s[:, :, :], b2_s[0:1, :])

            def expert_T(n, q, r):
                pe.wait_ge(g_ld[r], n * 16 + 16)
                unit_T(q, xg[r])

            def expert_gu(n, q, r):
                pe.wait_ge(gT_ready, q + 1)
                pe.wait_ge(ew_ld[r], n * 48 + 48)
                unit_gu(q, r, ew_g[r], ew_u[r])

            def expert_y(e, r):
                pe.wait_ge(yw_ready, e)
                unit_y(e + UNITS_R, ew_d[r], None)

            def back_attn(c, r, use):
                pe.wait_ge(bk_ld[r], use * 96 + 96)
                bk = (TB, LG)[r]
                for g in range(2):
                    mm(bk[:, 0:D], oT[r][:, g].rearrange("p b t -> p (b t)"), wo_s[:, g, :], start=(g == 0), stop=False)
                mm(bk[:, 0:D], ones[0:1, :], bo_s[0:1, :], start=False, stop=True).then_inc(at_done, 1)

            def back_T(c, r):
                pe.wait_ge(hb_ready, c + 1)
                for i in range(DC):
                    last = nc.tensor.transpose((TB, LG)[r][:, D + i * P:D + (i + 1) * P], hb[r][:, i * P:(i + 1) * P], ident[:, :])
                last.then_inc(hT_done, 1)

            def back_mid(c, r, half):
                if half == 0:
                    pe.wait_ge(hT_ready, c + 1)
                pe.wait_ge(gelu_done, c * 2 + half)
                for i in range(MC // 2):
                    m = half * (MC // 2) + i
                    for k in range(DC):
                        last = mm((G0, G1)[half][:, i * P:(i + 1) * P], w1_s[:, k, m * P:(m + 1) * P], hT[r][:, k, :],
                                  start=(k == 0), stop=(k == DC - 1))
                last.then_inc(mid_done, 1)

            def back_out(c, r):
                pe.wait_ge(gelu_done, c * 2 + 3)
                for m in range(MC):
                    last = mm((YB, LG)[r][:, 0:D], mid[r][:, m, :], w2_s[:, m, :], start=(m == 0), stop=(m == MC - 1))
                last.then_inc(out_done, 1)

            def back_mlp(c, rs):
                for r in rs:
                    back_T(c + r, r)
                back_mid(c + rs[0], rs[0], 0)
                back_mid(c + rs[0], rs[0], 1)
                if len(rs) == 2:
                    back_mid(c + 1, 1, 0)
                    back_out(c, 0)
                    back_mid(c + 1, 1, 1)
                back_out(c + rs[-1], rs[-1])

            for phase, kb0, nb in PHASES:
                if phase == EXPERTS:
                    pe.wait_ge(mT_ready, 2 * NB2)
                    with pe.Fori(0, E // RT // 2) as i:
                        for a in range(2):
                            pe.wait_ge(onh_ready, i * 2 + (a + 1))
                            pe.wait_ge(slot_used, i * 2)
                            for r in range(RT):
                                last = mm((LG, TB)[a][:, r * CW:(r + 1) * CW], onh[a][:, r, :], diff[a][:, r, :], start=True, stop=True)
                            last.then_inc(slot_mm, 1)
                    pe.wait_ge(slot_used, E // RT)
                    pe.wait_ge(acc_ready, NT)
                if phase == BACK2:
                    pe.wait_ge(h_ready, NT + E + 1)
                    pe.wait_ge(yw_ready, E)
                    pe.wait_ge(mlp_ld, 32)
                    for m in range(MC):
                        for c in range(DC):
                            last = mm(TB[:, m:m + 1], w1_s[:, c, m * P:(m + 1) * P], lncol[:, 3, c:c + 1],
                                      start=(c == 0), stop=(c == DC - 1))
                    last.then_inc(mlp_bias, 1)
                    pe.wait_ge(mlp_bias, 2)
                    pe.wait_ge(mlp_w, DC)
                with pe.Fori(0, nb) as kb:
                    with pe.Fori(0, NB2 // 2) as jj:
                        for h in range(2):
                            I = iteration(kb0, kb, jj, h)
                            j = jj * 2 + h
                            n = kb * NB2 + j
                            f = I + AHEAD * NB2
                            if phase == ROUTE:
                                q = n * RT
                                route_T(I, q, 0)
                                front_T(f)
                                route_gu(I, q, 0)
                                front_mm(f)
                                route_T(I, q + 1, 1)
                                route_gu(I, q + 1, 1)
                                route_y(q)
                                route_T(I, q + 2, 2)
                                route_gu(I, q + 2, 2)
                                route_y(q + 1)
                                route_T(I, q + 3, 3)
                                route_gu(I, q + 3, 3)
                                route_y(q + 2)
                                route_y(q + 3)
                                pe.wait_ge(mask_ready, I + 1)
                                pe.wait_ge(lg_copied, I + 1)
                                pe.sem_inc(passed, 1)
                                for r in range(RT):
                                    last = nc.tensor.transpose(LG[0:E, r * P:(r + 1) * P], mk[:, r, :], ident[:, :])
                                last.then_inc(mt_done, 1)
                            elif phase == EXPERTS:
                                q = n * RT + UNITS_R
                                expert_T(n, q, 0)
                                front_T(f)
                                expert_gu(n, q, 0)
                                front_mm(f)
                                expert_T(n, q + 1, 1)
                                expert_gu(n, q + 1, 1)
                                expert_y(n * RT, 0)
                                expert_T(n, q + 2, 2)
                                expert_gu(n, q + 2, 2)
                                expert_y(n * RT + 1, 1)
                                expert_T(n, q + 3, 3)
                                expert_gu(n, q + 3, 3)
                                expert_y(n * RT + 2, 2)
                                expert_y(n * RT + 3, 3)
                            else:
                                if phase == BACK1:
                                    c, rs, use = j + (6 * NB2 - h), (h,), jj + 24
                                elif phase == BACK2:
                                    c, rs, use = n * 2, (0, 1), n
                                else:
                                    c, rs, use = n * 2 + 4 * NB2, (0, 1), n + 16
                                for r in rs:
                                    back_attn(c + r, r, use)
                                if phase == BACK2:
                                    front_T(f)
                                    front_mm(f)
                                back_mlp(c, rs)
            with pe.Fori(0, NB2 // 2) as jj:
                c = jj * 2 + 7 * NB2
                for r in range(2):
                    back_attn(c + r, r, jj + 28)
                back_mlp(c, (0, 1))


_INS = ['L0_attn_x', 'L0_attn_Wq', 'L0_attn_Wk', 'L0_attn_Wv', 'L0_attn_Wb', 'L0_attn_Wg', 'L0_attn_Wo', 'L0_attn_bo',
        'L0_attn_ln1_g', 'L0_attn_ln1_b', 'L0_attn_ln2_g', 'L0_attn_ln2_b', 'L0_attn_w1', 'L0_attn_b1', 'L0_attn_w2',
        'L0_attn_b2', 'L0_ffn_router_w', 'L0_ffn_w_gate', 'L0_ffn_w_up', 'L0_ffn_w_down', 'L0_ffn_ws_gate_up',
        'L0_ffn_ws_down']


def kernel(**inputs):
    import numpy as _np
    import concourse.bacc as _bacc
    from concourse import mybir as _mybir
    from concourse.bass_utils import run_bass_kernel_spmd as _run

    nc = _bacc.Bacc("TRN2", target_bir_lowering=False, num_devices=1)
    arrays, args = {}, []
    for name in _INS:
        a = _np.asarray(inputs[name])
        if name == 'L0_ffn_router_w':
            a = a.T
        a = _np.ascontiguousarray(a)
        arrays[f"in_{name}"] = a
        args.append(nc.dram_tensor(f"in_{name}", a.shape, _mybir.dt.from_np(a.dtype), kind="ExternalInput").ap())
    out = nc.dram_tensor("out_0", (B, T, D), _mybir.dt.float32, kind="ExternalOutput").ap()
    layer(nc, *args, out)
    r = _run(nc, [arrays], core_ids=[0])
    return r.results[0]["out_0"]
```

```python
from contextlib import ExitStack

import concourse.bass as bass
from concourse import mybir

ALU = mybir.AluOpType
ACT = mybir.ActivationFunctionType
AX = mybir.AxisListType
F32 = mybir.dt.float32
BF16 = mybir.dt.bfloat16
I32 = mybir.dt.int32

P = 128
B, T, D = 16, 512, 256
H, DH = 16, 16
DC = D // P
BLK = 64
NBLK = T // BLK
ST = 8
NB2 = B // 2
NT = NBLK * NB2
E, K, CAP = 64, 8, 128
F = 192
FH = F // 2
M = 4 * D
MC = M // P
TOK = B * T
XW = D + E
EPS = 1e-5
AHEAD = 2
RT = 4
S2 = DH * DH
ROUTE, EXPERTS, BACK2, BACK2_LATE, BACK1 = range(5)
PHASES = [(ROUTE, 0, 2), (EXPERTS, 2, 2), (BACK2, 4, 2), (BACK2_LATE, 6, 1), (BACK1, 7, 1)]
FST = 2 * 16
WLD = 10 * 16
BUF = 2


def layer(nc, x, Wq, Wk, Wv, Wb, Wg, Wo, bo, ln1_g, ln1_b, ln2_g, ln2_b, w1, b1, w2, b2,
          router_wT, w_gate, w_up, w_down, ws_gate_up, ws_down, out):
    ctx = ExitStack()
    with ctx:
        def sb(name, shape, dt=F32):
            return ctx.enter_context(nc.sbuf_tensor(name, shape, dt))

        def sem(name):
            return ctx.enter_context(nc.semaphore(name))

        qkv_d = nc.dram_tensor("qkv_d", (NBLK, B, 6, P, BLK), F32, kind="Internal").ap()
        gat_d = nc.dram_tensor("gat_d", (NBLK, B, 2, H, BLK), F32, kind="Internal").ap()
        o_d = nc.dram_tensor("o_d", (NBLK, B, 2, P, BLK), F32, kind="Internal").ap()
        xw_d = nc.dram_tensor("xw_d", (TOK + P, XW), F32, kind="Internal").ap()
        acc_d = nc.dram_tensor("acc_d", (TOK + P, D), F32, kind="Internal").ap()
        cum_d = nc.dram_tensor("cum_d", (E, BLK + TOK), F32, kind="Internal").ap()

        ident = sb("ident", [P, P])
        ones = sb("ones", [P, P])
        iot = sb("iot", [P, CAP + 1], I32)
        zeros = sb("zeros", [P, XW])
        slot_row = sb("slot_row", [P, CAP])
        slot_col = sb("slot_col", [P, 1])
        half_pow = sb("half_pow", [P, 2])
        wqkvg = sb("wqkvg", [P, DC, 3 * D + 2 * H])
        wo_s = sb("wo_s", [P, DC, D])
        rw_s = sb("rw_s", [P, DC, E])
        wsgu_s = sb("wsgu_s", [P, DC, 2 * F])
        wsd_s = sb("wsd_s", [FH, 2, D])
        bo_s = sb("bo_s", [1, D])
        b2_s = sb("b2_s", [1, D])
        lncol = sb("lncol", [P, 4, DC])
        bqkv = sb("bqkv", [P, 8])
        b1_in = sb("b1_in", [P, MC])
        b1_s = sb("b1_s", [P, MC])
        mean = sb("mean", [P, NT])
        var = sb("var", [P, NT])
        rstd = sb("rstd", [P, NT])
        nmr = sb("nmr", [P, NT])
        sA = sb("sA", [P, NT])
        bA = sb("bA", [P, NT])
        tmp_st = sb("tmp_st", [P, NT])

        xt = [sb(f"xt{i}", [P, D])[:, :] for i in range(BUF)]
        xa = [sb(f"xa{i}", [P, D])[:, :] for i in range(BUF)]
        xaT = [sb(f"xaT{i}", [P, DC, P])[:, :, :] for i in range(BUF)]
        stg = [sb(f"stg{i}", [P, 2, 6, BLK])[:, :, :, :] for i in range(BUF)]
        gst = [sb(f"gst{i}", [2 * H, P])[:, :] for i in range(BUF)]

        win = [sb(f"win_{n}", [P, BUF, 2, DH, BLK]) for n in "qkv"]
        gwin = sb("gwin", [P, BUF, 2, 2, BLK])
        sq = sb("sq", [P, ST * 2, DH])
        n2 = sb("n2", [P, ST * 2])
        nrm = sb("nrm", [P, ST * 2])
        nrm_e = sb("nrm_e", [P, ST * 2])
        rk = [sb(f"rk{h}", [P, ST * 2]) for h in range(BUF)]
        kn = [sb(f"kn{h}", [P, ST, 2, DH]) for h in range(BUF)]
        bv = [sb(f"bv{h}", [P, ST, 2, DH]) for h in range(BUF)]
        qs = [sb(f"qs{h}", [P, ST, 2, DH]) for h in range(BUF)]
        g8 = [sb(f"g8{h}", [P, ST, 2]) for h in range(BUF)]
        bg = [sb(f"bg{h}", [P, ST, 2]) for h in range(BUF)]
        S = [sb(f"S{h}", [P, ST, 2, S2]) for h in range(BUF)]
        prod = sb("prod", [P, 2, S2])
        outer = sb("outer", [P, 2, S2])
        kS = sb("kS", [P, 2, DH])
        nu = sb("nu", [P, 2, DH])
        HS = ST // 2
        rp = sb("rp", [P, HS * 2 * DH, 16])
        r1 = sb("r1", [P, HS * 2 * DH, 8])
        r2 = sb("r2", [P, HS * 2 * DH, 4])
        r3 = sb("r3", [P, HS * 2 * DH, 2])
        oblk = sb("oblk", [P, 2, DH, BLK])

        gT = sb("gT", [P, DC, P])
        sgu = sb("sgu", [FH, 2 * P])
        hg_s = sb("hg_s", [FH, 2, P])

        REG = 12288
        region = sb("region", [P, REG])
        at = [0]

        def carve(words, restart=False):
            if restart:
                at[0] = 0
            a = region[:, at[0]:at[0] + words]
            at[0] += words
            assert at[0] <= REG
            return a

        xs = [carve(NB2 * D, n == 0).rearrange("p (q d) -> p q d", d=D) for n in range(BUF)]
        wraw = carve(DC * (3 * D + 2 * H)).rearrange("p (c n) -> p c n", c=DC)
        bn6 = carve(NB2 * 6).rearrange("p (q s) -> p q s", s=6)
        mv8 = carve(NB2 * 2).rearrange("p (q s) -> p q s", s=2)
        x4 = [carve(RT * D, i == 0).rearrange("p (r d) -> p r d", r=RT) for i in range(BUF)]
        xw = [carve(RT * XW).rearrange("p (r d) -> p r d", r=RT) for i in range(BUF)]
        acc4 = [carve(RT * D).rearrange("p (r d) -> p r d", r=RT) for i in range(BUF)]
        lg, ex, mk, wt, rep = [carve(RT * E).rearrange("p (r e) -> p r e", r=RT) for _ in range(5)]
        mx = carve(RT * 8).rearrange("p (r e) -> p r e", r=RT)
        negm, wsum, wrec = [carve(RT) for _ in range(3)]
        assert at[0] <= TOK
        at[0] = TOK
        maskT = carve(TOK // 2)[0:E, :].bitcast(BF16)
        cum = carve(TOK, True)[0:E, :]
        cur = region[:, 0:E * BLK].rearrange("p (e j) -> p e j", e=E)
        prv = region[:, E * BLK:2 * E * BLK].rearrange("p (e j) -> p e j", e=E)
        at[0] = 2 * E * BLK
        CW = BLK + 1
        onh = [carve(RT * CAP).rearrange("p (r s) -> p r s", r=RT) for _ in range(2)]
        diff = [carve(RT * CW).rearrange("p (r s) -> p r s", r=RT) for _ in range(2)]
        cnt = [carve(RT * BLK).rearrange("p (r s) -> p r s", r=RT) for _ in range(2)]
        csum = [carve(RT) for _ in range(2)]
        sidx = carve(E)
        sgei = carve(E)
        idx_i = sb("idx_i", [P, E], I32)
        ew_g = [carve(DC * F, r == 0).rearrange("p (c f) -> p c f", c=DC) for r in range(RT)]
        ew_u = [carve(DC * F).rearrange("p (c f) -> p c f", c=DC) for r in range(RT)]
        ew_d = [carve(2 * D)[0:FH, :].rearrange("p (c f) -> p c f", c=2) for r in range(RT)]
        xg = [[carve(XW) for r in range(RT)] for i in range(BUF)]
        yw = [[carve(D) for r in range(RT)] for i in range(BUF)]
        idx4 = [sb(f"idx4{i}", [P, RT], I32)[:, :] for i in range(BUF)]
        w1_s = carve(DC * M, True).rearrange("p (c n) -> p c n", c=DC)
        w2_s = carve(MC * D).rearrange("p (c n) -> p c n", c=MC)
        oT = [[carve(2 * 2 * BLK).rearrange("p (g b t) -> p g b t", b=2, g=2) for _ in range(2)] for _ in range(2)]
        xn_b = [[carve(D) for _ in range(2)] for _ in range(2)]
        ac_b = [[carve(D) for _ in range(2)] for _ in range(2)]
        x1 = [carve(D) for _ in range(2)]
        hb = [carve(D) for _ in range(2)]
        fin = [carve(D) for _ in range(2)]
        hT = [carve(DC * P).rearrange("p (c t) -> p c t", c=DC) for _ in range(2)]
        mid = [carve(MC * P).rearrange("p (c t) -> p c t", c=MC) for _ in range(2)]
        bn_b = carve(2 * 6).rearrange("p (r s) -> p r s", r=2)
        mv_b = carve(2 * 2).rearrange("p (r s) -> p r s", r=2)
        ve_b, sd_b, rs_b, nb_b = [carve(2) for _ in range(4)]

        bank = [ctx.enter_context(nc.psum_tensor(f"bank{i}", [P, 512], F32)) for i in range(8)]
        FT, FQ, FV, TB, LG, G0, G1, YB = bank
        FRONT = (FT, FQ, FV)
        FRONT0 = (FRONT, (TB, G0, G1))

        const_ld = sem("const_ld"); raw_ld = sem("raw_ld"); consts = sem("consts")
        xs_ld = [sem(f"xs_ld{i}") for i in range(BUF)]
        xs_more = [sem(f"xs_more{i}") for i in range(BUF)]
        xs_used = sem("xs_used"); stats_in = sem("stats_in"); stats_done = sem("stats_done")
        pch = sem("pch"); vch = sem("vch"); ach = sem("ach")
        bias_mm = sem("bias_mm"); w_scaled = sem("w_scaled"); bias_done = sem("bias_done")
        xt_ld = [sem(f"xt_ld{i}") for i in range(BUF)]; xa_ready = sem("xa_ready"); fT_done = sem("fT_done")
        xaT_ready = sem("xaT_ready"); qkv_done = sem("qkv_done"); stg_ready = sem("stg_ready")
        f_stored = [sem(f"f_stored{i}") for i in range(BUF)]
        win_ld = sem("win_ld"); sq_ready = sem("sq_ready"); n2_ready = sem("n2_ready")
        nrm_ready = sem("nrm_ready"); rk_ready = sem("rk_ready")
        act_staged = sem("act_staged"); pool_staged = sem("pool_staged")
        rec_done = sem("rec_done"); prod_done = sem("prod_done"); o_stored = sem("o_stored")
        x4_ld = [sem(f"x4_ld{i}") for i in range(BUF)]; xn_ready = sem("xn_ready"); t_done = sem("t_done")
        gT_ready = sem("gT_ready"); gu_done = sem("gu_done"); sg_ready = sem("sg_ready")
        h_ready = sem("h_ready"); y_done = sem("y_done"); acc_ready = sem("acc_ready")
        lg_done = sem("lg_done"); lg_copied = sem("lg_copied"); negm_ready = sem("negm_ready")
        e_ready = sem("e_ready"); mask_ready = sem("mask_ready"); w_ready = sem("w_ready")
        mt_done = sem("mt_done"); mT_ready = sem("mT_ready"); r_stored = [sem(f"r_stored{i}") for i in range(BUF)]
        zero_st = sem("zero_st")
        cum_ready = sem("cum_ready"); cum_st = sem("cum_st"); cur_ld = sem("cur_ld")
        onh_ready = sem("onh_ready"); slot_mm = sem("slot_mm"); slot_used = sem("slot_used")
        slots_ready = sem("slots_ready")
        ew_ld = [sem(f"ew_ld{r}") for r in range(RT)]
        g_ld = [[sem(f"g_ld{i}{r}") for r in range(RT)] for i in range(BUF)]
        yw_ready = sem("yw_ready"); sc_done = sem("sc_done")
        mlp_ld = sem("mlp_ld"); mlp_bias = sem("mlp_bias"); mlp_w = sem("mlp_w")
        bk_ld = [[sem(f"bk_ld{i}{r}") for r in range(2)] for i in range(BUF)]
        at_done = sem("at_done"); x1_ready = sem("x1_ready"); ve_ready = sem("ve_ready")
        sd_ready = sem("sd_ready"); nb_ready = sem("nb_ready"); hb_ready = sem("hb_ready")
        hT_done = sem("hT_done"); hT_ready = sem("hT_ready"); mid_done = sem("mid_done")
        gelu_done = sem("gelu_done"); out_done = sem("out_done"); fin_ready = sem("fin_ready")
        fin_st = [sem(f"fin_st{i}") for i in range(2)]

        passed = sem("passed")

        x_t = x.rearrange("(q b) (k t) d -> k q b t d", b=2, t=BLK)
        out_t = out.rearrange("(q b) (k t) d -> k q b t d", b=2, t=BLK)
        x_r = x.rearrange("(q b) (m r t) d -> m q b t r d", b=2, t=BLK, r=RT)
        xw_r = xw_d[0:TOK, :].rearrange("(q b m r t) d -> m q b t r d", q=NB2, b=2, m=T // (RT * BLK), t=BLK)
        acc_r = acc_d[0:TOK, :].rearrange("(q b m r t) d -> m q b t r d", q=NB2, b=2, m=T // (RT * BLK), t=BLK)
        xw_t = xw_d[0:TOK, :].rearrange("(q b k t) d -> k q b t d", q=NB2, b=2, t=BLK)
        acc_t = acc_d[0:TOK, :].rearrange("(q b k t) d -> k q b t d", q=NB2, b=2, t=BLK)
        qkv_st = qkv_d.rearrange("k (q b) i p t -> k q p (b i) t", b=2)
        gat_st = gat_d.rearrange("k (q b) w h t -> k q (w h) b t", b=2)
        qkv_ld = qkv_d.rearrange("k (s b) (m g) (h d) t -> k m s b (g h) (d t)", s=2, m=3, h=P // DH)
        gat_ld = gat_d.rearrange("k (s b) w h t -> k s w b h t", s=2)
        o_st = o_d.rearrange("k (s b) g (h v) t -> k (b g h) s (v t)", s=2, h=P // DH)
        o_ld = o_d.rearrange("k (q b) g p t -> k q g p b t", b=2)
        maskT_v = maskT.rearrange("e (q b m r t) -> e q m r b t", q=NB2, b=2, r=RT, t=BLK)

        def iteration(kb0, kb, jj, h):
            return (kb + kb0) * NB2 + jj * 2 + h

        def lookup(L):
            return (L >> 3) & 1, (L & 7) * ST

        UNITS_R = NT

        block = ctx.enter_context(nc.Block())

        def load_xs(queue, k, s, ld):
            for b in range(2):
                queue.dma_start(xs[s][BLK * b:BLK * (b + 1), :, :],
                                x_t[k].rearrange("q b t d -> b t q d")[b]).then_inc(ld[s], 16)

        @block.sync
        def _(sp):
            for s in range(2):
                load_xs(sp, s, s, xs_ld)
            for m, w in enumerate((Wq, Wk, Wv)):
                sp.dma_start(wraw[:, :, m * D:(m + 1) * D], w.rearrange("(c p) n -> p c n", p=P)).then_inc(raw_ld, 16)
            for m, w in enumerate((Wb, Wg)):
                sp.dma_start(wraw[:, :, 3 * D + m * H:3 * D + (m + 1) * H],
                             w.rearrange("(c p) n -> p c n", p=P)).then_inc(raw_ld, 16)
            for m, w in enumerate((ln1_g, ln1_b, ln2_g, ln2_b)):
                sp.dma_start(lncol[:, m, :], w.rearrange("(c p) -> p c", p=P), allow_slow_non_contiguous=True).then_inc(raw_ld, 16)

            def front_load(f, k, q, i):
                sp.dma_start(xt[i], x_t[k, q]).then_inc(xt_ld[i], 16)

            for i in range(2):
                front_load(i, 0, i, i)
            sp.dma_start(wo_s[:, :, :], Wo.rearrange("(c p) n -> p c n", p=P)).then_inc(const_ld, 16)
            sp.dma_start(rw_s[:, :, :], router_wT.rearrange("(c p) n -> p c n", p=P)).then_inc(const_ld, 16)
            sp.dma_start(wsgu_s[:, :, :], ws_gate_up.rearrange("(c p) n -> p c n", p=P)).then_inc(const_ld, 16)
            sp.dma_start(wsd_s[:, :, :], ws_down.rearrange("(c p) n -> p c n", p=FH)).then_inc(const_ld, 16)
            sp.dma_start(bo_s[:, :], bo.rearrange("(a n) -> a n", a=1)).then_inc(const_ld, 16)
            sp.dma_start(b2_s[:, :], b2.rearrange("(a n) -> a n", a=1)).then_inc(const_ld, 16)
            sp.dma_start(b1_in[:, :], b1.rearrange("(c p) -> p c", p=P), allow_slow_non_contiguous=True).then_inc(const_ld, 16)
            sp.wait_ge(consts, 5)
            sp.dma_start(xw_d[TOK:TOK + P, :], zeros[:, :]).then_inc(zero_st, 16)
            sp.dma_start(acc_d[TOK:TOK + P, :], zeros[:, 0:D]).then_inc(zero_st, 16)

            def front_store(f, k, q, i):
                sp.wait_ge(stg_ready, f + 1)
                sp.dma_start(qkv_st[k, q], stg[i].rearrange("p b i t -> p (b i) t")).then_inc(f_stored[i], 16)
                sp.dma_start(gat_st[k, q], gst[i].rearrange("p (b t) -> p b t", b=2)).then_inc(f_stored[i], 16)

            def load_window(k, par, jobs):
                for i in range(BUF):
                    sp.wait_ge(f_stored[i], jobs * (FST // 2))
                sp.sem_inc(passed, 1)
                for m in range(3):
                    for s in range(2):
                        sp.dma_start(win[m][:, par, s].rearrange("p d t -> p (d t)"), qkv_ld[k, m, s]).then_inc(win_ld, 16)
                for s in range(2):
                    for w in range(2):
                        sp.dma_start(gwin[:, par, s, w], gat_ld[k, s, w]).then_inc(win_ld, 16)

            def front_next(f, h):
                sp.wait_ge(xa_ready, f + 1)
                g_ = (f + 2) % NT
                front_load(f + 2, g_ // NB2, g_ % NB2, h)

            front_next(0, 0)
            with sp.Fori(0, AHEAD * NB2 // 2 - 1) as i:
                for h in range(2):
                    f = i * 2 + h
                    front_next(f + 1, 1 - h)
                    front_store(f, f // NB2, f % NB2, h)
            f = AHEAD * NB2 - 1
            front_next(f, 1)
            front_store(f - 1, AHEAD - 1, NB2 - 2, 0)
            front_store(f, AHEAD - 1, NB2 - 1, 1)
            load_window(0, 0, NB2)

            def route_load(I, k, q, h):
                for b in range(2):
                    sp.dma_start(x4[h][BLK * b:BLK * (b + 1), :, :], x_r[k, q, b]).then_inc(x4_ld[h], 16)

            def route_store(I, k, q, h):
                sp.wait_ge(w_ready, I + 1)
                sp.sem_inc(passed, 1)
                sp.wait_ge(acc_ready, (I + 1) * RT)
                for b in range(2):
                    sp.dma_start(xw_r[k, q, b], xw[h][BLK * b:BLK * (b + 1), :, :]).then_inc(r_stored[h], 16)
                    sp.dma_start(acc_r[k, q, b], acc4[h][BLK * b:BLK * (b + 1), :, :]).then_inc(r_stored[h], 16)

            def experts(n):
                for r in range(RT):
                    e = n * RT + r
                    sp.wait_ge(y_done, e + (UNITS_R - RT + 1))
                    sp.dma_start(ew_g[r], w_gate[e].rearrange("(c p) f -> p c f", p=P)).then_inc(ew_ld[r], 16)
                    sp.dma_start(ew_u[r], w_up[e].rearrange("(c p) f -> p c f", p=P)).then_inc(ew_ld[r], 16)
                    sp.dma_start(ew_d[r], w_down[e].rearrange("(c p) f -> p c f", p=FH)).then_inc(ew_ld[r], 16)

            def back_load(h, r, k, q):
                for g in range(2):
                    sp.dma_start(oT[h][r][:, g], o_ld[k, q, g]).then_inc(bk_ld[h][r], 16)
                sp.dma_start(xn_b[h][r], xw_t[k, q, :, :, 0:D]).then_inc(bk_ld[h][r], 16)
                sp.dma_start(ac_b[h][r], acc_t[k, q]).then_inc(bk_ld[h][r], 16)

            def back_store(c, r, k, q):
                sp.wait_ge(fin_ready, c + 1)
                sp.dma_start(out_t[k, q], fin[r]).then_inc(fin_st[r], 16)

            for phase, kb0, nb in PHASES:
                if phase == EXPERTS:
                    sp.wait_ge(cum_ready, 1)
                    sp.dma_start(cum_d[:, BLK:BLK + TOK], cum).then_inc(cum_st, 16)
                    sp.dma_start(cum_d[:, 0:BLK], zeros[0:E, 0:BLK]).then_inc(cum_st, 16)
                    sp.wait_ge(cum_st, 32)
                    cum_b = cum_d.rearrange("e (k j) -> k e j", j=BLK)
                    sp.dma_start(cur, cum_b[1:P + 1]).then_inc(cur_ld, 16)
                    sp.dma_start(prv, cum_b[0:P]).then_inc(cur_ld, 16)
                    sp.wait_ge(slots_ready, 1)
                if phase == ROUTE:
                    sp.wait_ge(stats_in, 2)
                    route_load(0, 0, 0, 0)
                if phase == BACK2:
                    sp.wait_ge(sc_done, 16 * E)
                    for r in range(RT):
                        sp.wait_ge(g_ld[0][r], 16 * (E // RT // 2 + 1))
                    sp.wait_ge(o_stored, 16)
                    sp.dma_start(w1_s, w1.rearrange("(c p) n -> p c n", p=P)).then_inc(mlp_ld, 16)
                    sp.dma_start(w2_s, w2.rearrange("(c p) n -> p c n", p=P)).then_inc(mlp_ld, 16)
                    for r in range(2):
                        back_load(0, r, 0, r)
                if phase == BACK1:
                    sp.wait_ge(o_stored, 7 * 16)
                    sp.wait_ge(fin_ready, 6 * NB2)
                    for r in range(2):
                        sp.wait_ge(bk_ld[0][r], 64 * 13)
                    back_load(0, 0, 6, 0)
                with sp.Fori(0, nb) as kb:
                    if phase != BACK1:
                        sp.wait_ge(act_staged, (kb + kb0) * NB2)
                        sp.wait_ge(pool_staged, (kb + kb0) * NB2)
                        sp.wait_ge(win_ld, (kb + (kb0 + 1)) * WLD)
                        load_window(kb + (kb0 + 1), (kb + (kb0 + 1)) & 1, (kb + (kb0 + 2)) * NB2)
                    with sp.Fori(0, NB2 // 2) as jj:
                        for h in range(2):
                            I = iteration(kb0, kb, jj, h)
                            j = jj * 2 + h
                            f = I + AHEAD * NB2
                            if phase in (ROUTE, EXPERTS, BACK2):
                                front_next(f, h)
                            if phase == ROUTE:
                                sp.wait_ge(acc_ready, I * RT)
                                n_ = (I + 1) % (2 * NB2)
                                route_load(I + 1, n_ // NB2, n_ % NB2, 1 - h)
                                front_store(f, f // NB2, f % NB2, h)
                                route_store(I, kb, j, h)
                            if phase == EXPERTS:
                                experts(kb * NB2 + j)
                                front_store(f, f // NB2, f % NB2, h)
                            if phase in (BACK2, BACK2_LATE):
                                n = (kb + (kb0 - 4)) * NB2 + j
                                n_ = (n + 1) % (3 * NB2)
                                sp.wait_ge(o_stored, (n_ // 4 + 1) * 16)
                                sp.sem_inc(passed, 1)
                                sp.wait_ge(fin_ready, n * 2)
                                for r in range(2):
                                    back_load(1 - h, r, n_ // 4, (n_ % 4) * 2 + r)
                                if phase == BACK2:
                                    front_store(f, f // NB2, f % NB2, h)
                                for r in range(2):
                                    back_store(n * 2 + r, r, n // 4, (n % 4) * 2 + r)
                            if phase == BACK1:
                                sp.wait_ge(fin_ready, j + 6 * NB2)
                                back_load(0, 1 - h, 6, (j + 1) % NB2)
                                back_store(j + 6 * NB2, h, 6, j)
            sp.wait_ge(o_stored, 16 * NBLK)
            for i in range(NB2 // 2 + 1):
                if i < NB2 // 2:
                    sp.wait_ge(fin_ready, 7 * NB2 + max(i - 1, 0) * 2)
                    if i == 1:
                        sp.wait_ge(bk_ld[0][0], 64 * (12 + 1 + 5))
                    for r in range(2):
                        back_load((i + 1) % 2, r, 7, i * 2 + r)
                if i:
                    for r in range(2):
                        back_store((i - 1) * 2 + r + 7 * NB2, r, 7, (i - 1) * 2 + r)
            for r in range(2):
                sp.wait_ge(fin_st[r], 16 * NT // 2)
                sp.wait_ge(r_stored[r], 64 * NB2)
            sp.wait_ge(zero_st, 32)
            for i in range(BUF):
                sp.wait_ge(f_stored[i], FST // 2 * NT)
                sp.wait_ge(xt_ld[i], 16 * (NT // 2 + 1))

        @block.gpsimd
        def _(pool):
            count = [0]

            def link(ins):
                count[0] += 1
                ins.then_inc(pch, 1)
                pool.wait_ge(pch, count[0])

            def relink():
                pool.wait_ge(pch, count[0])
                pool.sem_clear(pch)
                count[0] = 0

            g = nc.gpsimd
            link(g.memset(ident[:, :], 0.0))
            g.memset(ones[:, :], 1.0).then_inc(consts, 1)
            g.memset(zeros[:, :], 0.0).then_inc(consts, 1)
            g.memset(half_pow[:, 0:1], -0.5)
            link(g.memset(half_pow[:, 1:2], 0.5))
            link(g.iota(iot[:, 0:CAP], [[1, CAP]], base=0, channel_multiplier=0))
            link(g.iota(iot[:, CAP:CAP + 1], [[0, 1]], base=0, channel_multiplier=1))
            g.tensor_copy(slot_row[:, :], iot[:, 0:CAP]).then_inc(consts, 1)
            g.tensor_copy(slot_col[:, :], iot[:, CAP:CAP + 1]).then_inc(consts, 1)
            g.affine_select(out=ident[:, :], in_=ident[:, :], compare_op=ALU.not_equal, fill=1.0,
                            base=0, pattern=[[-1, P]], channel_multiplier=1).then_inc(consts, 1)
            pool.sem_inc(prod_done, 2)

            def power(o, a, which, n):
                return g.tensor_tensor(o, a, half_pow[:, which:which + 1].to_broadcast([P, n]), ALU.pow)

            def factors(part, lo, hi):
                n = hi - lo
                pool.wait_ge(stats_in, part + 1)
                link(g.tensor_scalar(tmp_st[:, lo:hi], var[:, lo:hi], EPS, None, ALU.add))
                link(power(rstd[:, lo:hi], tmp_st[:, lo:hi], 0, n))
                link(g.tensor_tensor(tmp_st[:, lo:hi], var[:, lo:hi], rstd[:, lo:hi], ALU.mult))
                link(g.tensor_tensor(tmp_st[:, lo:hi], tmp_st[:, lo:hi], rstd[:, lo:hi], ALU.mult))
                link(g.tensor_scalar(tmp_st[:, lo:hi], tmp_st[:, lo:hi], EPS, None, ALU.add))
                link(power(sA[:, lo:hi], tmp_st[:, lo:hi], 0, n))
                link(g.tensor_tensor(sA[:, lo:hi], sA[:, lo:hi], rstd[:, lo:hi], ALU.mult))
                link(g.tensor_scalar(tmp_st[:, lo:hi], mean[:, lo:hi], -1.0, None, ALU.mult))
                g.tensor_tensor(bA[:, lo:hi], tmp_st[:, lo:hi], sA[:, lo:hi], ALU.mult).then_inc(stats_done, 1)
                g.tensor_tensor(nmr[:, lo:hi], tmp_st[:, lo:hi], rstd[:, lo:hi], ALU.mult).then_inc(stats_done, 1)

            def more_xs(i):
                for s in range(2):
                    pool.wait_ge(xs_used, i * 2 + (s - 1))
                    load_xs(pool, i * 2 + s, s, xs_more)

            more_xs(1)
            factors(0, 0, AHEAD * NB2)
            with pool.Fori(2, NBLK // 2) as i:
                more_xs(i)
            factors(1, AHEAD * NB2, NT)
            relink()

            def stage_values(L, h):
                par, t0 = lookup(L)
                pool.wait_ge(win_ld, ((L >> 3) + 1) * WLD)
                pool.wait_ge(rec_done, L * 2)
                beta = gwin[:, par, :, 0, bass.ds(t0, ST)].rearrange("p s t -> p t s")
                gg = gwin[:, par, :, 1, bass.ds(t0, ST)].rearrange("p s t -> p t s")
                g.tensor_tensor(bg[h][:, :, :], beta, gg, ALU.mult)
                for s in range(2):
                    g.tensor_tensor(bv[h][:, :, s, :],
                                    win[2][:, par, s, :, bass.ds(t0, ST)].rearrange("p d t -> p t d"),
                                    gwin[:, par, s, 0, bass.ds(t0, ST)].unsqueeze(2).to_broadcast([P, ST, DH]),
                                    ALU.mult)

            def stage_norm(L):
                pool.wait_ge(n2_ready, L + 1)
                power(nrm[:, :], n2[:, :], 1, ST * 2).then_inc(nrm_ready, 1)

            def stage_keys(L, h):
                par, t0 = lookup(L)
                pool.wait_ge(rk_ready, L + 1)
                rk_ = rk[h][:, :].rearrange("p (t s) -> p t s", s=2)
                for s in range(2):
                    last = g.tensor_tensor(
                        kn[h][:, :, s, :],
                        win[1][:, par, s, :, bass.ds(t0, ST)].rearrange("p d t -> p t d"),
                        rk_[:, :, s].unsqueeze(2).to_broadcast([P, ST, DH]),
                        ALU.mult)
                last.then_inc(pool_staged, 1)

            def reads(I, h, half, j, mid_work=None):
                lo = half * HS
                pool.wait_ge(rec_done, I * 2 + (3 + half))
                if half == 0:
                    pool.wait_ge(o_stored, (I >> 3) * 16)
                pool.wait_ge(act_staged, I + 1)
                g.tensor_tensor(
                    rp[:, :, :].rearrange("p (a v) d -> p a v d", v=DH),
                    S[h][:, lo:lo + HS].rearrange("p t s (v d) -> p (t s) v d", v=DH),
                    qs[h][:, lo:lo + HS].rearrange("p t s d -> p (t s) d").unsqueeze(2).to_broadcast([P, HS * 2, DH, DH]),
                    ALU.mult).then_inc(prod_done, 1)
                if mid_work is not None:
                    mid_work()
                pool.wait_ge(prod_done, I * 2 + (3 + half))
                link(g.tensor_tensor(r1[:, :, :], rp[:, :, 0:8], rp[:, :, 8:16], ALU.add))
                link(g.tensor_tensor(r2[:, :, :], r1[:, :, 0:4], r1[:, :, 4:8], ALU.add))
                link(g.tensor_tensor(r3[:, :, :], r2[:, :, 0:2], r2[:, :, 2:4], ALU.add))
                a = r3[:, :, :].rearrange("p (t s v) c -> p s v t c", t=HS, s=2)
                for s in range(2):
                    link(g.tensor_tensor(oblk[:, s, :, bass.ds(j * ST + lo, HS)], a[:, s, :, :, 0], a[:, s, :, :, 1], ALU.add))

            def gather(n, before, h):
                if before is not None:
                    pool.wait_ge(sc_done, before * 16)
                    pool.wait_ge(yw_ready, before)
                link(g.tensor_copy(idx4[h], idx_i[:, bass.ds(n * RT, RT)]))
                for r in range(RT):
                    g.indirect_dma_start(xg[h][r], None, xw_d[:, :],
                                         bass.IndirectOffsetOnAxis(ap=idx4[h][:, r:r + 1], axis=0)).then_inc(g_ld[h][r], 16)

            def scatter(e, r, h):
                pool.wait_ge(yw_ready, e + 1)
                pool.wait_ge(sc_done, e * 16)
                pool.sem_inc(passed, 1)
                g.indirect_dma_start(acc_d[:, :], bass.IndirectOffsetOnAxis(ap=idx4[h][:, r:r + 1], axis=0),
                                     yw[h][r], None, compute_op=ALU.add).then_inc(sc_done, 16)

            stage_values(0, 0)
            stage_norm(0)
            stage_keys(0, 0)
            stage_norm(1)
            for phase, kb0, nb in PHASES:
                if phase == EXPERTS:
                    pool.wait_ge(slots_ready, 1)
                    for i in range(BUF):
                        pool.wait_ge(r_stored[i], 64 * NB2)
                    pool.wait_ge(zero_st, 32)
                    gather(0, None, 0)
                    relink()

                def body(kb, jj, h, last=False, last2=False):
                    I = iteration(kb0, kb, jj, h)
                    j = jj * 2 + h
                    n = kb * NB2 + j
                    if not last:
                        stage_values(I + 1, 1 - h)
                        stage_keys(I + 1, 1 - h)
                    if not last2:
                        stage_norm(I + 2)
                    if phase == EXPERTS:
                        reads(I, h, 0, j, lambda: scatter(n * RT, 0, h))
                        scatter(n * RT + 1, 1, h)
                        gather((n + 1) % (E // RT), n * RT, 1 - h)
                    else:
                        reads(I, h, 0, j)
                    if phase == EXPERTS:
                        reads(I, h, 1, j, lambda: scatter(n * RT + 2, 2, h))
                        scatter(n * RT + 3, 3, h)
                    else:
                        reads(I, h, 1, j)

                with pool.Fori(0, nb) as kb:
                    if phase != BACK1:
                        with pool.Fori(0, NB2 // 2) as jj:
                            body(kb, jj, 0)
                            body(kb, jj, 1)
                            relink()
                    else:
                        with pool.Fori(0, NB2 // 2 - 1) as jj:
                            body(kb, jj, 0)
                            body(kb, jj, 1)
                            relink()
                        body(kb, NB2 // 2 - 1, 0, last2=True)
                        body(kb, NB2 // 2 - 1, 1, last=True, last2=True)
                        relink()
                    g.dma_start(o_st[kb + kb0], oblk[:, :, :, :].rearrange("p s v t -> p s (v t)")).then_inc(o_stored, 16)
            pool.wait_ge(o_stored, 16 * NBLK)

        @block.vector
        def _(dve):
            v = nc.vector
            count = [0]

            def mark(ins):
                count[0] += 1
                ins.then_inc(vch, 1)
                return count[0]

            def link(ins):
                dve.wait_ge(vch, mark(ins))

            def relink():
                dve.wait_ge(vch, count[0])
                dve.sem_clear(vch)
                count[0] = 0

            def statistics(i, ld, n):
                for s in range(2):
                    dve.wait_ge(ld[s], n)
                    for q in range(NB2):
                        m = mark(v.bn_stats(bn6[:, q, :], xs[s][:, q, :]))
                    dve.wait_ge(vch, m)
                    for q in range(NB2):
                        m = mark(v.bn_aggr(mv8[:, q, :], bn6[:, q, :]))
                    dve.wait_ge(vch, m)
                    v.tensor_copy(mean[:, bass.ds((i * 2 + s) * NB2, NB2)], mv8[:, :, 0])
                    v.tensor_copy(var[:, bass.ds((i * 2 + s) * NB2, NB2)], mv8[:, :, 1]).then_inc(xs_used, 1)
                    dve.wait_ge(xs_used, i * 2 + (s + 1))
                    dve.sem_inc(passed, 1)
                relink()

            statistics(0, xs_ld, 32)
            dve.sem_inc(stats_in, 1)
            with dve.Fori(1, NBLK // 2) as i:
                statistics(i, xs_more, i * 32)
            dve.sem_inc(stats_in, 1)
            dve.sem_inc(h_ready, 1)
            link(v.memset(S[1][:, ST - 1], 0.0))
            dve.sem_inc(rec_done, 2)
            relink()

            def norms(L, h, part):
                if part == 0:
                    dve.wait_ge(sq_ready, L + 1)
                    v.tensor_reduce(n2[:, :], sq[:, :, :], AX.X, ALU.add).then_inc(n2_ready, 1)
                else:
                    dve.wait_ge(nrm_ready, L + 1)
                    link(v.tensor_scalar(nrm_e[:, :], nrm[:, :], 1e-6, None, ALU.add))
                    v.reciprocal(rk[h][:, :], nrm_e[:, :]).then_inc(rk_ready, 1)

            def unit_product(q):
                dve.wait_ge(sg_ready, q + 1)
                dve.wait_ge(y_done, q)
                b = GUB[0]
                v.tensor_tensor(hg_s[:, :, :].rearrange("p a t -> p (a t)"), sgu[:, :], b[0:FH, 2 * P:4 * P],
                                ALU.mult).then_inc(h_ready, 1)

            GUB = [None]

            def product(q, r):
                GUB[0] = (G0, G1)[r % 2]
                unit_product(q)

            def route_sum(q, r, h):
                dve.wait_ge(y_done, q + 1)
                v.tensor_tensor(acc4[h][:, r, :], YB[:, 0:D], x4[h][:, r, :], ALU.add).then_inc(acc_ready, 1)

            def top8(I):
                dve.wait_ge(lg_copied, I + 1)
                dve.sem_inc(passed, 1)
                for r in range(RT):
                    m = mark(v.max(mx[:, r, :], lg[:, r, :]))
                dve.wait_ge(vch, m)
                v.tensor_scalar(negm, mx[:, :, 0], -1.0, None, ALU.mult).then_inc(negm_ready, 1)
                for r in range(RT):
                    m = mark(v.match_replace(rep[:, r, :], mx[:, r, :], lg[:, r, :], -3.0e38))
                dve.wait_ge(vch, m)
                v.tensor_tensor(mk, rep, lg, ALU.not_equal).then_inc(mask_ready, 1)

            def top8_weights(I, h):
                dve.wait_ge(mask_ready, I + 1)
                dve.wait_ge(e_ready, I + 1)
                link(v.tensor_tensor(wt, ex, mk, ALU.mult))
                link(v.tensor_reduce(wsum, wt, AX.X, ALU.add))
                link(v.reciprocal(wrec, wsum))
                v.tensor_tensor(xw[h][:, :, D:XW], wt, wrec.unsqueeze(2).to_broadcast([P, RT, E]),
                                ALU.mult).then_inc(w_ready, 1)

            def back_x1(c, r, half):
                dve.wait_ge(at_done, c + 1)
                bk = (TB, LG)[r]
                m = mark(v.tensor_tensor(x1[r], bk[:, 0:D], xn_b[half][r], ALU.add))
                dve.wait_ge(vch, m)
                m = mark(v.bn_stats(bn_b[:, r, :], x1[r]))
                dve.wait_ge(vch, m)
                link(v.bn_aggr(mv_b[:, r, :], bn_b[:, r, :]))
                v.tensor_scalar(ve_b[:, r:r + 1], mv_b[:, r, 1:2], EPS, None, ALU.add).then_inc(ve_ready, 1)

            def back_rstd(c, r):
                dve.wait_ge(sd_ready, c + 1)
                link(v.reciprocal(rs_b[:, r:r + 1], sd_b[:, r:r + 1]))
                v.scalar_tensor_tensor(nb_b[:, r:r + 1], mv_b[:, r, 0:1], -1.0, rs_b[:, r:r + 1],
                                       ALU.mult, ALU.mult).then_inc(nb_ready, 1)

            def back_sum(c, r, ob, half, use):
                dve.wait_ge(fin_st[r], use * 16)
                dve.wait_ge(out_done, c + 1)
                link(v.tensor_tensor(fin[r], ob[:, 0:D], x1[r], ALU.add))
                v.tensor_tensor(fin[r], fin[r], ac_b[half][r], ALU.add).then_inc(fin_ready, 1)

            OUTB = (YB, LG)

            def step(I, h, s, ready):
                before = S[h][:, s - 1] if s else S[1 - h][:, ST - 1]
                key = [kn[h][:, s, G, :].unsqueeze(1).to_broadcast([P, DH, DH]) for G in range(2)]
                m = [0, 0]
                for G in range(2):
                    if ready[G] is not None:
                        dve.wait_ge(*ready[G])
                    m[G] = mark(v.tensor_tensor(prod[:, G].rearrange("p (v d) -> p v d", v=DH),
                                                before[:, G].rearrange("p (v d) -> p v d", v=DH), key[G], ALU.mult))
                for G in range(2):
                    dve.wait_ge(vch, m[G])
                    m[G] = mark(v.tensor_reduce(kS[:, G], prod[:, G].rearrange("p (v d) -> p v d", v=DH), AX.X, ALU.add))
                for G in range(2):
                    dve.wait_ge(vch, m[G])
                    m[G] = mark(v.scalar_tensor_tensor(nu[:, G], kS[:, G], bg[h][:, s, G:G + 1], bv[h][:, s, G, :],
                                                       ALU.mult, ALU.subtract))
                for G in range(2):
                    dve.wait_ge(vch, m[G])
                    m[G] = mark(v.tensor_tensor(outer[:, G].rearrange("p (v d) -> p v d", v=DH),
                                                nu[:, G].unsqueeze(2).to_broadcast([P, DH, DH]), key[G], ALU.mult))
                for G in range(2):
                    dve.wait_ge(vch, m[G])
                    ins = v.scalar_tensor_tensor(S[h][:, s, G], before[:, G], g8[h][:, s, G:G + 1], outer[:, G],
                                                 ALU.mult, ALU.subtract)
                    if G == 1 and s in (HS - 1, ST - 1):
                        ins.then_inc(rec_done, 1)
                        ready[G] = (rec_done, I * 2 + (3 if s == HS - 1 else 4))
                    else:
                        ready[G] = (vch, mark(ins))

            def slots():
                dve.wait_ge(mT_ready, 2 * NB2)
                for i in range(BUF):
                    dve.wait_ge(r_stored[i], 64 * NB2)
                dve.wait_ge(x4_ld[0], 32 * (NB2 + 1))
                v.tensor_tensor_scan(cum, ones[0:E, 0:1].to_broadcast([E, TOK]), maskT, 0.0,
                                     ALU.mult, ALU.add).then_inc(cum_ready, 1)
                dve.wait_ge(cum_ready, 1)
                for a in range(2):
                    link(v.memset(diff[a][:, :, BLK:CW], float(BLK)))
                dve.wait_ge(cur_ld, 32)
                relink()
                with dve.Fori(0, E // RT // 2) as i:
                    for a in range(2):
                        e0 = (i * 2 + a) * RT
                        dve.wait_ge(slot_mm, i * 2)
                        for r in range(RT):
                            v.tensor_scalar(onh[a][:, r, :], slot_row[:, :], prv[:, e0 + r, BLK - 1:BLK],
                                            None, ALU.is_ge)
                        v.tensor_tensor(diff[a][:, :, 0:BLK], cur[:, bass.ds(e0, RT), :], prv[:, bass.ds(e0, RT), :],
                                        ALU.subtract).then_inc(onh_ready, 1)
                    for a in range(2):
                        e0 = (i * 2 + a) * RT
                        dve.wait_ge(slot_mm, i * 2 + (a + 1))
                        ps = (LG, TB)[a][:, 0:RT * CW].rearrange("p (r j) -> p r j", r=RT)
                        link(v.tensor_scalar(cnt[a], ps[:, :, 0:BLK], slot_col[:, 0:1], None, ALU.is_le))
                        link(v.tensor_reduce(csum[a], cnt[a], AX.X, ALU.add))
                        v.scalar_tensor_tensor(sidx[:, bass.ds(e0, RT)], csum[a], -float(BLK), ps[:, :, BLK],
                                               ALU.add, ALU.add).then_inc(slot_used, 1)
                    relink()
                dve.wait_ge(slot_used, E // RT)
                link(v.tensor_scalar(sgei, sidx, float(TOK), None, ALU.is_ge))
                link(v.scalar_tensor_tensor(sidx, sgei, slot_col[:, 0:1], sidx, ALU.mult, ALU.add))
                v.tensor_copy(idx_i[:, :], sidx).then_inc(slots_ready, 1)
                relink()

            for L in range(2):
                norms(L, L, 0)
                norms(L, L, 1)
            relink()
            for phase, kb0, nb in PHASES:
                if phase == EXPERTS:
                    slots()
                if phase == BACK2:
                    dve.wait_ge(mlp_bias, 1)
                    v.tensor_tensor(b1_s[:, :], TB[:, 0:MC], b1_in[:, :], ALU.add).then_inc(mlp_bias, 1)

                def body(kb, jj, h, ready, last2=False):
                    I = iteration(kb0, kb, jj, h)
                    j = jj * 2 + h
                    n = kb * NB2 + j
                    dve.wait_ge(pool_staged, I + 1)
                    dve.wait_ge(act_staged, I + 1)
                    dve.wait_ge(prod_done, I * 2)
                    ready[1] = (rec_done, I * 2 + 2)
                    if phase in (BACK2, BACK2_LATE):
                        m = n + (0 if phase == BACK2 else 2 * NB2)
                        c, rs, half, use = m * 2, (0, 1), h, m
                    elif phase == BACK1:
                        c, rs, half, use = j + (6 * NB2 - h), (h,), 0, jj + 24
                    for s in range(ST):
                        step(I, h, s, ready)
                        if s == 1 and not last2:
                            norms(I + 2, h, 0)
                        if s == 6 and not last2:
                            norms(I + 2, h, 1)
                        if phase in (ROUTE, EXPERTS):
                            q = n * RT + (0 if phase == ROUTE else UNITS_R)
                            r = {2: 0, 4: 1, 5: 2, 6: 3}.get(s)
                            if r is not None:
                                product(q + r, r)
                            r = {4: 0, 5: 1, 6: 2, 7: 3}.get(s)
                            if phase == ROUTE and r is not None:
                                route_sum(q + r, r, h)
                            if phase == ROUTE and s == 7:
                                top8(I)
                                top8_weights(I, h)
                        else:
                            if s == 0:
                                for r in rs:
                                    back_x1(c + r, r, half)
                            if s == 1:
                                for r in rs:
                                    back_rstd(c + r, r)
                            if s == 6 and len(rs) == 2:
                                back_sum(c, 0, OUTB[0], half, use)
                            if s == 7:
                                back_sum(c + rs[-1], rs[-1], OUTB[rs[-1]], half, use)

                def pair(kb, jj, last=False):
                    ready = [None, None]
                    body(kb, jj, 0, ready, last)
                    body(kb, jj, 1, ready, last)
                    relink()

                with dve.Fori(0, nb) as kb:
                    if phase != BACK1:
                        with dve.Fori(0, NB2 // 2) as jj:
                            pair(kb, jj)
                    else:
                        with dve.Fori(0, NB2 // 2 - 1) as jj:
                            pair(kb, jj)
                        pair(kb, NB2 // 2 - 1, last=True)
            with dve.Fori(0, NB2 // 4) as jj:
                for m in range(2):
                    c = (jj * 2 + m) * 2 + 7 * NB2
                    for r in range(2):
                        back_x1(c + r, r, 1 - m)
                    for r in range(2):
                        back_rstd(c + r, r)
                    for r in range(2):
                        back_sum(c + r, r, OUTB[r], 1 - m, jj * 2 + (28 + m))
                relink()

        @block.scalar
        def _(act):
            a_ = nc.scalar
            act.sem_inc(gelu_done, 1)
            act.wait_ge(raw_ld, 16 * 9)
            for c in range(DC):
                a_.activation(wqkvg[:, c, :], wraw[:, c, :], ACT.Copy, scale=lncol[:, 0, c:c + 1]).then_inc(w_scaled, 1)
            act.wait_ge(bias_mm, 1)
            a_.activation(bqkv[:, 0:2], FT[:, 0:2], ACT.Copy, scale=DH ** -0.5).then_inc(bias_done, 1)
            a_.activation(bqkv[:, 2:6], FT[:, 2:6], ACT.Copy).then_inc(bias_done, 1)
            a_.activation(bqkv[0:2 * H, 6:7], FT[0:2 * H, 6:7], ACT.Copy).then_inc(bias_done, 1)
            act.wait_ge(stats_done, 2)
            act.wait_ge(bias_done, 3)

            def front_norm(f, i, behind=0):
                act.wait_ge(xt_ld[i], (f >> 1) * 16 + 16)
                if behind is not None:
                    act.wait_ge(fT_done, f - behind)
                a_.activation(xa[i], xt[i], ACT.Identity, scale=sA[:, bass.ds(f, 1)],
                              bias=bA[:, bass.ds(f, 1)]).then_inc(xa_ready, 1)

            def front_evac(f, i, banks, behind=0):
                act.wait_ge(fT_done, f + 1)
                act.wait_ge(qkv_done, f - behind)
                a_.activation(xaT[i].rearrange("p c t -> p (c t)"), banks[0][:, 0:DC * P], ACT.Copy).then_inc(xaT_ready, 1)

            def front_out(f, i, banks):
                act.wait_ge(qkv_done, f + 1)
                act.wait_ge(f_stored[i], (f >> 1) * FST)
                for m in range(3):
                    for hg in range(2):
                        n = m * 2 + hg
                        src = banks[1][:, n * P:(n + 1) * P] if n < 4 else banks[2][:, (n - 4) * P:(n - 3) * P]
                        a_.activation(stg[i][:, :, n, :], src.rearrange("p (b t) -> p b t", b=2), ACT.Identity,
                                      bias=bqkv[:, n:n + 1], scale=DH ** -0.5 if m == 0 else 1.0)
                a_.activation(gst[i], banks[2][0:2 * H, 2 * P:3 * P], ACT.Sigmoid, bias=bqkv[0:2 * H, 6:7]).then_inc(stg_ready, 1)

            def stage_squares(L):
                par, t0 = lookup(L)
                act.wait_ge(win_ld, ((L >> 3) + 1) * WLD)
                act.wait_ge(n2_ready, L)
                for s in range(2):
                    last = a_.activation(sq[:, :, :].rearrange("p (t s) d -> p t s d", s=2)[:, :, s],
                                         win[1][:, par, s, :, bass.ds(t0, ST)].rearrange("p d t -> p t d"), ACT.Square)
                last.then_inc(sq_ready, 1)

            def stage(L, h):
                par, t0 = lookup(L)
                act.wait_ge(win_ld, ((L >> 3) + 1) * WLD)
                act.wait_ge(prod_done, L * 2)
                act.wait_ge(rec_done, L * 2)
                for s in range(2):
                    a_.activation(qs[h][:, :, s, :], win[0][:, par, s, :, bass.ds(t0, ST)].rearrange("p d t -> p t d"),
                                  ACT.Copy)
                a_.activation(g8[h][:, :, :], gwin[:, par, :, 1, bass.ds(t0, ST)].rearrange("p s t -> p t s"),
                              ACT.Copy).then_inc(act_staged, 1)

            def route_norm(I, k, q, h):
                act.wait_ge(x4_ld[h], (I >> 1) * 32 + 32)
                act.wait_ge(r_stored[h], (I >> 1) * 64)
                for r in range(RT):
                    tile = (k * RT + r) * NB2 + q
                    a_.activation(xw[h][:, r, 0:D], x4[h][:, r, :], ACT.Identity, scale=rstd[:, bass.ds(tile, 1)],
                                  bias=nmr[:, bass.ds(tile, 1)]).then_inc(xn_ready, 1)

            def unit_evac(q):
                act.wait_ge(t_done, q + 1)
                act.wait_ge(gu_done, q)
                a_.activation(gT[:, :, :].rearrange("p c t -> p (c t)"), TB[:, 0:DC * P], ACT.Copy).then_inc(gT_ready, 1)

            def unit_silu(q, r):
                act.wait_ge(gu_done, q + 1)
                act.wait_ge(h_ready, q + 1)
                a_.activation(sgu[:, :], (G0, G1)[r % 2][0:FH, 0:2 * P], ACT.Silu).then_inc(sg_ready, 1)

            def expert_out(e, r, h):
                act.wait_ge(y_done, e + (UNITS_R + 1))
                a_.activation(yw[h][r], YB[:, 0:D], ACT.Copy, scale=xg[h][r][:, bass.ds(e + D, 1)]).then_inc(yw_ready, 1)

            front_norm(0, 0, None)
            front_norm(1, 1, None)
            front_evac(0, 0, FRONT0[0])
            with act.Fori(0, AHEAD * NB2 // 2 - 1) as m:
                for i in range(2):
                    f = m * 2 + i
                    front_norm(f + 2, i, 1)
                    front_evac(f + 1, 1 - i, FRONT0[1 - i], 1)
                    front_out(f, i, FRONT0[i])
            f = AHEAD * NB2 - 1
            front_evac(f, 1, FRONT0[1], 1)
            front_out(f - 1, 0, FRONT0[0])
            front_out(f, 1, FRONT0[1])
            act.wait_ge(stats_done, 4)
            stage_squares(0)
            stage(0, 0)
            stage_squares(1)

            def back_sqrt(c, rs):
                act.wait_ge(ve_ready, c + len(rs))
                for r in rs:
                    a_.activation(sd_b[:, r:r + 1], ve_b[:, r:r + 1], ACT.Sqrt).then_inc(sd_ready, 1)

            def back_norm(c, r):
                act.wait_ge(nb_ready, c + 1)
                a_.activation(hb[r], x1[r], ACT.Identity, scale=rs_b[:, r:r + 1], bias=nb_b[:, r:r + 1]).then_inc(hb_ready, 1)

            def back_evac(c, r):
                act.wait_ge(hT_done, c + 1)
                a_.activation(hT[r].rearrange("p c t -> p (c t)"), (TB, LG)[r][:, D:2 * D], ACT.Copy).then_inc(hT_ready, 1)

            def back_gelu(c, r, half):
                act.wait_ge(mid_done, c * 2 + (half + 1))
                for i in range(MC // 2):
                    m = half * (MC // 2) + i
                    last = a_.activation(mid[r][:, m, :], (G0, G1)[half][:, i * P:(i + 1) * P], ACT.Gelu, bias=b1_s[:, m:m + 1])
                last.then_inc(gelu_done, 1)

            for phase, kb0, nb in PHASES:
                if phase == BACK2:
                    act.wait_ge(mlp_bias, 2)
                    for c in range(DC):
                        a_.activation(w1_s[:, c, :], w1_s[:, c, :], ACT.Copy, scale=lncol[:, 2, c:c + 1]).then_inc(mlp_w, 1)

                def body(kb, jj, h, last=False, last2=False):
                    I = iteration(kb0, kb, jj, h)
                    j = jj * 2 + h
                    n = kb * NB2 + j
                    f = I + AHEAD * NB2
                    if not last2:
                        stage_squares(I + 2)
                    if phase in (ROUTE, EXPERTS):
                        q = n * RT + (0 if phase == ROUTE else UNITS_R)
                        front_norm(f, h)
                        if phase == ROUTE:
                            route_norm(I, kb, j, h)
                        unit_evac(q)
                        front_evac(f, h, FRONT)
                        unit_silu(q, 0)
                        front_out(f, h, FRONT)
                        stage(I + 1, 1 - h)
                        unit_evac(q + 1)
                        unit_silu(q + 1, 1)
                        unit_evac(q + 2)
                        if phase == EXPERTS:
                            expert_out(n * RT, 0, h)
                        unit_silu(q + 2, 2)
                        unit_evac(q + 3)
                        if phase == EXPERTS:
                            expert_out(n * RT + 1, 1, h)
                        unit_silu(q + 3, 3)
                        if phase == EXPERTS:
                            expert_out(n * RT + 2, 2, h)
                            expert_out(n * RT + 3, 3, h)
                        else:
                            act.wait_ge(lg_done, I + 1)
                            act.wait_ge(w_ready, I)
                            a_.activation(lg.rearrange("p r e -> p (r e)"), LG[:, 0:RT * E], ACT.Copy).then_inc(lg_copied, 1)
                            act.wait_ge(negm_ready, I + 1)
                            for r in range(RT):
                                x_ = a_.activation(ex[:, r, :], lg[:, r, :], ACT.Exp, bias=negm[:, r:r + 1])
                            x_.then_inc(e_ready, 1)
                            act.wait_ge(mt_done, I + 1)
                            for r in range(RT):
                                x_ = a_.activation(maskT_v[:, j, kb, r],
                                                   LG[0:E, r * P:(r + 1) * P].rearrange("e (b t) -> e b t", b=2), ACT.Copy)
                            x_.then_inc(mT_ready, 1)
                        return
                    if phase == BACK1:
                        c, rs = j + (6 * NB2 - h), (h,)
                    else:
                        c, rs = n * 2 + (0 if phase == BACK2 else 4 * NB2), (0, 1)
                    if phase == BACK2:
                        front_norm(f, h)
                        front_evac(f, h, FRONT)

                    def between():
                        if phase == BACK2:
                            front_out(f, h, FRONT)
                        if not last:
                            stage(I + 1, 1 - h)
                    back_act(c, rs, between)

                def back_act(c, rs, between):
                    c0 = c + rs[0]
                    back_sqrt(c0, rs)
                    for r in rs:
                        back_norm(c + r, r)
                    if between is not None:
                        between()
                    for r in rs:
                        back_evac(c + r, r)
                    for r in rs:
                        for half in range(2):
                            back_gelu(c + r, r, half)

                with act.Fori(0, nb) as kb:
                    if phase != BACK1:
                        with act.Fori(0, NB2 // 2) as jj:
                            body(kb, jj, 0)
                            body(kb, jj, 1)
                    else:
                        with act.Fori(0, NB2 // 2 - 1) as jj:
                            body(kb, jj, 0)
                            body(kb, jj, 1)
                        body(kb, NB2 // 2 - 1, 0, last2=True)
                        body(kb, NB2 // 2 - 1, 1, last=True, last2=True)
            with act.Fori(0, NB2 // 2) as i:
                back_act(i * 2 + 7 * NB2, (0, 1), None)

        @block.tensor
        def _(pe):
            mm = nc.tensor.matmul
            pe.wait_ge(consts, 5)
            pe.wait_ge(raw_ld, 16 * 9)
            for i in range(7):
                n = P if i < 6 else 2 * H
                for c in range(DC):
                    last = mm(FT[0:n, i:i + 1], wraw[:, c, i * P:i * P + n], lncol[:, 1, c:c + 1], start=(c == 0), stop=(c == DC - 1))
            last.then_inc(bias_mm, 1)
            pe.wait_ge(w_scaled, DC)
            pe.wait_ge(bias_done, 3)
            pe.wait_ge(const_ld, 16 * 7)

            def front_T(f, h, banks=FRONT, behind=0):
                pe.wait_ge(xa_ready, f + 1)
                pe.wait_ge(xaT_ready, f - behind)
                for c in range(DC):
                    last = nc.tensor.transpose(banks[0][:, c * P:(c + 1) * P], xa[h][:, c * P:(c + 1) * P], ident[:, :])
                last.then_inc(fT_done, 1)

            def front_mm(f, h, banks=FRONT, behind=0):
                pe.wait_ge(xaT_ready, f + 1)
                pe.wait_ge(stg_ready, f - behind)
                for i in range(7):
                    n = P if i < 6 else 2 * H
                    dst = banks[1][:, i * P:(i + 1) * P] if i < 4 else banks[2][0:n, (i - 4) * P:(i - 3) * P]
                    for c in range(DC):
                        last = mm(dst, wqkvg[:, c, i * P:i * P + n], xaT[h][:, c, :], start=(c == 0), stop=(c == DC - 1))
                last.then_inc(qkv_done, 1)

            def unit_T(q, src):
                pe.wait_ge(gT_ready, q)
                for c in range(DC):
                    last = nc.tensor.transpose(TB[:, c * P:(c + 1) * P], src[:, c * P:(c + 1) * P], ident[:, :])
                last.then_inc(t_done, 1)

            def unit_gu(q, r, wg, wu):
                pe.wait_ge(h_ready, q)
                bk = (G0, G1)[r % 2]
                for i in range(4):
                    w = wg if i < 2 else wu
                    for c in range(DC):
                        last = mm(bk[0:FH, i * P:(i + 1) * P], w[:, c, (i % 2) * FH:(i % 2 + 1) * FH], gT[:, c, :],
                                  start=(c == 0), stop=(c == DC - 1))
                last.then_inc(gu_done, 1)

            def unit_y(q, wd, bias):
                pe.wait_ge(h_ready, q + 2)
                for c in range(2):
                    last = mm(YB[:, 0:D], hg_s[:, c, :], wd[:, c, :], start=(c == 0), stop=(c == 1 and bias is None))
                if bias is not None:
                    last = mm(YB[:, 0:D], ones[0:1, :], bias, start=False, stop=True)
                last.then_inc(y_done, 1)

            front_T(0, 0, FRONT0[0])
            front_T(1, 1, FRONT0[1], 1)
            front_mm(0, 0, FRONT0[0])
            with pe.Fori(0, AHEAD * NB2 // 2 - 1) as m:
                for i in range(2):
                    f = m * 2 + i + 2
                    front_T(f, i, FRONT0[i], 1)
                    front_mm(f - 1, 1 - i, FRONT0[1 - i], 1)
            front_mm(AHEAD * NB2 - 1, 1, FRONT0[1], 1)

            def route_T(h, q, r):
                pe.wait_ge(xn_ready, q + 1)
                unit_T(q, xw[h][:, r, :])

            def route_gu(I, q, r):
                pe.wait_ge(gT_ready, q + 1)
                if r == 0:
                    pe.wait_ge(mT_ready, I)
                for c in range(DC):
                    last = mm(LG[:, r * E:(r + 1) * E], gT[:, c, :], rw_s[:, c, :], start=(c == 0), stop=(c == DC - 1))
                if r == RT - 1:
                    last.then_inc(lg_done, 1)
                unit_gu(q, r, wsgu_s[:, :, 0:F], wsgu_s[:, :, F:2 * F])

            def route_y(q):
                pe.wait_ge(acc_ready, q)
                unit_y(q, wsd_s[:, :, :], b2_s[0:1, :])

            def expert_T(n, q, r, h):
                pe.wait_ge(g_ld[h][r], (n >> 1) * 16 + 16)
                unit_T(q, xg[h][r])

            def expert_gu(n, q, r):
                pe.wait_ge(gT_ready, q + 1)
                pe.wait_ge(ew_ld[r], n * 48 + 48)
                unit_gu(q, r, ew_g[r], ew_u[r])

            def expert_y(e, r):
                pe.wait_ge(yw_ready, e)
                unit_y(e + UNITS_R, ew_d[r], None)

            def back_attn(c, r, half, use):
                pe.wait_ge(bk_ld[half][r], use * 64 + 64)
                if r == 1:
                    pe.wait_ge(fin_ready, c - 1)
                bk = (TB, LG)[r]
                for g in range(2):
                    mm(bk[:, 0:D], oT[half][r][:, g].rearrange("p b t -> p (b t)"), wo_s[:, g, :], start=(g == 0), stop=False)
                mm(bk[:, 0:D], ones[0:1, :], bo_s[0:1, :], start=False, stop=True).then_inc(at_done, 1)

            def back_T(c, r):
                pe.wait_ge(hb_ready, c + 1)
                for i in range(DC):
                    last = nc.tensor.transpose((TB, LG)[r][:, D + i * P:D + (i + 1) * P], hb[r][:, i * P:(i + 1) * P], ident[:, :])
                last.then_inc(hT_done, 1)

            def back_mid(c, r, half):
                if half == 0:
                    pe.wait_ge(hT_ready, c + 1)
                pe.wait_ge(gelu_done, c * 2 + half)
                for i in range(MC // 2):
                    m = half * (MC // 2) + i
                    for k in range(DC):
                        last = mm((G0, G1)[half][:, i * P:(i + 1) * P], w1_s[:, k, m * P:(m + 1) * P], hT[r][:, k, :],
                                  start=(k == 0), stop=(k == DC - 1))
                last.then_inc(mid_done, 1)

            def back_out(c, r):
                pe.wait_ge(gelu_done, c * 2 + 3)
                if r == 0:
                    pe.wait_ge(fin_ready, c)
                for m in range(MC):
                    last = mm((YB, LG)[r][:, 0:D], mid[r][:, m, :], w2_s[:, m, :], start=(m == 0), stop=(m == MC - 1))
                last.then_inc(out_done, 1)

            def back_mlp(c, rs):
                for r in rs:
                    back_T(c + r, r)
                back_mid(c + rs[0], rs[0], 0)
                back_mid(c + rs[0], rs[0], 1)
                if len(rs) == 2:
                    back_mid(c + 1, 1, 0)
                    back_out(c, 0)
                    back_mid(c + 1, 1, 1)
                back_out(c + rs[-1], rs[-1])

            for phase, kb0, nb in PHASES:
                if phase == EXPERTS:
                    pe.wait_ge(mT_ready, 2 * NB2)
                    with pe.Fori(0, E // RT // 2) as i:
                        for a in range(2):
                            pe.wait_ge(onh_ready, i * 2 + (a + 1))
                            pe.wait_ge(slot_used, i * 2)
                            for r in range(RT):
                                last = mm((LG, TB)[a][:, r * CW:(r + 1) * CW], onh[a][:, r, :], diff[a][:, r, :], start=True, stop=True)
                            last.then_inc(slot_mm, 1)
                    pe.wait_ge(slot_used, E // RT)
                    pe.wait_ge(acc_ready, NT)
                if phase == BACK2:
                    pe.wait_ge(h_ready, NT + E + 1)
                    pe.wait_ge(yw_ready, E)
                    pe.wait_ge(mlp_ld, 32)
                    for m in range(MC):
                        for c in range(DC):
                            last = mm(TB[:, m:m + 1], w1_s[:, c, m * P:(m + 1) * P], lncol[:, 3, c:c + 1],
                                      start=(c == 0), stop=(c == DC - 1))
                    last.then_inc(mlp_bias, 1)
                    pe.wait_ge(mlp_bias, 2)
                    pe.wait_ge(mlp_w, DC)
                with pe.Fori(0, nb) as kb:
                    with pe.Fori(0, NB2 // 2) as jj:
                        for h in range(2):
                            I = iteration(kb0, kb, jj, h)
                            j = jj * 2 + h
                            n = kb * NB2 + j
                            f = I + AHEAD * NB2
                            if phase == ROUTE:
                                q = n * RT
                                route_T(h, q, 0)
                                front_T(f, h)
                                route_gu(I, q, 0)
                                front_mm(f, h)
                                route_T(h, q + 1, 1)
                                route_gu(I, q + 1, 1)
                                route_y(q)
                                route_T(h, q + 2, 2)
                                route_gu(I, q + 2, 2)
                                route_y(q + 1)
                                route_T(h, q + 3, 3)
                                route_gu(I, q + 3, 3)
                                route_y(q + 2)
                                route_y(q + 3)
                                pe.wait_ge(mask_ready, I + 1)
                                pe.wait_ge(lg_copied, I + 1)
                                pe.sem_inc(passed, 1)
                                for r in range(RT):
                                    last = nc.tensor.transpose(LG[0:E, r * P:(r + 1) * P], mk[:, r, :], ident[:, :])
                                last.then_inc(mt_done, 1)
                            elif phase == EXPERTS:
                                q = n * RT + UNITS_R
                                expert_T(n, q, 0, h)
                                front_T(f, h)
                                expert_gu(n, q, 0)
                                front_mm(f, h)
                                expert_T(n, q + 1, 1, h)
                                expert_gu(n, q + 1, 1)
                                expert_y(n * RT, 0)
                                expert_T(n, q + 2, 2, h)
                                expert_gu(n, q + 2, 2)
                                expert_y(n * RT + 1, 1)
                                expert_T(n, q + 3, 3, h)
                                expert_gu(n, q + 3, 3)
                                expert_y(n * RT + 2, 2)
                                expert_y(n * RT + 3, 3)
                            else:
                                if phase == BACK1:
                                    c, rs, half, use = j + (6 * NB2 - h), (h,), 0, jj + 13
                                else:
                                    m = n + (0 if phase == BACK2 else 2 * NB2)
                                    c, rs, half, use = m * 2, (0, 1), h, m >> 1
                                for r in rs:
                                    back_attn(c + r, r, half, use)
                                if phase == BACK2:
                                    front_T(f, h)
                                    front_mm(f, h)
                                back_mlp(c, rs)
            with pe.Fori(0, NB2 // 4) as jj:
                for m in range(2):
                    c = (jj * 2 + m) * 2 + 7 * NB2
                    for r in range(2):
                        back_attn(c + r, r, 1 - m, jj + (12 if m == 0 else 18 - r))
                    back_mlp(c, (0, 1))


_INS = ['L0_attn_x', 'L0_attn_Wq', 'L0_attn_Wk', 'L0_attn_Wv', 'L0_attn_Wb', 'L0_attn_Wg', 'L0_attn_Wo', 'L0_attn_bo',
        'L0_attn_ln1_g', 'L0_attn_ln1_b', 'L0_attn_ln2_g', 'L0_attn_ln2_b', 'L0_attn_w1', 'L0_attn_b1', 'L0_attn_w2',
        'L0_attn_b2', 'L0_ffn_router_w', 'L0_ffn_w_gate', 'L0_ffn_w_up', 'L0_ffn_w_down', 'L0_ffn_ws_gate_up',
        'L0_ffn_ws_down']


def kernel(**inputs):
    import numpy as _np
    import concourse.bacc as _bacc
    from concourse import mybir as _mybir
    from concourse.bass_utils import run_bass_kernel_spmd as _run

    nc = _bacc.Bacc("TRN2", target_bir_lowering=False, num_devices=1)
    arrays, args = {}, []
    for name in _INS:
        a = _np.asarray(inputs[name])
        if name == 'L0_ffn_router_w':
            a = a.T
        a = _np.ascontiguousarray(a)
        arrays[f"in_{name}"] = a
        args.append(nc.dram_tensor(f"in_{name}", a.shape, _mybir.dt.from_np(a.dtype), kind="ExternalInput").ap())
    out = nc.dram_tensor("out_0", (B, T, D), _mybir.dt.float32, kind="ExternalOutput").ap()
    layer(nc, *args, out)
    r = _run(nc, [arrays], core_ids=[0])
    return r.results[0]["out_0"]
```

```python
from contextlib import ExitStack

import concourse.bass as bass
from concourse import mybir

ALU = mybir.AluOpType
ACT = mybir.ActivationFunctionType
AX = mybir.AxisListType
F32 = mybir.dt.float32
BF16 = mybir.dt.bfloat16
I32 = mybir.dt.int32

P = 128
B, T, D = 16, 512, 256
H, DH = 16, 16
DC = D // P
BLK = 64
NBLK = T // BLK
ST = 8
NB2 = B // 2
NT = NBLK * NB2
E, K, CAP = 64, 8, 128
F = 192
FH = F // 2
M = 4 * D
MC = M // P
TOK = B * T
XW = D + E
EPS = 1e-5
AHEAD = 2
RT = 4
S2 = DH * DH
ROUTE, EXPERTS, BACK2, BACK2_LATE, BACK1 = range(5)
PHASES = [(ROUTE, 0, 2), (EXPERTS, 2, 2), (BACK2, 4, 2), (BACK2_LATE, 6, 1), (BACK1, 7, 1)]
FST = 2 * 16
WLD = 10 * 16
BUF = 2


def layer(nc, x, Wq, Wk, Wv, Wb, Wg, Wo, bo, ln1_g, ln1_b, ln2_g, ln2_b, w1, b1, w2, b2,
          router_wT, w_gate, w_up, w_down, ws_gate_up, ws_down, out):
    ctx = ExitStack()
    with ctx:
        def sb(name, shape, dt=F32):
            return ctx.enter_context(nc.sbuf_tensor(name, shape, dt))

        def sem(name):
            return ctx.enter_context(nc.semaphore(name))

        qkv_d = nc.dram_tensor("qkv_d", (NBLK, B, 6, P, BLK), F32, kind="Internal").ap()
        gat_d = nc.dram_tensor("gat_d", (NBLK, B, 2, H, BLK), F32, kind="Internal").ap()
        o_d = nc.dram_tensor("o_d", (NBLK, B, 2, P, BLK), F32, kind="Internal").ap()
        xw_d = nc.dram_tensor("xw_d", (TOK + P, XW), F32, kind="Internal").ap()
        acc_d = nc.dram_tensor("acc_d", (TOK + P, D), F32, kind="Internal").ap()
        cum_d = nc.dram_tensor("cum_d", (E, BLK + TOK), F32, kind="Internal").ap()

        ident = sb("ident", [P, P])
        ones = sb("ones", [P, P])
        iot = sb("iot", [P, CAP + 1], I32)
        zeros = sb("zeros", [P, XW])
        slot_row = sb("slot_row", [P, CAP])
        slot_col = sb("slot_col", [P, 1])
        half_pow = sb("half_pow", [P, 2])
        wqkvg = sb("wqkvg", [P, DC, 3 * D + 2 * H])
        wo_s = sb("wo_s", [P, DC, D])
        rw_s = sb("rw_s", [P, DC, E])
        wsgu_s = sb("wsgu_s", [P, DC, 2 * F])
        wsd_s = sb("wsd_s", [FH, 2, D])
        bo_s = sb("bo_s", [1, D])
        b2_s = sb("b2_s", [1, D])
        lncol = sb("lncol", [P, 4, DC])
        bqkv = sb("bqkv", [P, 8])
        b1_in = sb("b1_in", [P, MC])
        b1_s = sb("b1_s", [P, MC])
        mean = sb("mean", [P, NT])
        var = sb("var", [P, NT])
        rstd = sb("rstd", [P, NT])
        nmr = sb("nmr", [P, NT])
        sA = sb("sA", [P, NT])
        bA = sb("bA", [P, NT])
        tmp_st = sb("tmp_st", [P, NT])

        xt = [sb(f"xt{i}", [P, D])[:, :] for i in range(BUF)]
        xa = [sb(f"xa{i}", [P, D])[:, :] for i in range(BUF)]
        xaT = [sb(f"xaT{i}", [P, DC, P])[:, :, :] for i in range(BUF)]
        stg = [sb(f"stg{i}", [P, 2, 6, BLK])[:, :, :, :] for i in range(BUF)]
        gst = [sb(f"gst{i}", [2 * H, P])[:, :] for i in range(BUF)]

        win = [sb(f"win_{n}", [P, BUF, 2, DH, BLK]) for n in "qkv"]
        gwin = sb("gwin", [P, BUF, 2, 2, BLK])
        sq = sb("sq", [P, ST * 2, DH])
        n2 = sb("n2", [P, ST * 2])
        nrm = sb("nrm", [P, ST * 2])
        nrm_e = sb("nrm_e", [P, ST * 2])
        rk = [sb(f"rk{h}", [P, ST * 2]) for h in range(BUF)]
        kn = [sb(f"kn{h}", [P, ST, 2, DH]) for h in range(BUF)]
        bv = [sb(f"bv{h}", [P, ST, 2, DH]) for h in range(BUF)]
        qs = [sb(f"qs{h}", [P, ST, 2, DH]) for h in range(BUF)]
        g8 = [sb(f"g8{h}", [P, ST, 2]) for h in range(BUF)]
        bg = [sb(f"bg{h}", [P, ST, 2]) for h in range(BUF)]
        S = [sb(f"S{h}", [P, ST, 2, S2]) for h in range(BUF)]
        prod = sb("prod", [P, 2, S2])
        outer = sb("outer", [P, 2, S2])
        kS = sb("kS", [P, 2, DH])
        nu = sb("nu", [P, 2, DH])
        HS = ST // 2
        rp = sb("rp", [P, HS * 2 * DH, 16])
        r1 = sb("r1", [P, HS * 2 * DH, 8])
        r2 = sb("r2", [P, HS * 2 * DH, 4])
        r3 = sb("r3", [P, HS * 2 * DH, 2])
        oblk = sb("oblk", [P, 2, DH, BLK])

        gT = sb("gT", [P, DC, P])
        sgu = sb("sgu", [FH, 2 * P])
        hg_s = sb("hg_s", [FH, 2, P])

        REG = 12288
        region = sb("region", [P, REG])
        at = [0]

        def carve(words, restart=False):
            if restart:
                at[0] = 0
            a = region[:, at[0]:at[0] + words]
            at[0] += words
            assert at[0] <= REG
            return a

        xs = [carve(NB2 * D, n == 0).rearrange("p (q d) -> p q d", d=D) for n in range(BUF)]
        wraw = carve(DC * (3 * D + 2 * H)).rearrange("p (c n) -> p c n", c=DC)
        bn6 = carve(NB2 * 6).rearrange("p (q s) -> p q s", s=6)
        mv8 = carve(NB2 * 2).rearrange("p (q s) -> p q s", s=2)
        x4 = [carve(RT * D, i == 0).rearrange("p (r d) -> p r d", r=RT) for i in range(BUF)]
        xw = [carve(RT * XW).rearrange("p (r d) -> p r d", r=RT) for i in range(BUF)]
        acc4 = [carve(RT * D).rearrange("p (r d) -> p r d", r=RT) for i in range(BUF)]
        lg, ex, mk, wt, rep = [carve(RT * E).rearrange("p (r e) -> p r e", r=RT) for _ in range(5)]
        mx = carve(RT * 8).rearrange("p (r e) -> p r e", r=RT)
        negm, wsum, wrec = [carve(RT) for _ in range(3)]
        assert at[0] <= TOK
        at[0] = TOK
        maskT = carve(TOK // 2)[0:E, :].bitcast(BF16)
        cum = carve(TOK, True)[0:E, :]
        cur = region[:, 0:E * BLK].rearrange("p (e j) -> p e j", e=E)
        prv = region[:, E * BLK:2 * E * BLK].rearrange("p (e j) -> p e j", e=E)
        at[0] = 2 * E * BLK
        CW = BLK + 1
        onh = [carve(RT * CAP).rearrange("p (r s) -> p r s", r=RT) for _ in range(2)]
        diff = [carve(RT * CW).rearrange("p (r s) -> p r s", r=RT) for _ in range(2)]
        cnt = [carve(RT * BLK).rearrange("p (r s) -> p r s", r=RT) for _ in range(2)]
        csum = [carve(RT) for _ in range(2)]
        sidx = carve(E)
        sgei = carve(E)
        idx_i = sb("idx_i", [P, E], I32)
        ew_g = [carve(DC * F, r == 0).rearrange("p (c f) -> p c f", c=DC) for r in range(RT)]
        ew_u = [carve(DC * F).rearrange("p (c f) -> p c f", c=DC) for r in range(RT)]
        ew_d = [carve(2 * D)[0:FH, :].rearrange("p (c f) -> p c f", c=2) for r in range(RT)]
        xg = [[carve(XW) for r in range(RT)] for i in range(BUF)]
        yw = [[carve(D) for r in range(RT)] for i in range(BUF)]
        idx4 = [sb(f"idx4{i}", [P, RT], I32)[:, :] for i in range(BUF)]
        def load_bufs():
            return [carve(D) for _ in range(2)]

        EW = RT * (2 * DC * F + 2 * D)
        EX = EW + BUF * RT * (XW + D)
        w2_s = carve(MC * D, True).rearrange("p (c n) -> p c n", c=MC)
        oT, xn_b, ac_b = [load_bufs()], [load_bufs()], []
        x1 = [carve(D) for _ in range(2)]
        hb = [carve(D) for _ in range(2)]
        fin = [carve(D) for _ in range(2)]
        hT = [carve(DC * P).rearrange("p (c t) -> p c t", c=DC) for _ in range(2)]
        assert at[0] <= EW
        at[0] = EW
        oT.append(load_bufs()); xn_b.append(load_bufs())
        ac_b = [load_bufs() for _ in range(2)]
        mid = [carve(MC * P).rearrange("p (c t) -> p c t", c=MC) for _ in range(2)]
        assert at[0] <= EX
        x1_odd = [win[0][:, 0, 0].rearrange("p d t -> p (d t)")[:, r * D:(r + 1) * D] for r in range(2)]
        at[0] = EX
        w1_s = carve(DC * M).rearrange("p (c n) -> p c n", c=DC)
        bn_b = carve(2 * 6).rearrange("p (r s) -> p r s", r=2)
        mv_b = carve(2 * 2).rearrange("p (r s) -> p r s", r=2)
        ve_b, sd_b, rs_b, nb_b = [carve(2) for _ in range(4)]
        oT = [[x.rearrange("p (g b t) -> p g b t", b=2, g=2) for x in half] for half in oT]

        bank = [ctx.enter_context(nc.psum_tensor(f"bank{i}", [P, 512], F32)) for i in range(8)]
        FT, FQ, FV, TB, LG, G0, G1, YB = bank
        FRONT = (FT, FQ, FV)
        FRONT0 = (FRONT, (TB, G0, G1))

        const_ld = sem("const_ld"); raw_ld = sem("raw_ld"); consts = sem("consts")
        xs_ld = [sem(f"xs_ld{i}") for i in range(BUF)]
        xs_more = [sem(f"xs_more{i}") for i in range(BUF)]
        xs_used = sem("xs_used"); stats_in = sem("stats_in"); stats_done = sem("stats_done")
        pch = sem("pch"); vch = sem("vch"); ach = sem("ach")
        bias_mm = sem("bias_mm"); w_scaled = sem("w_scaled"); bias_done = sem("bias_done")
        xt_ld = [sem(f"xt_ld{i}") for i in range(BUF)]; xa_ready = sem("xa_ready"); fT_done = sem("fT_done")
        xaT_ready = sem("xaT_ready"); qkv_done = sem("qkv_done"); stg_ready = sem("stg_ready")
        f_stored = [sem(f"f_stored{i}") for i in range(BUF)]
        win_ld = sem("win_ld"); sq_ready = sem("sq_ready"); n2_ready = sem("n2_ready")
        nrm_ready = sem("nrm_ready"); rk_ready = sem("rk_ready")
        act_staged = sem("act_staged"); pool_staged = sem("pool_staged")
        rec_done = sem("rec_done"); prod_done = sem("prod_done"); o_stored = sem("o_stored")
        x4_ld = [sem(f"x4_ld{i}") for i in range(BUF)]; xn_ready = sem("xn_ready"); t_done = sem("t_done")
        gT_ready = sem("gT_ready"); gu_done = sem("gu_done"); sg_ready = sem("sg_ready")
        h_ready = sem("h_ready"); y_done = sem("y_done"); acc_ready = sem("acc_ready")
        lg_done = sem("lg_done"); lg_copied = sem("lg_copied"); negm_ready = sem("negm_ready")
        e_ready = sem("e_ready"); mask_ready = sem("mask_ready"); w_ready = sem("w_ready")
        mt_done = sem("mt_done"); mT_ready = sem("mT_ready"); r_stored = [sem(f"r_stored{i}") for i in range(BUF)]
        zero_st = sem("zero_st")
        cum_ready = sem("cum_ready"); cum_st = sem("cum_st"); cur_ld = [sem(f"cur_ld{i}") for i in range(2)]
        onh_ready = sem("onh_ready"); slot_mm = sem("slot_mm"); slot_used = sem("slot_used")
        slots_ready = sem("slots_ready")
        ew_ld = [sem(f"ew_ld{r}") for r in range(RT)]
        g_ld = [[sem(f"g_ld{i}{r}") for r in range(RT)] for i in range(BUF)]
        yw_ready = sem("yw_ready"); sc_done = sem("sc_done")
        mlp_ld = sem("mlp_ld"); mlp_bias = sem("mlp_bias"); mlp_w = sem("mlp_w")
        bk_ld = [[sem(f"bk_ld{i}{r}") for r in range(2)] for i in range(BUF)]
        ac_ld = [[sem(f"ac_ld{i}{r}") for r in range(2)] for i in range(BUF)]
        rows_free = sem("rows_free"); last_read = sem("last_read")
        at_done = sem("at_done"); x1_ready = sem("x1_ready"); ve_ready = sem("ve_ready")
        sd_ready = sem("sd_ready"); nb_ready = sem("nb_ready"); hb_ready = sem("hb_ready")
        hT_done = sem("hT_done"); hT_ready = sem("hT_ready"); mid_done = sem("mid_done")
        gelu_done = sem("gelu_done"); out_done = sem("out_done"); fin_ready = sem("fin_ready")
        fin_st = [sem(f"fin_st{i}") for i in range(2)]

        passed = sem("passed")

        x_t = x.rearrange("(q b) (k t) d -> k q b t d", b=2, t=BLK)
        out_t = out.rearrange("(q b) (k t) d -> k q b t d", b=2, t=BLK)
        x_r = x.rearrange("(q b) (m r t) d -> m q b t r d", b=2, t=BLK, r=RT)
        xw_r = xw_d[0:TOK, :].rearrange("(q b m r t) d -> m q b t r d", q=NB2, b=2, m=T // (RT * BLK), t=BLK)
        acc_r = acc_d[0:TOK, :].rearrange("(q b m r t) d -> m q b t r d", q=NB2, b=2, m=T // (RT * BLK), t=BLK)
        xw_t = xw_d[0:TOK, :].rearrange("(q b k t) d -> k q b t d", q=NB2, b=2, t=BLK)
        acc_t = acc_d[0:TOK, :].rearrange("(q b k t) d -> k q b t d", q=NB2, b=2, t=BLK)
        qkv_st = qkv_d.rearrange("k (q b) i p t -> k q p (b i) t", b=2)
        gat_st = gat_d.rearrange("k (q b) w h t -> k q (w h) b t", b=2)
        qkv_ld = qkv_d.rearrange("k (s b) (m g) (h d) t -> k m s b (g h) (d t)", s=2, m=3, h=P // DH)
        gat_ld = gat_d.rearrange("k (s b) w h t -> k s w b h t", s=2)
        o_st = o_d.rearrange("k (s b) g (h v) t -> k (b g h) s (v t)", s=2, h=P // DH)
        o_ld = o_d.rearrange("k (q b) g p t -> k q g p b t", b=2)
        maskT_v = maskT.rearrange("e (q b m r t) -> e q m r b t", q=NB2, b=2, r=RT, t=BLK)

        def iteration(kb0, kb, jj, h):
            return (kb + kb0) * NB2 + jj * 2 + h

        def lookup(L):
            return (L >> 3) & 1, (L & 7) * ST

        UNITS_R = NT

        block = ctx.enter_context(nc.Block())

        def load_xs(queue, k, s, ld):
            for b in range(2):
                queue.dma_start(xs[s][BLK * b:BLK * (b + 1), :, :],
                                x_t[k].rearrange("q b t d -> b t q d")[b]).then_inc(ld[s], 16)

        def stage_values(queue, engine, L, h):
            par, t0 = lookup(L)
            queue.wait_ge(win_ld, ((L >> 3) + 1) * WLD)
            queue.wait_ge(rec_done, L * 2)
            beta = gwin[:, par, :, 0, bass.ds(t0, ST)].rearrange("p s t -> p t s")
            gg = gwin[:, par, :, 1, bass.ds(t0, ST)].rearrange("p s t -> p t s")
            engine.tensor_tensor(bg[h][:, :, :], beta, gg, ALU.mult)
            for s in range(2):
                engine.tensor_tensor(bv[h][:, :, s, :],
                                win[2][:, par, s, :, bass.ds(t0, ST)].rearrange("p d t -> p t d"),
                                gwin[:, par, s, 0, bass.ds(t0, ST)].unsqueeze(2).to_broadcast([P, ST, DH]),
                                ALU.mult)

        def stage_keys(queue, engine, L, h):
            par, t0 = lookup(L)
            queue.wait_ge(rk_ready, L + 1)
            rk_ = rk[h][:, :].rearrange("p (t s) -> p t s", s=2)
            for s in range(2):
                last = engine.tensor_tensor(
                    kn[h][:, :, s, :],
                    win[1][:, par, s, :, bass.ds(t0, ST)].rearrange("p d t -> p t d"),
                    rk_[:, :, s].unsqueeze(2).to_broadcast([P, ST, DH]),
                    ALU.mult)
            last.then_inc(pool_staged, 1)

        @block.sync
        def _(sp):
            for s in range(2):
                load_xs(sp, s, s, xs_ld)
            for m, w in enumerate((Wq, Wk, Wv)):
                sp.dma_start(wraw[:, :, m * D:(m + 1) * D], w.rearrange("(c p) n -> p c n", p=P)).then_inc(raw_ld, 16)
            for m, w in enumerate((Wb, Wg)):
                sp.dma_start(wraw[:, :, 3 * D + m * H:3 * D + (m + 1) * H],
                             w.rearrange("(c p) n -> p c n", p=P)).then_inc(raw_ld, 16)
            for m, w in enumerate((ln1_g, ln1_b, ln2_g, ln2_b)):
                sp.dma_start(lncol[:, m, :], w.rearrange("(c p) -> p c", p=P), allow_slow_non_contiguous=True).then_inc(raw_ld, 16)

            def front_load(f, k, q, i):
                sp.dma_start(xt[i], x_t[k, q]).then_inc(xt_ld[i], 16)

            for i in range(2):
                front_load(i, 0, i, i)
            sp.dma_start(wo_s[:, :, :], Wo.rearrange("(c p) n -> p c n", p=P)).then_inc(const_ld, 16)
            sp.dma_start(rw_s[:, :, :], router_wT.rearrange("(c p) n -> p c n", p=P)).then_inc(const_ld, 16)
            sp.dma_start(wsgu_s[:, :, :], ws_gate_up.rearrange("(c p) n -> p c n", p=P)).then_inc(const_ld, 16)
            sp.dma_start(wsd_s[:, :, :], ws_down.rearrange("(c p) n -> p c n", p=FH)).then_inc(const_ld, 16)
            sp.dma_start(bo_s[:, :], bo.rearrange("(a n) -> a n", a=1)).then_inc(const_ld, 16)
            sp.dma_start(b2_s[:, :], b2.rearrange("(a n) -> a n", a=1)).then_inc(const_ld, 16)
            sp.dma_start(b1_in[:, :], b1.rearrange("(c p) -> p c", p=P), allow_slow_non_contiguous=True).then_inc(const_ld, 16)
            sp.wait_ge(consts, 5)
            sp.dma_start(xw_d[TOK:TOK + P, :], zeros[:, :]).then_inc(zero_st, 16)
            sp.dma_start(acc_d[TOK:TOK + P, :], zeros[:, 0:D]).then_inc(zero_st, 16)

            def front_store(f, k, q, i):
                sp.wait_ge(stg_ready, f + 1)
                sp.dma_start(qkv_st[k, q], stg[i].rearrange("p b i t -> p (b i) t")).then_inc(f_stored[i], 16)
                sp.dma_start(gat_st[k, q], gst[i].rearrange("p (b t) -> p b t", b=2)).then_inc(f_stored[i], 16)

            def load_window(k, par, jobs):
                for i in range(BUF):
                    sp.wait_ge(f_stored[i], jobs * (FST // 2))
                sp.sem_inc(passed, 1)
                for m in range(3):
                    for s in range(2):
                        sp.dma_start(win[m][:, par, s].rearrange("p d t -> p (d t)"), qkv_ld[k, m, s]).then_inc(win_ld, 16)
                for s in range(2):
                    for w in range(2):
                        sp.dma_start(gwin[:, par, s, w], gat_ld[k, s, w]).then_inc(win_ld, 16)

            def front_next(f, h):
                sp.wait_ge(xa_ready, f + 1)
                g_ = (f + 2) % NT
                front_load(f + 2, g_ // NB2, g_ % NB2, h)

            front_next(0, 0)
            for lo, hi in ((0, NB2 // 2 + 1), (NB2 // 2 + 1, AHEAD * NB2 // 2 - 1)):
                with sp.Fori(lo, hi) as i:
                    for h in range(2):
                        f = i * 2 + h
                        front_next(f + 1, 1 - h)
                        front_store(f, f // NB2, f % NB2, h)
                if lo == 0:
                    load_window(0, 0, NB2)
            f = AHEAD * NB2 - 1
            front_next(f, 1)
            front_store(f - 1, AHEAD - 1, NB2 - 2, 0)
            front_store(f, AHEAD - 1, NB2 - 1, 1)

            def route_load(I, k, q, h):
                for b in range(2):
                    sp.dma_start(x4[h][BLK * b:BLK * (b + 1), :, :], x_r[k, q, b]).then_inc(x4_ld[h], 16)

            def route_store(I, k, q, h):
                sp.wait_ge(w_ready, I + 1)
                sp.sem_inc(passed, 1)
                sp.wait_ge(acc_ready, (I + 1) * RT)
                for b in range(2):
                    sp.dma_start(xw_r[k, q, b], xw[h][BLK * b:BLK * (b + 1), :, :]).then_inc(r_stored[h], 16)
                    sp.dma_start(acc_r[k, q, b], acc4[h][BLK * b:BLK * (b + 1), :, :]).then_inc(r_stored[h], 16)

            def experts(n):
                for r in range(RT):
                    e = n * RT + r
                    sp.wait_ge(y_done, e + (UNITS_R - RT + 1))
                    sp.dma_start(ew_g[r], w_gate[e].rearrange("(c p) f -> p c f", p=P)).then_inc(ew_ld[r], 16)
                    sp.dma_start(ew_u[r], w_up[e].rearrange("(c p) f -> p c f", p=P)).then_inc(ew_ld[r], 16)
                    sp.dma_start(ew_d[r], w_down[e].rearrange("(c p) f -> p c f", p=FH)).then_inc(ew_ld[r], 16)

            def back_load_rows(h, r, k, q):
                for g in range(2):
                    sp.dma_start(oT[h][r][:, g], o_ld[k, q, g]).then_inc(bk_ld[h][r], 16)
                sp.dma_start(xn_b[h][r], xw_t[k, q, :, :, 0:D]).then_inc(bk_ld[h][r], 16)

            def back_load_sums(h, r, k, q):
                sp.dma_start(ac_b[h][r], acc_t[k, q]).then_inc(ac_ld[h][r], 16)

            def back_load(h, r, k, q):
                back_load_rows(h, r, k, q)
                back_load_sums(h, r, k, q)

            def back_store(c, r, k, q):
                sp.wait_ge(fin_ready, c + 1)
                sp.dma_start(out_t[k, q], fin[r]).then_inc(fin_st[r], 16)

            for phase, kb0, nb in PHASES:
                if phase == EXPERTS:
                    sp.wait_ge(cum_ready, 1)
                    sp.dma_start(cum_d[:, BLK:BLK + TOK], cum).then_inc(cum_st, 16)
                    sp.dma_start(cum_d[:, 0:BLK], zeros[0:E, 0:BLK]).then_inc(cum_st, 16)
                    sp.wait_ge(cum_st, 32)
                    cum_b = cum_d.rearrange("e (k j) -> k e j", j=BLK)
                    for e in range(2):
                        es = slice(e * E // 2, (e + 1) * E // 2)
                        sp.dma_start(cur[:, es], cum_b[1:P + 1, es]).then_inc(cur_ld[e], 16)
                        sp.dma_start(prv[:, es], cum_b[0:P, es]).then_inc(cur_ld[e], 16)
                    sp.wait_ge(slots_ready, 1)
                if phase == ROUTE:
                    sp.wait_ge(stats_in, 2)
                    route_load(0, 0, 0, 0)
                if phase == BACK2:
                    sp.dma_start(w1_s, w1.rearrange("(c p) n -> p c n", p=P)).then_inc(mlp_ld, 16)
                    sp.wait_ge(y_done, UNITS_R + E)
                    sp.wait_ge(o_stored, 16)
                    for r in range(2):
                        back_load_rows(0, r, 0, r)
                    sp.wait_ge(mlp_ld, 16)
                    sp.dma_start(w2_s, w2.rearrange("(c p) n -> p c n", p=P)).then_inc(mlp_ld, 16)
                if phase == BACK1:
                    sp.wait_ge(o_stored, 7 * 16)
                    sp.wait_ge(fin_ready, 6 * NB2)
                    for r in range(2):
                        sp.wait_ge(bk_ld[0][r], 48 * 13)
                        sp.wait_ge(ac_ld[0][r], 16 * 13)
                    back_load(0, 0, 6, 0)
                def last_rows():
                    sp.wait_ge(sc_done, 16 * E)
                    for r in range(RT):
                        sp.wait_ge(g_ld[0][r], 16 * (E // RT // 2 + 1))
                    for r in range(2):
                        back_load_sums(0, r, 0, r)
                    sp.sem_inc(rows_free, 1)

                if phase == BACK2:
                    last_rows()
                with sp.Fori(0, nb) as kb:
                    def jobs(jj):
                        for h in range(2):
                            I = iteration(kb0, kb, jj, h)
                            j = jj * 2 + h
                            f = I + AHEAD * NB2
                            if phase == EXPERTS:
                                experts(kb * NB2 + j)
                            if phase in (ROUTE, EXPERTS, BACK2):
                                front_next(f, h)
                            if phase == ROUTE:
                                sp.wait_ge(acc_ready, I * RT)
                                n_ = (I + 1) % (2 * NB2)
                                route_load(I + 1, n_ // NB2, n_ % NB2, 1 - h)
                                front_store(f, f // NB2, f % NB2, h)
                                route_store(I, kb, j, h)
                            if phase == EXPERTS:
                                front_store(f, f // NB2, f % NB2, h)
                            if phase in (BACK2, BACK2_LATE):
                                n = (kb + (kb0 - 4)) * NB2 + j
                                n_ = (n + 1) % (3 * NB2)
                                sp.wait_ge(o_stored, (n_ // 4 + 1) * 16)
                                sp.sem_inc(passed, 1)
                                sp.wait_ge(fin_ready, n * 2)
                                for r in range(2):
                                    back_load(1 - h, r, n_ // 4, (n_ % 4) * 2 + r)
                                if phase == BACK2:
                                    front_store(f, f // NB2, f % NB2, h)
                                for r in range(2):
                                    back_store(n * 2 + r, r, n // 4, (n % 4) * 2 + r)
                            if phase == BACK1:
                                sp.wait_ge(fin_ready, j + 6 * NB2)
                                back_load(0, 1 - h, 6, (j + 1) % NB2)
                                back_store(j + 6 * NB2, h, 6, j)
                    with sp.Fori(0, 1) as jj:
                        jobs(jj)
                    if phase != BACK1:
                        sp.wait_ge(act_staged, (kb + kb0) * NB2)
                        sp.wait_ge(pool_staged, (kb + kb0) * NB2)
                        sp.wait_ge(win_ld, (kb + (kb0 + 1)) * WLD)
                        load_window(kb + (kb0 + 1), (kb + (kb0 + 1)) & 1, (kb + (kb0 + 2)) * NB2)
                    with sp.Fori(1, NB2 // 2) as jj:
                        jobs(jj)
            sp.wait_ge(o_stored, 16 * NBLK)
            for i in range(NB2 // 2 + 1):
                if i < NB2 // 2:
                    sp.wait_ge(fin_ready, 7 * NB2 + max(i - 1, 0) * 2)
                    if i == 1:
                        sp.wait_ge(bk_ld[0][0], 48 * (12 + 1 + 5))
                        sp.wait_ge(ac_ld[0][0], 16 * (12 + 1 + 5))
                    for r in range(2):
                        back_load((i + 1) % 2, r, 7, i * 2 + r)
                if i:
                    for r in range(2):
                        back_store((i - 1) * 2 + r + 7 * NB2, r, 7, (i - 1) * 2 + r)
            for r in range(2):
                sp.wait_ge(fin_st[r], 16 * NT // 2)
                sp.wait_ge(r_stored[r], 64 * NB2)
            sp.wait_ge(zero_st, 32)
            for i in range(BUF):
                sp.wait_ge(f_stored[i], FST // 2 * NT)
                sp.wait_ge(xt_ld[i], 16 * (NT // 2 + 1))

        @block.gpsimd
        def _(pool):
            count = [0]

            def link(ins):
                count[0] += 1
                ins.then_inc(pch, 1)
                pool.wait_ge(pch, count[0])

            def relink():
                pool.wait_ge(pch, count[0])
                pool.sem_clear(pch)
                count[0] = 0

            g = nc.gpsimd
            link(g.memset(ident[:, :], 0.0))
            g.memset(ones[:, :], 1.0).then_inc(consts, 1)
            g.memset(zeros[:, :], 0.0).then_inc(consts, 1)
            g.memset(half_pow[:, 0:1], -0.5)
            link(g.memset(half_pow[:, 1:2], 0.5))
            link(g.iota(iot[:, 0:CAP], [[1, CAP]], base=0, channel_multiplier=0))
            link(g.iota(iot[:, CAP:CAP + 1], [[0, 1]], base=0, channel_multiplier=1))
            g.tensor_copy(slot_row[:, :], iot[:, 0:CAP]).then_inc(consts, 1)
            g.tensor_copy(slot_col[:, :], iot[:, CAP:CAP + 1]).then_inc(consts, 1)
            g.affine_select(out=ident[:, :], in_=ident[:, :], compare_op=ALU.not_equal, fill=1.0,
                            base=0, pattern=[[-1, P]], channel_multiplier=1).then_inc(consts, 1)
            pool.sem_inc(prod_done, 2)

            def power(o, a, which, n):
                return g.tensor_tensor(o, a, half_pow[:, which:which + 1].to_broadcast([P, n]), ALU.pow)

            def factors(part, lo, hi):
                n = hi - lo
                pool.wait_ge(stats_in, part + 1)
                link(g.tensor_scalar(tmp_st[:, lo:hi], var[:, lo:hi], EPS, None, ALU.add))
                link(power(rstd[:, lo:hi], tmp_st[:, lo:hi], 0, n))
                link(g.tensor_tensor(tmp_st[:, lo:hi], var[:, lo:hi], rstd[:, lo:hi], ALU.mult))
                link(g.tensor_tensor(tmp_st[:, lo:hi], tmp_st[:, lo:hi], rstd[:, lo:hi], ALU.mult))
                link(g.tensor_scalar(tmp_st[:, lo:hi], tmp_st[:, lo:hi], EPS, None, ALU.add))
                link(power(sA[:, lo:hi], tmp_st[:, lo:hi], 0, n))
                link(g.tensor_tensor(sA[:, lo:hi], sA[:, lo:hi], rstd[:, lo:hi], ALU.mult))
                link(g.tensor_scalar(tmp_st[:, lo:hi], mean[:, lo:hi], -1.0, None, ALU.mult))
                g.tensor_tensor(bA[:, lo:hi], tmp_st[:, lo:hi], sA[:, lo:hi], ALU.mult).then_inc(stats_done, 1)
                g.tensor_tensor(nmr[:, lo:hi], tmp_st[:, lo:hi], rstd[:, lo:hi], ALU.mult).then_inc(stats_done, 1)

            def more_xs(i):
                for s in range(2):
                    pool.wait_ge(xs_used, i * 2 + (s - 1))
                    load_xs(pool, i * 2 + s, s, xs_more)

            more_xs(1)
            factors(0, 0, AHEAD * NB2)
            with pool.Fori(2, NBLK // 2) as i:
                more_xs(i)
            factors(1, AHEAD * NB2, NT)
            relink()

            def stage_norm(L):
                pool.wait_ge(n2_ready, L + 1)
                power(nrm[:, :], n2[:, :], 1, ST * 2).then_inc(nrm_ready, 1)

            def reads(I, h, half, j, mid_work=None):
                lo = half * HS
                pool.wait_ge(rec_done, I * 2 + (3 + half))
                if half == 0:
                    pool.wait_ge(o_stored, (I >> 3) * 16)
                pool.wait_ge(act_staged, I + 1)
                g.tensor_tensor(
                    rp[:, :, :].rearrange("p (a v) d -> p a v d", v=DH),
                    S[h][:, lo:lo + HS].rearrange("p t s (v d) -> p (t s) v d", v=DH),
                    qs[h][:, lo:lo + HS].rearrange("p t s d -> p (t s) d").unsqueeze(2).to_broadcast([P, HS * 2, DH, DH]),
                    ALU.mult).then_inc(prod_done, 1)
                if mid_work is not None:
                    mid_work()
                pool.wait_ge(prod_done, I * 2 + (3 + half))
                link(g.tensor_tensor(r1[:, :, :], rp[:, :, 0:8], rp[:, :, 8:16], ALU.add))
                link(g.tensor_tensor(r2[:, :, :], r1[:, :, 0:4], r1[:, :, 4:8], ALU.add))
                link(g.tensor_tensor(r3[:, :, :], r2[:, :, 0:2], r2[:, :, 2:4], ALU.add))
                a = r3[:, :, :].rearrange("p (t s v) c -> p s v t c", t=HS, s=2)
                for s in range(2):
                    link(g.tensor_tensor(oblk[:, s, :, bass.ds(j * ST + lo, HS)], a[:, s, :, :, 0], a[:, s, :, :, 1], ALU.add))

            def gather(n, before, h):
                if before is not None:
                    pool.wait_ge(sc_done, before * 16)
                    pool.wait_ge(yw_ready, before)
                link(g.tensor_copy(idx4[h], idx_i[:, bass.ds(n * RT, RT)]))
                for r in range(RT):
                    g.indirect_dma_start(xg[h][r], None, xw_d[:, :],
                                         bass.IndirectOffsetOnAxis(ap=idx4[h][:, r:r + 1], axis=0)).then_inc(g_ld[h][r], 16)

            def scatter(e, r, h):
                pool.wait_ge(yw_ready, e + 1)
                pool.wait_ge(sc_done, e * 16)
                pool.sem_inc(passed, 1)
                g.indirect_dma_start(acc_d[:, :], bass.IndirectOffsetOnAxis(ap=idx4[h][:, r:r + 1], axis=0),
                                     yw[h][r], None, compute_op=ALU.add).then_inc(sc_done, 16)

            stage_values(pool, g, 0, 0)
            stage_norm(0)
            stage_keys(pool, g, 0, 0)
            stage_norm(1)
            for phase, kb0, nb in PHASES:
                if phase == EXPERTS:
                    pool.wait_ge(slots_ready, 1)
                    for i in range(BUF):
                        pool.wait_ge(r_stored[i], 64 * NB2)
                    pool.wait_ge(zero_st, 32)
                    gather(0, None, 0)
                    relink()

                def body(kb, jj, h, last=False, last2=False):
                    I = iteration(kb0, kb, jj, h)
                    j = jj * 2 + h
                    n = kb * NB2 + j
                    if not last and phase != EXPERTS:
                        stage_values(pool, g, I + 1, 1 - h)
                        stage_keys(pool, g, I + 1, 1 - h)
                    if not last2:
                        stage_norm(I + 2)
                    if phase == EXPERTS:
                        reads(I, h, 0, j, lambda: scatter(n * RT, 0, h))
                        scatter(n * RT + 1, 1, h)
                        gather((n + 1) % (E // RT), n * RT, 1 - h)
                    else:
                        reads(I, h, 0, j)
                    if phase == EXPERTS:
                        reads(I, h, 1, j, lambda: scatter(n * RT + 2, 2, h))
                        scatter(n * RT + 3, 3, h)
                    elif not last:
                        reads(I, h, 1, j)

                with pool.Fori(0, nb) as kb:
                    if phase != BACK1:
                        with pool.Fori(0, NB2 // 2) as jj:
                            body(kb, jj, 0)
                            body(kb, jj, 1)
                            relink()
                    else:
                        with pool.Fori(0, NB2 // 2 - 1) as jj:
                            body(kb, jj, 0)
                            body(kb, jj, 1)
                            relink()
                        body(kb, NB2 // 2 - 1, 0, last2=True)
                        body(kb, NB2 // 2 - 1, 1, last=True, last2=True)
                        relink()
                        pool.wait_ge(last_read, 2)
                    g.dma_start(o_st[kb + kb0], oblk[:, :, :, :].rearrange("p s v t -> p s (v t)")).then_inc(o_stored, 16)
            pool.wait_ge(o_stored, 16 * NBLK)

        @block.vector
        def _(dve):
            v = nc.vector
            count = [0]

            def mark(ins):
                count[0] += 1
                ins.then_inc(vch, 1)
                return count[0]

            def link(ins):
                dve.wait_ge(vch, mark(ins))

            def relink():
                dve.wait_ge(vch, count[0])
                dve.sem_clear(vch)
                count[0] = 0

            def statistics(i, ld, n):
                for s in range(2):
                    dve.wait_ge(ld[s], n)
                    for q in range(NB2):
                        m = mark(v.bn_stats(bn6[:, q, :], xs[s][:, q, :]))
                    dve.wait_ge(vch, m)
                    for q in range(NB2):
                        m = mark(v.bn_aggr(mv8[:, q, :], bn6[:, q, :]))
                    dve.wait_ge(vch, m)
                    v.tensor_copy(mean[:, bass.ds((i * 2 + s) * NB2, NB2)], mv8[:, :, 0])
                    v.tensor_copy(var[:, bass.ds((i * 2 + s) * NB2, NB2)], mv8[:, :, 1]).then_inc(xs_used, 1)
                    dve.wait_ge(xs_used, i * 2 + (s + 1))
                    dve.sem_inc(passed, 1)
                relink()

            statistics(0, xs_ld, 32)
            dve.sem_inc(stats_in, 1)
            with dve.Fori(1, NBLK // 2) as i:
                statistics(i, xs_more, i * 32)
            dve.sem_inc(stats_in, 1)
            dve.sem_inc(h_ready, 1)
            link(v.memset(S[1][:, ST - 1], 0.0))
            dve.sem_inc(rec_done, 2)
            relink()

            def norms(L, h, part):
                if part == 0:
                    dve.wait_ge(sq_ready, L + 1)
                    v.tensor_reduce(n2[:, :], sq[:, :, :], AX.X, ALU.add).then_inc(n2_ready, 1)
                else:
                    dve.wait_ge(nrm_ready, L + 1)
                    link(v.tensor_scalar(nrm_e[:, :], nrm[:, :], 1e-6, None, ALU.add))
                    v.reciprocal(rk[h][:, :], nrm_e[:, :]).then_inc(rk_ready, 1)

            def product(q, r):
                dve.wait_ge(sg_ready, q + 1)
                dve.wait_ge(y_done, q)
                v.tensor_tensor(hg_s[:, :, :].rearrange("p a t -> p (a t)"), sgu[:, :],
                                (G0, G1)[r % 2][0:FH, 2 * P:4 * P], ALU.mult).then_inc(h_ready, 1)

            def top8(I):
                dve.wait_ge(lg_copied, I + 1)
                dve.sem_inc(passed, 1)
                for r in range(RT):
                    m = mark(v.max(mx[:, r, :], lg[:, r, :]))
                dve.wait_ge(vch, m)
                v.tensor_scalar(negm, mx[:, :, 0], -1.0, None, ALU.mult).then_inc(negm_ready, 1)
                for r in range(RT):
                    m = mark(v.match_replace(rep[:, r, :], mx[:, r, :], lg[:, r, :], -3.0e38))
                dve.wait_ge(vch, m)
                v.tensor_tensor(mk, rep, lg, ALU.not_equal).then_inc(mask_ready, 1)

            def top8_weights(I, h):
                dve.wait_ge(mask_ready, I + 1)
                dve.wait_ge(e_ready, I + 1)
                link(v.tensor_tensor(wt, ex, mk, ALU.mult))
                link(v.tensor_reduce(wsum, wt, AX.X, ALU.add))
                link(v.reciprocal(wrec, wsum))
                v.tensor_tensor(xw[h][:, :, D:XW], wt, wrec.unsqueeze(2).to_broadcast([P, RT, E]),
                                ALU.mult).then_inc(w_ready, 1)

            def back_x1(c, r, half, x1=x1):
                dve.wait_ge(at_done, c + 1)
                bk = (TB, LG)[r]
                m = mark(v.tensor_tensor(x1[r], bk[:, 0:D], xn_b[half][r], ALU.add))
                dve.wait_ge(vch, m)
                m = mark(v.bn_stats(bn_b[:, r, :], x1[r]))
                dve.wait_ge(vch, m)
                link(v.bn_aggr(mv_b[:, r, :], bn_b[:, r, :]))
                v.tensor_scalar(ve_b[:, r:r + 1], mv_b[:, r, 1:2], EPS, None, ALU.add).then_inc(ve_ready, 1)

            def back_rstd(c, r):
                dve.wait_ge(sd_ready, c + 1)
                link(v.reciprocal(rs_b[:, r:r + 1], sd_b[:, r:r + 1]))
                v.scalar_tensor_tensor(nb_b[:, r:r + 1], mv_b[:, r, 0:1], -1.0, rs_b[:, r:r + 1],
                                       ALU.mult, ALU.mult).then_inc(nb_ready, 1)

            def back_sum(c, r, ob, half, use, loads):
                dve.wait_ge(fin_st[r], use * 16)
                dve.wait_ge(ac_ld[half][r], loads * 16 + 16)
                dve.wait_ge(out_done, c + 1)
                v.tensor_tensor(fin[r], ob[:, 0:D], ac_b[half][r], ALU.add).then_inc(fin_ready, 1)

            OUTB = (YB, LG)

            def step(I, h, s, ready):
                before = S[h][:, s - 1] if s else S[1 - h][:, ST - 1]
                key = [kn[h][:, s, G, :].unsqueeze(1).to_broadcast([P, DH, DH]) for G in range(2)]
                m = [0, 0]
                for G in range(2):
                    if ready[G] is not None:
                        dve.wait_ge(*ready[G])
                    m[G] = mark(v.tensor_tensor(prod[:, G].rearrange("p (v d) -> p v d", v=DH),
                                                before[:, G].rearrange("p (v d) -> p v d", v=DH), key[G], ALU.mult))
                for G in range(2):
                    dve.wait_ge(vch, m[G])
                    m[G] = mark(v.tensor_reduce(kS[:, G], prod[:, G].rearrange("p (v d) -> p v d", v=DH), AX.X, ALU.add))
                for G in range(2):
                    dve.wait_ge(vch, m[G])
                    m[G] = mark(v.scalar_tensor_tensor(nu[:, G], kS[:, G], bg[h][:, s, G:G + 1], bv[h][:, s, G, :],
                                                       ALU.mult, ALU.subtract))
                for G in range(2):
                    dve.wait_ge(vch, m[G])
                    m[G] = mark(v.tensor_tensor(outer[:, G].rearrange("p (v d) -> p v d", v=DH),
                                                nu[:, G].unsqueeze(2).to_broadcast([P, DH, DH]), key[G], ALU.mult))
                for G in range(2):
                    dve.wait_ge(vch, m[G])
                    ins = v.scalar_tensor_tensor(S[h][:, s, G], before[:, G], g8[h][:, s, G:G + 1], outer[:, G],
                                                 ALU.mult, ALU.subtract)
                    if G == 1 and s in (HS - 1, ST - 1):
                        ins.then_inc(rec_done, 1)
                        ready[G] = (rec_done, I * 2 + (3 if s == HS - 1 else 4))
                    else:
                        ready[G] = (vch, mark(ins))

            def slots():
                dve.wait_ge(mT_ready, 2 * NB2)
                for i in range(BUF):
                    dve.wait_ge(r_stored[i], 64 * NB2)
                dve.wait_ge(x4_ld[0], 32 * (NB2 + 1))
                v.tensor_tensor_scan(cum, ones[0:E, 0:1].to_broadcast([E, TOK]), maskT, 0.0,
                                     ALU.mult, ALU.add).then_inc(cum_ready, 1)
                dve.wait_ge(cum_ready, 1)
                for a in range(2):
                    link(v.memset(diff[a][:, :, BLK:CW], float(BLK)))
                relink()
                dve.sem_inc(slot_used, 1)

                def choose(t, a):
                    dve.wait_ge(slot_mm, t - a)
                    for r in range(RT):
                        v.tensor_scalar(onh[a][:, r, :], slot_row[:, :], prv[:, t * RT + r, BLK - 1:BLK],
                                        None, ALU.is_ge)
                    v.tensor_tensor(diff[a][:, :, 0:BLK], cur[:, bass.ds(t * RT, RT), :],
                                    prv[:, bass.ds(t * RT, RT), :], ALU.subtract).then_inc(onh_ready, 1)

                def count_up(t, a):
                    dve.wait_ge(slot_mm, t + 1)
                    ps = (LG, TB)[a][:, 0:RT * CW].rearrange("p (r j) -> p r j", r=RT)
                    link(v.tensor_scalar(cnt[a], ps[:, :, 0:BLK], slot_col[:, 0:1], None, ALU.is_le))
                    link(v.tensor_reduce(csum[a], cnt[a], AX.X, ALU.add))
                    v.scalar_tensor_tensor(sidx[:, bass.ds(t * RT, RT)], csum[a], -float(BLK), ps[:, :, BLK],
                                           ALU.add, ALU.add).then_inc(slot_used, 1)

                for e in range(2):
                    dve.wait_ge(cur_ld[e], 32)
                    n = E // RT // 4
                    choose(e * n * 2, 0)
                    with dve.Fori(e * n, (e + 1) * n - 1) as i:
                        for a in range(2):
                            choose(i * 2 + (a + 1), 1 - a)
                            count_up(i * 2 + a, a)
                        relink()
                    choose((e + 1) * n * 2 - 1, 1)
                    for a in range(2):
                        count_up((e + 1) * n * 2 - 2 + a, a)
                    relink()
                dve.wait_ge(slot_used, E // RT + 1)
                link(v.tensor_scalar(sgei, sidx, float(TOK), None, ALU.is_ge))
                link(v.scalar_tensor_tensor(sidx, sgei, slot_col[:, 0:1], sidx, ALU.mult, ALU.add))
                v.tensor_copy(idx_i[:, :], sidx).then_inc(slots_ready, 1)
                relink()

            for L in range(2):
                norms(L, L, 0)
                norms(L, L, 1)
            relink()
            for phase, kb0, nb in PHASES:
                if phase == EXPERTS:
                    slots()
                if phase == BACK2:
                    dve.wait_ge(mlp_bias, 1)
                    v.tensor_tensor(b1_s[:, :], TB[:, 0:MC], b1_in[:, :], ALU.add).then_inc(mlp_bias, 1)

                def body(kb, jj, h, ready, last2=False):
                    I = iteration(kb0, kb, jj, h)
                    j = jj * 2 + h
                    n = kb * NB2 + j
                    dve.wait_ge(pool_staged, I + 1)
                    dve.wait_ge(act_staged, I + 1)
                    dve.wait_ge(prod_done, I * 2)
                    ready[1] = (rec_done, I * 2 + 2)
                    if phase in (BACK2, BACK2_LATE):
                        m = n + (0 if phase == BACK2 else 2 * NB2)
                        c, rs, half, use, loads = m * 2, (0, 1), h, m, m >> 1
                    elif phase == BACK1:
                        c, rs, half, use, loads = j + (6 * NB2 - h), (h,), 0, jj + 24, jj + 13
                    for s in range(ST):
                        step(I, h, s, ready)
                        if s == 1 and not last2:
                            norms(I + 2, h, 0)
                        if s == 6 and not last2:
                            norms(I + 2, h, 1)
                        if s == 3 and phase == EXPERTS:
                            stage_values(dve, v, I + 1, 1 - h)
                            stage_keys(dve, v, I + 1, 1 - h)
                        if phase in (ROUTE, EXPERTS):
                            q = n * RT + (0 if phase == ROUTE else UNITS_R)
                            r = {2: 0, 3: 1, 5: 2, 6: 3}.get(s)
                            if r is not None:
                                product(q + r, r)
                            if phase == ROUTE and s == 7:
                                top8(I)
                                top8_weights(I, h)
                        else:
                            first = 2 if phase == BACK1 else 0
                            if s == first:
                                for r in rs:
                                    back_x1(c + r, r, half)
                            if s == first + 1:
                                for r in rs:
                                    back_rstd(c + r, r)
                            if s == 6 and len(rs) == 2:
                                back_sum(c, 0, OUTB[0], half, use, loads)
                            if s == 7:
                                back_sum(c + rs[-1], rs[-1], OUTB[rs[-1]], half, use, loads)

                def pair(kb, jj, last=False):
                    ready = [None, None]
                    body(kb, jj, 0, ready, last)
                    body(kb, jj, 1, ready, last)
                    relink()

                with dve.Fori(0, nb) as kb:
                    if phase != BACK1:
                        with dve.Fori(0, NB2 // 2) as jj:
                            pair(kb, jj)
                    else:
                        with dve.Fori(0, NB2 // 2 - 1) as jj:
                            pair(kb, jj)
                        pair(kb, NB2 // 2 - 1, last=True)
            dve.wait_ge(prod_done, 2 * NT)
            dve.wait_ge(rec_done, 2 * NT + 2)
            lo = HS
            room = S[0][:, :].rearrange("p t s n -> p (t s n)")

            def tree(o, n):
                return room[:, o:o + n * HS * 2 * DH].rearrange("p (a d) -> p a d", d=n)

            p16, p8, p4, p2 = tree(0, 16), tree(2048, 8), tree(3072, 4), tree(3584, 2)
            link(v.tensor_tensor(p16.rearrange("p (a v) d -> p a v d", v=DH),
                                 S[1][:, lo:lo + HS].rearrange("p t s (v d) -> p (t s) v d", v=DH),
                                 qs[1][:, lo:lo + HS].rearrange("p t s d -> p (t s) d").unsqueeze(2).to_broadcast([P, HS * 2, DH, DH]),
                                 ALU.mult))
            link(v.tensor_tensor(p8, p16[:, :, 0:8], p16[:, :, 8:16], ALU.add))
            link(v.tensor_tensor(p4, p8[:, :, 0:4], p8[:, :, 4:8], ALU.add))
            link(v.tensor_tensor(p2, p4[:, :, 0:2], p4[:, :, 2:4], ALU.add))
            a = p2.rearrange("p (t s v) c -> p s v t c", t=HS, s=2)
            for s in range(2):
                v.tensor_tensor(oblk[:, s, :, BLK - HS:BLK], a[:, s, :, :, 0], a[:, s, :, :, 1], ALU.add).then_inc(last_read, 1)
            X1 = (x1, x1_odd)

            def back_first(m):
                for r in range(2):
                    back_x1(7 * NB2 + m * 2 + r, r, (m + 1) % 2, X1[m % 2])
                for r in range(2):
                    back_rstd(7 * NB2 + m * 2 + r, r)

            back_first(0)
            for m in range(NB2 // 2):
                if m + 1 < NB2 // 2:
                    back_first(m + 1)
                for r in range(2):
                    back_sum(7 * NB2 + m * 2 + r, r, (YB, FQ)[r], (m + 1) % 2, 28 + m, m // 2 + (12 if m % 2 == 0 else 18 - r))
            relink()

        @block.scalar
        def _(act):
            a_ = nc.scalar
            act.sem_inc(gelu_done, 1)
            act.wait_ge(raw_ld, 16 * 9)
            for c in range(DC):
                a_.activation(wqkvg[:, c, :], wraw[:, c, :], ACT.Copy, scale=lncol[:, 0, c:c + 1]).then_inc(w_scaled, 1)
            act.wait_ge(bias_mm, 1)
            a_.activation(bqkv[:, 0:2], FT[:, 0:2], ACT.Copy, scale=DH ** -0.5).then_inc(bias_done, 1)
            a_.activation(bqkv[:, 2:6], FT[:, 2:6], ACT.Copy).then_inc(bias_done, 1)
            a_.activation(bqkv[0:2 * H, 6:7], FT[0:2 * H, 6:7], ACT.Copy).then_inc(bias_done, 1)
            act.wait_ge(stats_done, 2)
            act.wait_ge(bias_done, 3)

            def front_norm(f, i, behind=0):
                act.wait_ge(xt_ld[i], (f >> 1) * 16 + 16)
                if behind is not None:
                    act.wait_ge(fT_done, f - behind)
                a_.activation(xa[i], xt[i], ACT.Identity, scale=sA[:, bass.ds(f, 1)],
                              bias=bA[:, bass.ds(f, 1)]).then_inc(xa_ready, 1)

            def front_evac(f, i, banks, behind=0):
                act.wait_ge(fT_done, f + 1)
                act.wait_ge(qkv_done, f - behind)
                a_.activation(xaT[i].rearrange("p c t -> p (c t)"), banks[0][:, 0:DC * P], ACT.Copy).then_inc(xaT_ready, 1)

            def front_out(f, i, banks):
                act.wait_ge(qkv_done, f + 1)
                act.wait_ge(f_stored[i], (f >> 1) * FST)
                for m in range(3):
                    for hg in range(2):
                        n = m * 2 + hg
                        src = banks[1][:, n * P:(n + 1) * P] if n < 4 else banks[2][:, (n - 4) * P:(n - 3) * P]
                        a_.activation(stg[i][:, :, n, :], src.rearrange("p (b t) -> p b t", b=2), ACT.Identity,
                                      bias=bqkv[:, n:n + 1], scale=DH ** -0.5 if m == 0 else 1.0)
                a_.activation(gst[i], banks[2][0:2 * H, 2 * P:3 * P], ACT.Sigmoid, bias=bqkv[0:2 * H, 6:7]).then_inc(stg_ready, 1)

            def stage_squares(L):
                par, t0 = lookup(L)
                act.wait_ge(win_ld, ((L >> 3) + 1) * WLD)
                act.wait_ge(n2_ready, L)
                for s in range(2):
                    last = a_.activation(sq[:, :, :].rearrange("p (t s) d -> p t s d", s=2)[:, :, s],
                                         win[1][:, par, s, :, bass.ds(t0, ST)].rearrange("p d t -> p t d"), ACT.Square)
                last.then_inc(sq_ready, 1)

            def stage(L, h):
                par, t0 = lookup(L)
                act.wait_ge(win_ld, ((L >> 3) + 1) * WLD)
                act.wait_ge(prod_done, L * 2)
                act.wait_ge(rec_done, L * 2)
                for s in range(2):
                    a_.activation(qs[h][:, :, s, :], win[0][:, par, s, :, bass.ds(t0, ST)].rearrange("p d t -> p t d"),
                                  ACT.Copy)
                a_.activation(g8[h][:, :, :], gwin[:, par, :, 1, bass.ds(t0, ST)].rearrange("p s t -> p t s"),
                              ACT.Copy).then_inc(act_staged, 1)

            def route_norm(I, n, h):
                act.wait_ge(x4_ld[h], (I >> 1) * 32 + 32)
                act.wait_ge(r_stored[h], (I >> 1) * 64)
                for r in range(RT):
                    tile = n + n // NB2 * ((RT - 1) * NB2) + r * NB2
                    a_.activation(xw[h][:, r, 0:D], x4[h][:, r, :], ACT.Identity, scale=rstd[:, bass.ds(tile, 1)],
                                  bias=nmr[:, bass.ds(tile, 1)]).then_inc(xn_ready, 1)

            def unit_evac(q):
                act.wait_ge(t_done, q + 1)
                act.wait_ge(gu_done, q)
                a_.activation(gT[:, :, :].rearrange("p c t -> p (c t)"), TB[:, 0:DC * P], ACT.Copy).then_inc(gT_ready, 1)

            def unit_silu(q, r):
                act.wait_ge(gu_done, q + 1)
                act.wait_ge(h_ready, q + 1)
                a_.activation(sgu[:, :], (G0, G1)[r % 2][0:FH, 0:2 * P], ACT.Silu).then_inc(sg_ready, 1)

            def route_out(q, r, h):
                act.wait_ge(y_done, q + 1)
                a_.activation(acc4[h][:, r, :], YB[:, 0:D], ACT.Copy).then_inc(acc_ready, 1)

            def expert_out(e, r, h):
                act.wait_ge(y_done, e + (UNITS_R + 1))
                a_.activation(yw[h][r], YB[:, 0:D], ACT.Copy, scale=xg[h][r][:, bass.ds(e + D, 1)]).then_inc(yw_ready, 1)

            front_norm(0, 0, None)
            front_norm(1, 1, None)
            front_evac(0, 0, FRONT0[0])
            for lo, hi in ((0, NB2 // 2 + 2), (NB2 // 2 + 2, AHEAD * NB2 // 2 - 1)):
                with act.Fori(lo, hi) as m:
                    for i in range(2):
                        f = m * 2 + i
                        front_norm(f + 2, i, 1)
                        front_evac(f + 1, 1 - i, FRONT0[1 - i], 1)
                        front_out(f, i, FRONT0[i])
                if lo == 0:
                    stage_squares(0)
                    stage(0, 0)
                    stage_squares(1)
            f = AHEAD * NB2 - 1
            front_evac(f, 1, FRONT0[1], 1)
            front_out(f - 1, 0, FRONT0[0])
            front_out(f, 1, FRONT0[1])
            act.wait_ge(stats_done, 4)

            def back_sqrt(c, r):
                act.wait_ge(ve_ready, c + 1)
                a_.activation(sd_b[:, r:r + 1], ve_b[:, r:r + 1], ACT.Sqrt).then_inc(sd_ready, 1)

            def back_norm(c, r, x1=x1):
                act.wait_ge(nb_ready, c + 1)
                a_.activation(hb[r], x1[r], ACT.Identity, scale=rs_b[:, r:r + 1], bias=nb_b[:, r:r + 1]).then_inc(hb_ready, 1)

            def back_evac(c, r):
                act.wait_ge(hT_done, c + 1)
                a_.activation(hT[r].rearrange("p c t -> p (c t)"), (TB, LG)[r][:, D:2 * D], ACT.Copy).then_inc(hT_ready, 1)

            def back_gelu(c, r, half):
                act.wait_ge(rows_free, 1)
                act.wait_ge(mid_done, c * 2 + (half + 1))
                for i in range(MC // 2):
                    m = half * (MC // 2) + i
                    last = a_.activation(mid[r][:, m, :], (G0, G1)[half][:, i * P:(i + 1) * P], ACT.Gelu, bias=b1_s[:, m:m + 1])
                last.then_inc(gelu_done, 1)

            for phase, kb0, nb in PHASES:
                if phase == ROUTE:
                    route_norm(0, 0, 0)
                if phase == BACK2:
                    act.wait_ge(mlp_bias, 2)
                    for c in range(DC):
                        a_.activation(w1_s[:, c, :], w1_s[:, c, :], ACT.Copy, scale=lncol[:, 2, c:c + 1]).then_inc(mlp_w, 1)

                def body(kb, jj, h, last=False, last2=False):
                    I = iteration(kb0, kb, jj, h)
                    j = jj * 2 + h
                    n = kb * NB2 + j
                    f = I + AHEAD * NB2
                    if not last2 and phase >= BACK2:
                        stage_squares(I + 2)
                    if phase in (ROUTE, EXPERTS):
                        q = n * RT + (0 if phase == ROUTE else UNITS_R)
                        unit_evac(q)
                        front_norm(f, h)
                        stage_squares(I + 2)
                        unit_silu(q, 0)
                        unit_evac(q + 1)
                        front_evac(f, h, FRONT)
                        unit_silu(q + 1, 1)
                        unit_evac(q + 2)
                        front_out(f, h, FRONT)
                        if phase == EXPERTS:
                            expert_out(n * RT, 0, h)
                        else:
                            route_out(q, 0, h)
                        unit_silu(q + 2, 2)
                        stage(I + 1, 1 - h)
                        unit_evac(q + 3)
                        if phase == EXPERTS:
                            expert_out(n * RT + 1, 1, h)
                        else:
                            route_out(q + 1, 1, h)
                        unit_silu(q + 3, 3)
                        if phase == ROUTE:
                            route_norm(I + 1, (I + 1) % (2 * NB2), 1 - h)
                        if phase == EXPERTS:
                            expert_out(n * RT + 2, 2, h)
                            expert_out(n * RT + 3, 3, h)
                        else:
                            route_out(q + 2, 2, h)
                            act.wait_ge(lg_done, I + 1)
                            act.wait_ge(w_ready, I)
                            a_.activation(lg.rearrange("p r e -> p (r e)"), LG[:, 0:RT * E], ACT.Copy).then_inc(lg_copied, 1)
                            route_out(q + 3, 3, h)
                            act.wait_ge(negm_ready, I + 1)
                            for r in range(RT):
                                x_ = a_.activation(ex[:, r, :], lg[:, r, :], ACT.Exp, bias=negm[:, r:r + 1])
                            x_.then_inc(e_ready, 1)
                            act.wait_ge(mt_done, I + 1)
                            for r in range(RT):
                                x_ = a_.activation(maskT_v[:, j, kb, r],
                                                   LG[0:E, r * P:(r + 1) * P].rearrange("e (b t) -> e b t", b=2), ACT.Copy)
                            x_.then_inc(mT_ready, 1)
                        return
                    if phase == BACK1:
                        c, rs = j + (6 * NB2 - h), (h,)
                    else:
                        c, rs = n * 2 + (0 if phase == BACK2 else 4 * NB2), (0, 1)
                    if phase == BACK2:
                        front_norm(f, h)
                        front_evac(f, h, FRONT)

                    def between():
                        if phase == BACK2:
                            front_out(f, h, FRONT)
                        if not last:
                            stage(I + 1, 1 - h)
                    back_act(c, rs, between)

                def back_act(c, rs, between):
                    for r in rs:
                        back_sqrt(c + r, r)
                    for r in rs:
                        back_norm(c + r, r)
                    for r in rs:
                        back_evac(c + r, r)
                    for r in rs:
                        for half in range(2):
                            back_gelu(c + r, r, half)
                            if between is not None and r == rs[0] and half == 1:
                                between()

                with act.Fori(0, nb) as kb:
                    if phase != BACK1:
                        with act.Fori(0, NB2 // 2) as jj:
                            body(kb, jj, 0)
                            body(kb, jj, 1)
                    else:
                        with act.Fori(0, NB2 // 2 - 1) as jj:
                            body(kb, jj, 0)
                            body(kb, jj, 1)
                        body(kb, NB2 // 2 - 1, 0, last2=True)
                        body(kb, NB2 // 2 - 1, 1, last=True, last2=True)
            for m in range(NB2 // 2 + 1):
                if m:
                    c = 7 * NB2 + (m - 1) * 2
                    for r in range(2):
                        back_evac(c + r, r)
                    for r in range(2):
                        for half in range(2):
                            back_gelu(c + r, r, half)
                if m < NB2 // 2:
                    c = 7 * NB2 + m * 2
                    for r in range(2):
                        back_sqrt(c + r, r)
                    for r in range(2):
                        back_norm(c + r, r, (x1, x1_odd)[m % 2])

        @block.tensor
        def _(pe):
            mm = nc.tensor.matmul
            pe.wait_ge(consts, 5)
            pe.wait_ge(raw_ld, 16 * 9)
            for i in range(7):
                n = P if i < 6 else 2 * H
                for c in range(DC):
                    last = mm(FT[0:n, i:i + 1], wraw[:, c, i * P:i * P + n], lncol[:, 1, c:c + 1], start=(c == 0), stop=(c == DC - 1))
            last.then_inc(bias_mm, 1)
            pe.wait_ge(w_scaled, DC)
            pe.wait_ge(bias_done, 3)
            pe.wait_ge(const_ld, 16 * 7)

            def front_T(f, h, banks=FRONT, behind=0):
                pe.wait_ge(xa_ready, f + 1)
                pe.wait_ge(xaT_ready, f - behind)
                for c in range(DC):
                    last = nc.tensor.transpose(banks[0][:, c * P:(c + 1) * P], xa[h][:, c * P:(c + 1) * P], ident[:, :])
                last.then_inc(fT_done, 1)

            def front_mm(f, h, banks=FRONT, behind=0):
                pe.wait_ge(xaT_ready, f + 1)
                pe.wait_ge(stg_ready, f - behind)
                for i in range(7):
                    n = P if i < 6 else 2 * H
                    dst = banks[1][:, i * P:(i + 1) * P] if i < 4 else banks[2][0:n, (i - 4) * P:(i - 3) * P]
                    for c in range(DC):
                        last = mm(dst, wqkvg[:, c, i * P:i * P + n], xaT[h][:, c, :], start=(c == 0), stop=(c == DC - 1))
                last.then_inc(qkv_done, 1)

            def unit_T(q, src):
                pe.wait_ge(gT_ready, q)
                for c in range(DC):
                    last = nc.tensor.transpose(TB[:, c * P:(c + 1) * P], src[:, c * P:(c + 1) * P], ident[:, :])
                last.then_inc(t_done, 1)

            def unit_gu(q, r, wg, wu):
                pe.wait_ge(h_ready, q)
                bk = (G0, G1)[r % 2]
                for i in range(4):
                    w = wg if i < 2 else wu
                    for c in range(DC):
                        last = mm(bk[0:FH, i * P:(i + 1) * P], w[:, c, (i % 2) * FH:(i % 2 + 1) * FH], gT[:, c, :],
                                  start=(c == 0), stop=(c == DC - 1))
                last.then_inc(gu_done, 1)

            def unit_y(q, wd, bias, tokens):
                pe.wait_ge(h_ready, q + 2)
                for c in range(2):
                    last = mm(YB[:, 0:D], hg_s[:, c, :], wd[:, c, :], start=(c == 0), stop=(c == 1 and bias is None))
                if bias is not None:
                    mm(YB[:, 0:D], ones[0:1, :], bias, start=False, stop=False)
                    last = mm(YB[:, 0:D], ident[:, :], tokens, start=False, stop=True)
                last.then_inc(y_done, 1)

            front_T(0, 0, FRONT0[0])
            front_T(1, 1, FRONT0[1], 1)
            front_mm(0, 0, FRONT0[0])
            with pe.Fori(0, AHEAD * NB2 // 2 - 1) as m:
                for i in range(2):
                    f = m * 2 + i + 2
                    front_T(f, i, FRONT0[i], 1)
                    front_mm(f - 1, 1 - i, FRONT0[1 - i], 1)
            front_mm(AHEAD * NB2 - 1, 1, FRONT0[1], 1)

            def route_T(h, q, r):
                pe.wait_ge(xn_ready, q + 1)
                unit_T(q, xw[h][:, r, :])

            def route_gu(I, q, r):
                pe.wait_ge(gT_ready, q + 1)
                if r == 0:
                    pe.wait_ge(mT_ready, I)
                for c in range(DC):
                    last = mm(LG[:, r * E:(r + 1) * E], gT[:, c, :], rw_s[:, c, :], start=(c == 0), stop=(c == DC - 1))
                if r == RT - 1:
                    last.then_inc(lg_done, 1)
                unit_gu(q, r, wsgu_s[:, :, 0:F], wsgu_s[:, :, F:2 * F])

            def route_y(q, r, h):
                pe.wait_ge(acc_ready, q)
                unit_y(q, wsd_s[:, :, :], b2_s[0:1, :], x4[h][:, r, :])

            def expert_T(n, q, r, h):
                pe.wait_ge(g_ld[h][r], (n >> 1) * 16 + 16)
                unit_T(q, xg[h][r])

            def expert_gu(n, q, r):
                pe.wait_ge(gT_ready, q + 1)
                pe.wait_ge(ew_ld[r], n * 48 + 48)
                unit_gu(q, r, ew_g[r], ew_u[r])

            def expert_y(e, r):
                pe.wait_ge(yw_ready, e)
                unit_y(e + UNITS_R, ew_d[r], None, None)

            def back_attn(c, r, half, use, apart=False):
                pe.wait_ge(bk_ld[half][r], use * 48 + 48)
                if r == 1 and not apart:
                    pe.wait_ge(fin_ready, c - 1)
                bk = (TB, LG)[r]
                for g in range(2):
                    mm(bk[:, 0:D], oT[half][r][:, g].rearrange("p b t -> p (b t)"), wo_s[:, g, :], start=(g == 0), stop=False)
                mm(bk[:, 0:D], ones[0:1, :], bo_s[0:1, :], start=False, stop=True).then_inc(at_done, 1)

            def back_T(c, r):
                pe.wait_ge(hb_ready, c + 1)
                for i in range(DC):
                    last = nc.tensor.transpose((TB, LG)[r][:, D + i * P:D + (i + 1) * P], hb[r][:, i * P:(i + 1) * P], ident[:, :])
                last.then_inc(hT_done, 1)

            def back_mid(c, r, half):
                if half == 0:
                    pe.wait_ge(hT_ready, c + 1)
                pe.wait_ge(gelu_done, c * 2 + half)
                for i in range(MC // 2):
                    m = half * (MC // 2) + i
                    for k in range(DC):
                        last = mm((G0, G1)[half][:, i * P:(i + 1) * P], w1_s[:, k, m * P:(m + 1) * P], hT[r][:, k, :],
                                  start=(k == 0), stop=(k == DC - 1))
                last.then_inc(mid_done, 1)

            def back_out(c, r, bank=None, rows=None):
                x1r = x1[r] if rows is None else rows
                ob = (YB, LG)[r] if bank is None else bank
                pe.wait_ge(gelu_done, c * 2 + 3)
                pe.wait_ge(mlp_ld, 32)
                if r == 0:
                    pe.wait_ge(fin_ready, c)
                for m in range(MC):
                    mm(ob[:, 0:D], mid[r][:, m, :], w2_s[:, m, :], start=(m == 0), stop=False)
                mm(ob[:, 0:D], ident[:, :], x1r, start=False, stop=True).then_inc(out_done, 1)

            def back_mlp(c, rs):
                for r in rs:
                    back_T(c + r, r)
                back_mid(c + rs[0], rs[0], 0)
                back_mid(c + rs[0], rs[0], 1)
                if len(rs) == 2:
                    back_mid(c + 1, 1, 0)
                    back_out(c, 0)
                    back_mid(c + 1, 1, 1)
                back_out(c + rs[-1], rs[-1])

            for phase, kb0, nb in PHASES:
                if phase == EXPERTS:
                    pe.wait_ge(mT_ready, 2 * NB2)
                    with pe.Fori(0, E // RT // 2) as i:
                        for a in range(2):
                            pe.wait_ge(onh_ready, i * 2 + (a + 1))
                            pe.wait_ge(slot_used, i * 2 + a)
                            for r in range(RT):
                                last = mm((LG, TB)[a][:, r * CW:(r + 1) * CW], onh[a][:, r, :], diff[a][:, r, :], start=True, stop=True)
                            last.then_inc(slot_mm, 1)
                    pe.wait_ge(slot_used, E // RT + 1)
                    pe.wait_ge(acc_ready, NT)
                if phase == BACK2:
                    pe.wait_ge(h_ready, NT + E + 1)
                    pe.wait_ge(yw_ready, E)
                    pe.wait_ge(mlp_ld, 16)
                    for m in range(MC):
                        for c in range(DC):
                            last = mm(TB[:, m:m + 1], w1_s[:, c, m * P:(m + 1) * P], lncol[:, 3, c:c + 1],
                                      start=(c == 0), stop=(c == DC - 1))
                    last.then_inc(mlp_bias, 1)
                    pe.wait_ge(mlp_bias, 2)
                    pe.wait_ge(mlp_w, DC)
                with pe.Fori(0, nb) as kb:
                    with pe.Fori(0, NB2 // 2) as jj:
                        for h in range(2):
                            I = iteration(kb0, kb, jj, h)
                            j = jj * 2 + h
                            n = kb * NB2 + j
                            f = I + AHEAD * NB2
                            if phase == ROUTE:
                                q = n * RT
                                route_T(h, q, 0)
                                route_gu(I, q, 0)
                                route_T(h, q + 1, 1)
                                front_T(f, h)
                                route_gu(I, q + 1, 1)
                                route_T(h, q + 2, 2)
                                front_mm(f, h)
                                route_y(q, 0, h)
                                route_gu(I, q + 2, 2)
                                route_y(q + 1, 1, h)
                                route_T(h, q + 3, 3)
                                route_gu(I, q + 3, 3)
                                route_y(q + 2, 2, h)
                                route_y(q + 3, 3, h)
                                pe.wait_ge(mask_ready, I + 1)
                                pe.wait_ge(lg_copied, I + 1)
                                pe.sem_inc(passed, 1)
                                for r in range(RT):
                                    last = nc.tensor.transpose(LG[0:E, r * P:(r + 1) * P], mk[:, r, :], ident[:, :])
                                last.then_inc(mt_done, 1)
                            elif phase == EXPERTS:
                                q = n * RT + UNITS_R
                                expert_T(n, q, 0, h)
                                expert_gu(n, q, 0)
                                expert_T(n, q + 1, 1, h)
                                front_T(f, h)
                                expert_gu(n, q + 1, 1)
                                expert_T(n, q + 2, 2, h)
                                front_mm(f, h)
                                expert_y(n * RT, 0)
                                expert_gu(n, q + 2, 2)
                                expert_y(n * RT + 1, 1)
                                expert_T(n, q + 3, 3, h)
                                expert_gu(n, q + 3, 3)
                                expert_y(n * RT + 2, 2)
                                expert_y(n * RT + 3, 3)
                            else:
                                if phase == BACK1:
                                    c, rs, half, use = j + (6 * NB2 - h), (h,), 0, jj + 13
                                else:
                                    m = n + (0 if phase == BACK2 else 2 * NB2)
                                    c, rs, half, use = m * 2, (0, 1), h, m >> 1
                                for r in rs:
                                    back_attn(c + r, r, half, use)
                                if phase == BACK2:
                                    front_T(f, h)
                                    front_mm(f, h)
                                back_mlp(c, rs)
            def attn(m):
                for r in range(2):
                    back_attn(7 * NB2 + m * 2 + r, r, (m + 1) % 2, m // 2 + (12 if m % 2 == 0 else 18 - r), m > 0)

            attn(0)
            for m in range(NB2 // 2):
                c = 7 * NB2 + m * 2
                for r in range(2):
                    back_T(c + r, r)
                back_mid(c, 0, 0)
                back_mid(c, 0, 1)
                back_mid(c + 1, 1, 0)
                if m + 1 < NB2 // 2:
                    attn(m + 1)
                back_out(c, 0, YB, (x1, x1_odd)[m % 2][0])
                back_mid(c + 1, 1, 1)
                back_out(c + 1, 1, FQ, (x1, x1_odd)[m % 2][1])


_INS = ['L0_attn_x', 'L0_attn_Wq', 'L0_attn_Wk', 'L0_attn_Wv', 'L0_attn_Wb', 'L0_attn_Wg', 'L0_attn_Wo', 'L0_attn_bo',
        'L0_attn_ln1_g', 'L0_attn_ln1_b', 'L0_attn_ln2_g', 'L0_attn_ln2_b', 'L0_attn_w1', 'L0_attn_b1', 'L0_attn_w2',
        'L0_attn_b2', 'L0_ffn_router_w', 'L0_ffn_w_gate', 'L0_ffn_w_up', 'L0_ffn_w_down', 'L0_ffn_ws_gate_up',
        'L0_ffn_ws_down']


def kernel(**inputs):
    import numpy as _np
    import concourse.bacc as _bacc
    from concourse import mybir as _mybir
    from concourse.bass_utils import run_bass_kernel_spmd as _run

    nc = _bacc.Bacc("TRN2", target_bir_lowering=False, num_devices=1)
    arrays, args = {}, []
    for name in _INS:
        a = _np.asarray(inputs[name])
        if name == 'L0_ffn_router_w':
            a = a.T
        a = _np.ascontiguousarray(a)
        arrays[f"in_{name}"] = a
        args.append(nc.dram_tensor(f"in_{name}", a.shape, _mybir.dt.from_np(a.dtype), kind="ExternalInput").ap())
    out = nc.dram_tensor("out_0", (B, T, D), _mybir.dt.float32, kind="ExternalOutput").ap()
    layer(nc, *args, out)
    r = _run(nc, [arrays], core_ids=[0])
    return r.results[0]["out_0"]
```
